# Optimizing a Trainium2 kernel written in Bass

```python
import numpy as np
import jax
import jax.numpy as jnp

def _softmax(x, axis=-1):
    return jax.nn.softmax(x, axis=axis)

def _gelu(x):
    return jax.nn.gelu(x, approximate=True)

def _silu(x):
    return jax.nn.silu(x)

def _sigmoid(x):
    return jax.nn.sigmoid(x)

def _layernorm(x, axis=-1, eps=1e-05):
    m = jnp.mean(x, axis=axis, keepdims=True)
    v = jnp.var(x, axis=axis, keepdims=True)
    return (x - m) / jnp.sqrt(v + eps)

def _scatter_add(tgt, idx, src, axis=0):
    return tgt.at[idx].add(src)

def _segment_sum(src, seg, n):
    return jax.ops.segment_sum(src, seg, n)
kernel_name = 'mk_gnn_preln_d1_gnn_r32_6affc7'

def setup_inputs(seed: int=0):
    np.random.seed(seed)
    _w = jnp.asarray

    def _rec_inputs():
        import jax
        import jax.numpy as jnp
        _gk = jax.random.key(seed)
        x = -0.0005121 + 1.001 * jax.random.normal(jax.random.fold_in(_gk, 1), (3125, 64), jnp.float32)
        _s = jax.random.randint(jax.random.fold_in(_gk, 2), (25000,), 0, 3125, jnp.int32)
        _d = jax.random.randint(jax.random.fold_in(_gk, 3), (25000,), 0, 3125, jnp.int32)
        _loop = jnp.arange(3125, dtype=jnp.int32)
        src = jnp.concatenate([_s, _d, _loop])
        dst = jnp.concatenate([_d, _s, _loop])
        _o = jnp.argsort(dst, stable=True)
        src = src[_o]
        dst = dst[_o]
        edge_attr_16 = 0.000254156 + 0.999948 * jax.random.normal(jax.random.fold_in(_gk, 11), (53125, 16), jnp.float32)
        return (x, src, dst, edge_attr_16)
    x, src, dst, edge_attr_16 = _rec_inputs()

    def _L0_gnn_setup():
        import jax, jax.numpy as jnp
        import numpy as np
        N, E, D, ED = (50000, 25000, 64, 16)
        H1 = 2 * D + ED

        def _forward(x, edge_weights, W_att1, b_att1, W_att2, b_att2, W_lin, b_lin, W_ih, b_ih, W_hh, b_hh, edge_idx):
            num_nodes = x.shape[0]
            src = edge_idx[0]
            dst = edge_idx[1]
            lin_x = x @ W_lin.T + b_lin
            feat = jnp.concatenate([x[src], edge_weights, x[dst]], axis=1)
            h = jax.nn.relu(feat @ W_att1.T + b_att1)
            scores = (h @ W_att2.T + b_att2)[:, 0]
            m = jax.ops.segment_max(scores, src, num_segments=num_nodes)
            e = jnp.exp(scores - m[src])
            denom = jax.ops.segment_sum(e, src, num_segments=num_nodes)
            alpha = e / denom[src]
            msg = jax.ops.segment_sum(alpha[:, None] * lin_x[dst], src, num_segments=num_nodes)
            gi = x @ W_ih.T + b_ih
            gh = msg @ W_hh.T + b_hh
            i_r, i_z, i_n = jnp.split(gi, 3, axis=1)
            h_r, h_z, h_n = jnp.split(gh, 3, axis=1)
            r = jax.nn.sigmoid(i_r + h_r)
            z = jax.nn.sigmoid(i_z + h_z)
            n = jnp.tanh(i_n + r * h_n)
            new_h = (1.0 - z) * n + z * msg
            deg = jax.ops.segment_sum(jnp.ones_like(scores), src, num_segments=num_nodes)
            return jnp.where(deg[:, None] > 0, new_h, x)
        key = jax.random.key(seed)
        ks = jax.random.split(key, 16)
        s = 0.05
        inp = {'x': jax.random.normal(ks[0], (N, D), jnp.float32), 'edge_idx': jax.random.randint(ks[1], (2, E), 0, N, jnp.int64), 'edge_weights': jax.random.normal(ks[2], (E, ED), jnp.float32), 'W_att1': jax.random.normal(ks[3], (H1, H1), jnp.float32) * s, 'b_att1': jnp.zeros((H1,), jnp.float32), 'W_att2': jax.random.normal(ks[4], (1, H1), jnp.float32) * s, 'b_att2': jnp.zeros((1,), jnp.float32), 'W_lin': jax.random.normal(ks[5], (D, D), jnp.float32) * s, 'b_lin': jnp.zeros((D,), jnp.float32), 'W_ih': jax.random.normal(ks[6], (3 * D, D), jnp.float32) * s, 'b_ih': jnp.zeros((3 * D,), jnp.float32), 'W_hh': jax.random.normal(ks[7], (3 * D, D), jnp.float32) * s, 'b_hh': jnp.zeros((3 * D,), jnp.float32)}
        return inp
    _L0_gnn_all = _L0_gnn_setup()
    _L0_gnn_in = {k: v for k, v in _L0_gnn_all.items() if k in ('W_att1', 'b_att1', 'W_att2', 'b_att2', 'W_lin', 'b_lin', 'W_ih', 'b_ih', 'W_hh', 'b_hh')}
    del _L0_gnn_all
    return {'x': x, 'src': src, 'dst': dst, 'edge_attr_16': edge_attr_16, 'L0_gnn_W_att1': _L0_gnn_in['W_att1'], 'L0_gnn_b_att1': _L0_gnn_in['b_att1'], 'L0_gnn_W_att2': _L0_gnn_in['W_att2'], 'L0_gnn_b_att2': _L0_gnn_in['b_att2'], 'L0_gnn_W_lin': _L0_gnn_in['W_lin'], 'L0_gnn_b_lin': _L0_gnn_in['b_lin'], 'L0_gnn_W_ih': _L0_gnn_in['W_ih'], 'L0_gnn_b_ih': _L0_gnn_in['b_ih'], 'L0_gnn_W_hh': _L0_gnn_in['W_hh'], 'L0_gnn_b_hh': _L0_gnn_in['b_hh']}

def reference(x, src, dst, edge_attr_16, L0_gnn_W_att1, L0_gnn_b_att1, L0_gnn_W_att2, L0_gnn_b_att2, L0_gnn_W_lin, L0_gnn_b_lin, L0_gnn_W_ih, L0_gnn_b_ih, L0_gnn_W_hh, L0_gnn_b_hh):
    import jax
    import jax.numpy as jnp

    def _L0_gnn_ref(x, edge_idx, edge_weights, W_att1, b_att1, W_att2, b_att2, W_lin, b_lin, W_ih, b_ih, W_hh, b_hh):
        import jax, jax.numpy as jnp
        import numpy as np
        N, E, D, ED = (50000, 25000, 64, 16)
        H1 = 2 * D + ED

        def _forward(x, edge_weights, W_att1, b_att1, W_att2, b_att2, W_lin, b_lin, W_ih, b_ih, W_hh, b_hh, edge_idx):
            num_nodes = x.shape[0]
            src = edge_idx[0]
            dst = edge_idx[1]
            lin_x = x @ W_lin.T + b_lin
            feat = jnp.concatenate([x[src], edge_weights, x[dst]], axis=1)
            h = jax.nn.relu(feat @ W_att1.T + b_att1)
            scores = (h @ W_att2.T + b_att2)[:, 0]
            m = jax.ops.segment_max(scores, src, num_segments=num_nodes)
            e = jnp.exp(scores - m[src])
            denom = jax.ops.segment_sum(e, src, num_segments=num_nodes)
            alpha = e / denom[src]
            msg = jax.ops.segment_sum(alpha[:, None] * lin_x[dst], src, num_segments=num_nodes)
            gi = x @ W_ih.T + b_ih
            gh = msg @ W_hh.T + b_hh
            i_r, i_z, i_n = jnp.split(gi, 3, axis=1)
            h_r, h_z, h_n = jnp.split(gh, 3, axis=1)
            r = jax.nn.sigmoid(i_r + h_r)
            z = jax.nn.sigmoid(i_z + h_z)
            n = jnp.tanh(i_n + r * h_n)
            new_h = (1.0 - z) * n + z * msg
            deg = jax.ops.segment_sum(jnp.ones_like(scores), src, num_segments=num_nodes)
            return jnp.where(deg[:, None] > 0, new_h, x)
        return _forward(x, edge_weights, W_att1, b_att1, W_att2, b_att2, W_lin, b_lin, W_ih, b_ih, W_hh, b_hh, edge_idx)
    edge_index = jnp.stack([src, dst])
    h = jnp.maximum(_layernorm(x, axis=-1), 0.0)
    x = x + _L0_gnn_ref(h, edge_index, edge_attr_16, L0_gnn_W_att1, L0_gnn_b_att1, L0_gnn_W_att2, L0_gnn_b_att2, L0_gnn_W_lin, L0_gnn_b_lin, L0_gnn_W_ih, L0_gnn_b_ih, L0_gnn_W_hh, L0_gnn_b_hh)
    return x

_drawn_inputs = setup_inputs


def setup_inputs(seed=0):
    import zlib

    import numpy as np

    out = dict(_drawn_inputs(seed))
    spreads = {'L0_gnn_b_att1': (0.0, 2.0),
     'L0_gnn_b_lin': (0.0, 0.1),
     'L0_gnn_b_ih': (0.0, 0.1),
     'L0_gnn_b_hh': (0.0, 0.305)}
    factors = {'edge_attr_16': 8.0, 'L0_gnn_W_att1': 8.0, 'L0_gnn_W_att2': 8.0, 'L0_gnn_W_hh': 3.312}
    for name, (base, spread) in spreads.items():
        noise = np.random.default_rng([zlib.crc32(name.encode()), seed]).standard_normal(out[name].shape)
        drawn = base * np.exp(spread * noise) if base else spread * noise
        out[name] = jnp.asarray(drawn.astype(out[name].dtype))
    for name, factor in factors.items():
        out[name] = (out[name] * factor).astype(out[name].dtype)
    return out
```

```python
import numpy as np
import concourse.bass as bass
from concourse import mybir
from contextlib import ExitStack

F32 = mybir.dt.float32
BF16 = mybir.dt.bfloat16
I32 = mybir.dt.int32
U32 = mybir.dt.uint32
ALU = mybir.AluOpType
ACT = mybir.ActivationFunctionType
AX = mybir.AxisListType

P = 128
NODES = 3125
EDGES = 53125
D = 64
ED = 16
H1 = 2 * D + ED
FULL = EDGES // P
TILES = (EDGES + NODES + P - 1) // P
EXTRA = TILES - FULL
LO, HI = 125, 25
QUAD = 4
PAIRS = TILES // (2 * QUAD)
OCT = 2 * QUAD
ROW = ED + 1
PARTS = 3
PAY = 28
C_VALID, C_NODE, C_DST = PARTS * ED // 2, PARTS * ED // 2 + 1, PARTS * ED // 2 + 2
TAB = H1 + D
CHUNK, CHUNKS, SUB = 448, 7, 112
TAB_AT = 7
TAB_END = TAB_AT + HI - 1
NPAD = NODES + P
WIDE = 3264
MAGIC = 12582912.0
DUMMY = -1e30
APART = 1e33
EPS = 1e-5
TB = 110
NTB = TILES // TB

LAYOUT, _at = {}, 0
for _name, _n in [("ident", P), ("before", P), ("after", P), ("iota", CHUNK), ("first", P),
                  ("w1", 2 * H1), ("wedge", 3 * 2 * H1), ("w2", H1), ("b2", 1), ("wlin", D), ("wih", 3 * D),
                  ("whh", 3 * D), ("last", 1), ("spread", D + 1)]:
    LAYOUT[_name] = (_at, _at + _n)
    _at += _n
PACK = _at


class Steps:

    def __init__(self, engine, sem):
        self.engine, self.sem, self.base, self.n = engine, sem, 0, 0

    def mark(self, ins):
        ins.then_inc(self.sem, 1)
        self.n += 1

    def sync(self, n=None):
        self.engine.wait_ge(self.sem, self.base + (self.n if n is None else n))

    def link(self, ins):
        self.mark(ins)
        self.sync()


def gnn_kernel(nc, x, src, dst, rows, pack, out):
    sorted_rows = nc.dram_tensor("sorted_rows", (TILES * P, PAY), F32, kind="Internal").ap()
    src_table = nc.dram_tensor("src_table", (NPAD, PARTS * H1), BF16, kind="Internal").ap()
    dst_table = nc.dram_tensor("dst_table", (NODES, TAB), F32, kind="Internal").ap()

    ctx = ExitStack()
    with ctx:
        def sb(name, shape, dt=F32):
            return ctx.enter_context(nc.sbuf_tensor(name, shape, dt))

        def sem(name):
            return ctx.enter_context(nc.semaphore(name))

        banks = [ctx.enter_context(nc.psum_tensor(f"bank{i}", [P, 512], F32)) for i in range(8)]

        wp = sb("wp", [P, PACK])

        def const(name, parts=P):
            a, b = LAYOUT[name]
            return wp[0:parts, a:b]

        ident, iota = const("ident"), const("iota")[:, 0:P]
        iota_b = sb("iota_b", [P, P], BF16)
        ident_b = sb("ident_b", [P, P], BF16)

        hT = sb("hT", [D + 1, CHUNK * CHUNKS])
        early = ExitStack()

        def eb(name, shape, dt=F32):
            return early.enter_context(nc.sbuf_tensor(name, shape, dt))

        xs = eb("xs", [LO, HI, D])
        h = eb("h", [LO, HI, D])
        mean = eb("mean", [LO, HI])
        var = eb("var", [LO, HI])
        std = eb("std", [LO, HI])
        rstd = eb("rstd", [LO, HI])
        hc = eb("hc", [LO, D])
        hcT = eb("hcT", [D + 1, LO])
        tab_src = eb("tab_src", [LO, HI, H1])
        tab_dst = eb("tab_dst", [LO, HI, TAB])
        zero_rows = eb("zero_rows", [P, PARTS * H1], BF16)

        edges = eb("edges", [P, TILES, ROW])
        edge_rest = eb("edge_rest", [P, OCT, ED])
        src_i = eb("src_i", [P, TILES], I32)
        dst_i = eb("dst_i", [P, TILES], I32)
        dst_f = eb("dst_f", [P, TILES])
        lo = eb("lo", [P, TILES])
        hi = eb("hi", [P, TILES])
        hi1 = eb("hi1", [P, TILES])
        hi1sq = eb("hi1sq", [P, TILES])
        rhi = eb("rhi", [P, TILES])
        nodef = eb("nodef", [P, TILES])

        oh_lo = [eb(f"oh_lo{q}", [P, QUAD, P], BF16) for q in range(2)]
        oh_hi = [eb(f"oh_hi{q}", [P, QUAD, HI], BF16) for q in range(2)]
        lo_b = eb("lo_b", [P, TILES], BF16)
        hi_b = eb("hi_b", [P, TILES], BF16)
        count = eb("count", [LO, HI * TILES], BF16)
        tab_split = count[:, 0:HI * PARTS * H1].rearrange("p (c s f) -> p c s f", c=HI, s=PARTS)
        total = eb("total", [LO, 2 * PAIRS])
        total1 = eb("total1", [LO, 1])
        start = eb("start", [LO, HI * TILES + 1])

        marked_T = [eb(f"marked_T{q}", [LO, QUAD, P], BF16) for q in range(2)]
        start_q = [eb(f"start_q{q}", [LO, QUAD, 2, HI], BF16) for q in range(2)]
        same = eb("same", [P, OCT, P], BF16)
        rank = eb("rank", [P, OCT])
        own_hi = eb("own_hi", [P, OCT, HI])
        pick = eb("pick", [P, OCT, 2 * HI])
        place = eb("place", [P, OCT])
        place_t = eb("place_t", [P, OCT])
        place_u = eb("place_u", [P, OCT])
        addr = [eb(f"addr{par}", [P, OCT], U32) for par in range(2)]
        pay = [eb(f"pay{par}", [P, OCT, PAY]) for par in range(2)]

        early.close()

        sums = sb("sums", [D + 1, WIDE])
        firsts = sb("firsts", [D + 1, TILES])
        piece_top = sb("piece_top", [OCT, 2, PAIRS])
        window_at = sb("window_at", [1, TILES], I32)
        row = {n: sb(f"row_{n}", [1, TILES + 1]) for n in ("first", "last")}
        x_out = sb("x_out", [SUB, CHUNKS * CHUNK // SUB, D])
        result = sb("result", [SUB, CHUNKS * CHUNK // SUB, D])
        middle = ExitStack()

        def mb(name, shape, dt=F32):
            return middle.enter_context(nc.sbuf_tensor(name, shape, dt))

        entries = mb("entries", [P, TILES, PAY])
        node = mb("node", [P, TILES])
        local = mb("local", [P, TILES])
        penalty = mb("penalty", [P, TILES])
        edge_w = mb("edge_w", [2 * PARTS * ED, PARTS, 2, H1], BF16)
        edge_w_rest = mb("edge_w_rest", [2 * PARTS * ED, PARTS, 2, H1])

        dst_at = [mb(f"dst_at{par}", [P, OCT], U32) for par in range(2)]
        got = [mb(f"got{par}", [P, OCT, TAB]) for par in range(2)]
        window = [mb(f"window{par}", [P, OCT, PARTS * H1], BF16) for par in range(2)]
        onehot = [mb(f"onehot{par}", [P, OCT, P], BF16) for par in range(2)]
        onehot_f = [mb(f"onehot_f{par}", [P, OCT, P]) for par in range(2)]
        onehot_T = [mb(f"onehot_T{q}", [P, QUAD, P], BF16) for q in range(2)]
        feat = [mb(f"feat{q}", [P, QUAD, PARTS * ED], BF16) for q in range(2)]
        feat_T = [mb(f"feat_T{q}", [2 * PARTS * ED, 2, P], BF16) for q in range(2)]
        hidden = [mb(f"hidden{d}", [P, 2, H1]) for d in range(2)]
        weighed = mb("weighed", [P, OCT, H1], BF16)
        score = mb("score", [P, OCT])
        masked = mb("masked", [P, OCT])
        node_q = mb("node_q", [P, OCT])

        node_T = mb("node_T", [OCT, P])
        step_T = mb("step_T", [OCT, P + 1])
        ahead = mb("ahead", [OCT, P])
        behind = mb("behind", [OCT, P])
        top = mb("top", [OCT, P])
        power = mb("power", [OCT, P])
        weight = mb("weight", [P, OCT])
        feats = [mb(f"feats{par}", [P, OCT, D + 1]) for par in range(2)]
        scaled = [mb(f"scaled{par}", [P, OCT, D + 1]) for par in range(2)]

        middle.close()

        row |= {n: sb(f"row_{n}", [1, TILES + 1]) for n in
                ("top_first", "top_last", "link", "one", "pass_f", "pass_b", "run_f", "run_b",
                 "scale_f", "scale_l")}
        col = sb("col", [TB, 4, NTB])
        firsts_T = sb("firsts_T", [TB, NTB, D + 1])
        first_parts = sb("first_parts", [TB, NTB, PARTS, D + 1], BF16)
        last_rep = sb("last_rep", [TB, NTB, D + 1])
        last_parts = sb("last_parts", [TB, NTB, PARTS, D + 1], BF16)
        at_first = sb("at_first", [TB, NTB, CHUNK], BF16)
        at_last = sb("at_last", [TB, NTB, CHUNK], BF16)

        merged = sb("merged", [D + 1, CHUNK])
        den = sb("den", [D + 1, CHUNK])
        some = sb("some", [D, CHUNK])
        msg = sb("msg", [D + 1, CHUNK])
        gate_r = sb("gate_r", [D, CHUNK])
        gate_z = sb("gate_z", [D, CHUNK])
        gate_n = sb("gate_n", [D, CHUNK])
        new = sb("new", [D, CHUNK])
        old = sb("old", [D, CHUNK])

        def parts(par):
            return pay[par][:, :, 0:C_VALID].bitcast(BF16).rearrange("p t (s f) -> p t s f", s=PARTS)

        count_v = count[:, :].rearrange("p (h t) -> p h t", h=HI)
        start_v = start[:, 0:HI * TILES].rearrange("p (h t) -> p t h", h=HI)

        def S(*names):
            return [sem(n) for n in names]

        x_in, src_in, dst_in, rows_in, pack_in = S("x_in", "src_in", "dst_in", "rows_in", "pack_in")
        dve_step, act_step, pool_step = S("dve_step", "act_step", "pool_step")
        var_ready, std_ready, rstd_ready, h_ready, rows_ready = S(
            "var_ready", "std_ready", "rstd_ready", "h_ready", "rows_ready")
        onehot_ready = S("onehot_ready0", "onehot_ready1")
        counted = S("counted0", "counted1")
        count_kept = S("count_kept0", "count_kept1")
        total_ready, base_ready, start_ready, consts_ready = S(
            "total_ready", "base_ready", "start_ready", "consts_ready")
        marked = S("marked0", "marked1")
        start_high = S("start_high0", "start_high1")
        start_split = S("start_split0", "start_split1")
        turned = S("turned0", "turned1")
        turned_kept = S("turned_kept0", "turned_kept1")
        ranked = S("ranked0", "ranked1")
        rank_read = S("rank_read0", "rank_read1")
        addr_ready = S("addr_ready_even", "addr_ready_odd")
        scattered = S("scattered_even", "scattered_odd")
        tab_split_ready, edge_high, edge_rest_ready, edge_mid, edge_split = S(
            "tab_split_ready", "edge_high", "edge_rest_ready", "edge_mid", "edge_split")
        tab_rest_ready = sem("tab_rest_ready")
        rest_cleared = sem("rest_cleared")
        hc_ready, hcT_made, hcT_ready, tab_made, tab_kept, tables_out = S(
            "hc_ready", "hcT_made", "hcT_ready", "tab_made", "tab_kept", "tables_out")

        late_step, late_act = S("late_step", "late_act")
        sorted_first, sorted_in, x_again, piece_rows, node_ready, firsts_ps_ready, prepared, dst_ready0, dst_ready1 = S(
            "sorted_first", "sorted_in", "x_again", "piece_rows", "node_ready", "firsts_ps_ready", "prepared",
            "dst_ready_even", "dst_ready_odd")
        dst_ready = [dst_ready0, dst_ready1]
        gathered = S("gathered_even", "gathered_odd")
        summed = S("summed_even", "summed_odd")
        window_in = S("window_in_even", "window_in_odd")
        (onehot_made, feat_ready, feat_turned, feat_T_kept, hidden_ps_ready,
         hidden_read, scored, masked_ready, masked_turned, node_q_ready, node_turned, node_T_kept, power_from,
         power_ready, power_turned, weight_read, feats_kept, onehot_f_kept, scaled_ready,
         sums_kept) = S(
            "onehot_made", "feat_ready", "feat_turned", "feat_T_kept",
            "hidden_ps_ready", "hidden_read", "scored", "masked_ready", "masked_turned", "node_q_ready",
            "node_turned", "node_T_kept", "power_from", "power_ready", "power_turned", "weight_read",
            "feats_kept", "onehot_f_kept", "scaled_ready", "sums_kept")
        (tops_on_row, tops_read, scales_exp, scales_ready, cols_made, cols_kept, parts_step, parts_ready, at_ready, merged_ps, merged_ready,
         den_ps_ready, msg_in, msg_ps_ready, msg_ready, gates_ps, gate_rz, gate_n_in, gate_n_ready, result_T, result_ps,
         result_ready, stored) = S(
            "tops_on_row", "tops_read", "scales_exp", "scales_ready", "cols_made", "cols_kept", "parts_step", "parts_ready", "at_ready",
            "merged_ps", "merged_ready", "den_ps_ready", "msg_in", "msg_ps_ready", "msg_ready", "gates_ps",
            "gate_rz", "gate_n_in", "gate_n_ready", "result_T", "result_ps", "result_ready", "stored")

        onehot_ps = [banks[q][:, 0:256].bitcast(BF16).rearrange("p (t e) -> p t e", t=QUAD) for q in range(2)]
        feat_ps = [banks[q][0:2 * PARTS * ED, 256:384].bitcast(BF16)
                   .rearrange("p (t e) -> p t e", t=2) for q in range(2)]
        hidden_ps = [banks[3 + d][:, 0:2 * H1].rearrange("p (t f) -> p t f", t=2) for d in range(2)]
        score_T = banks[5][0:OCT, 0:P]
        node_ps = banks[2][0:OCT, 0:P]
        weight_ps = banks[5][:, 2 * P:2 * P + OCT]
        sum_ps = [banks[6 + q][0:D + 1, :].rearrange("p (t n) -> p t n", t=QUAD) for q in range(2)]
        first_ps = banks[0][:, 0:TILES]
        last_ps = banks[1][0:1, 0:TILES]

        marks = oh_lo
        turned_ps = [banks[q][:, 0:256].bitcast(BF16).rearrange("p (t e) -> p t e", t=QUAD)
                     for q in range(2)]
        gram_ps = [banks[2 + q][:, :].rearrange("p (t e) -> p t e", t=QUAD) for q in range(2)]
        start_ps = [banks[4 + q][:, 0:2 * QUAD * HI].rearrange("p (t s h) -> p t s h", t=QUAD, s=2)
                    for q in range(2)]
        count_ps = [banks[q][0:LO, 0:QUAD * HI].rearrange("p (t h) -> p t h", t=QUAD)
                    for q in range(2)]
        base_ps = banks[2][0:LO, 0:1]
        hcT_ps = banks[6][0:D, 0:LO]
        tab_ps = banks[7][0:LO, 0:2 * H1]

        block = ctx.enter_context(nc.Block())

        @block.sync
        def _(sp):
            sp.dma_start(src_i[:, :], src).then_inc(src_in, 16)
            sp.dma_start(wp[:, :], pack).then_inc(pack_in, 16)
            sp.dma_start(xs[:, :, :], x.rearrange("(p c) d -> p c d", c=HI)).then_inc(x_in, 16)
            sp.dma_start(dst_i[:, :], dst).then_inc(dst_in, 16)
            sp.dma_start(edges[:, :, :], rows.rearrange("p (t w) -> p t w", w=ROW)).then_inc(rows_in, 16)
            sp.wait_ge(h_ready, 3)
            sp.dma_start(src_table[NODES:NPAD, :], zero_rows[:, :]).then_inc(tables_out, 16)
            sp.wait_ge(tab_split_ready, PARTS)
            sp.dma_start(src_table[0:NODES, :].rearrange("(p c) f -> p (c f)", c=HI),
                         count[:, 0:HI * PARTS * H1]).then_inc(tables_out, 16)
            sp.dma_start(dst_table.rearrange("(p c) f -> p c f", c=HI),
                         tab_dst[:, :, :]).then_inc(tables_out, 16)
            sp.wait_ge(tables_out, 48)
            for par in range(2):
                sp.wait_ge(scattered[par], 16 * OCT * ((PAIRS + 1 - par) // 2))
            sorted_v = sorted_rows.rearrange("(p t) w -> p t w", t=TILES)
            sp.dma_start(entries[:, 0:2 * OCT, :], sorted_v[:, 0:2 * OCT, :]).then_inc(sorted_first, 16)
            sp.dma_start(entries[:, 2 * OCT:TILES, :], sorted_v[:, 2 * OCT:TILES, :]).then_inc(sorted_in, 16)

            def load_windows(j, par):
                i = j * 2 + par
                at = [sp.value_load(window_at[0:1, bass.ds(i * OCT + k, 1)], min_val=0, max_val=NODES - 1)
                      for k in range(OCT)]
                for k in range(OCT):
                    sp.dma_start(window[par][:, k, :], src_table[bass.ds(at[k], P), :]
                                 ).then_inc(window_in[par], 16)

            sp.wait_ge(prepared, 1)
            load_windows(0, 0)
            load_windows(0, 1)
            with sp.Fori(1, PAIRS // 2) as j:
                for par in range(2):
                    sp.wait_ge(hidden_ps_ready, j * (2 * QUAD) + (QUAD * par - QUAD))
                    load_windows(j, par)
            sp.wait_ge(hidden_ps_ready, (PAIRS - 2) * QUAD)
            load_windows(PAIRS // 2, 0)

            blocks = CHUNKS * CHUNK // SUB
            whole = (blocks - 1) * SUB
            sp.wait_ge(rest_cleared, 1)
            sp.dma_start(x_out[:, 0:blocks - 1, :], x[0:whole, :].rearrange("(k p) d -> p k d", p=SUB)
                         ).then_inc(x_again, 16)
            sp.dma_start(x_out[0:NODES - whole, blocks - 1, :], x[whole:NODES, :]).then_inc(x_again, 16)
            sp.wait_ge(result_ready, CHUNKS)
            sp.dma_start(out[0:whole, :].rearrange("(k p) d -> p k d", p=SUB), result[:, 0:blocks - 1, :]
                         ).then_inc(stored, 16)
            sp.dma_start(out[whole:NODES, :], result[0:NODES - whole, blocks - 1, :]).then_inc(stored, 16)
            sp.wait_ge(stored, 32)

        @block.gpsimd
        def _(pool):
            g = nc.gpsimd
            st = Steps(pool, pool_step)

            def wide(a):
                return a[:, :].unsqueeze(2).broadcast_to((LO, HI, D))

            def fold(n):
                while n:
                    st.link(g.tensor_tensor(h[:, :, 0:n], h[:, :, 0:n], h[:, :, n:2 * n], ALU.add))
                    n //= 2

            pool.wait_ge(x_in, 16)
            st.link(g.tensor_tensor(h[:, :, 0:D // 2], xs[:, :, 0:D // 2], xs[:, :, D // 2:D], ALU.add))
            fold(D // 4)
            st.link(g.tensor_scalar(mean[:, :], h[:, :, 0], 1.0 / D, None, ALU.mult))
            st.link(g.tensor_tensor(xs[:, :, :], xs[:, :, :], wide(mean), ALU.subtract))
            st.link(g.tensor_tensor(h[:, :, :], xs[:, :, :], xs[:, :, :], ALU.mult))
            fold(D // 2)
            g.tensor_scalar(var[:, :], h[:, :, 0], 1.0 / D, EPS, ALU.mult, ALU.add).then_inc(var_ready, 1)
            pool.wait_ge(rstd_ready, 1)
            st.link(g.tensor_tensor(h[:, :, :], xs[:, :, :], wide(rstd), ALU.mult))
            g.tensor_scalar(h[:, :, :], h[:, :, :], 0.0, None, ALU.max).then_inc(h_ready, 1)
            g.memset(zero_rows[:, :], 0.0).then_inc(h_ready, 1)
            pool.wait_ge(h_ready, 2)
            g.tensor_copy(tab_dst[:, :, H1:TAB], h[:, :, :]).then_inc(h_ready, 1)

            def scatter(j, par):
                pool.wait_ge(h_ready, 1)
                pool.wait_ge(addr_ready[par], j + 1)
                pool.wait_ge(edge_split, j * 2 + (par + 1))
                pool.nop(nofuse=True)
                for k in range(OCT):
                    g.indirect_dma_start(
                        sorted_rows, bass.IndirectOffsetOnAxis(ap=addr[par][:, k:k + 1], axis=0),
                        pay[par][:, k, :], None).then_inc(scattered[par], 16)

            with pool.Fori(0, PAIRS // 2) as j:
                for par in range(2):
                    scatter(j, par)
            scatter(PAIRS // 2, 0)
            def gather(j, par):
                pool.wait_ge(h_ready, 1)
                pool.wait_ge(dst_ready[par], j + 1)
                pool.nop(nofuse=True)
                for k in range(OCT):
                    g.indirect_dma_start(
                        got[par][:, k, :], None, dst_table,
                        bass.IndirectOffsetOnAxis(ap=dst_at[par][:, k:k + 1], axis=0)).then_inc(gathered[par], 16)

            pool.wait_ge(tables_out, 48)
            with pool.Fori(0, PAIRS // 2) as j:
                for par in range(2):
                    gather(j, par)
            gather(PAIRS // 2, 0)

        @block.scalar
        def _(act):
            s = nc.scalar
            st = Steps(act, act_step)
            act.wait_ge(var_ready, 1)
            s.activation(std[:, :], var[:, :], ACT.Sqrt).then_inc(std_ready, 1)

            with act.Fori(0, PAIRS) as i:
                for q in range(2):
                    act.wait_ge(counted[q], i + 1)
                    t0 = i * OCT + q * QUAD
                    s.activation(count_v[:, :, bass.ds(t0, QUAD)], count_ps[q].rearrange("p t h -> p h t"),
                                 ACT.Copy, accum_out=total[:, bass.ds(i * 2 + q, 1)]
                                 ).then_inc(count_kept[q], 1)

            def keep_turned(j, q):
                act.wait_ge(ranked[q], j)
                t0 = j * OCT + q * QUAD
                s.activation(start_q[q][:, :, 0, :], start_v[:, bass.ds(t0, QUAD), :], ACT.Copy
                             ).then_inc(start_high[q], 1)
                act.wait_ge(turned[q], j + 1)
                s.activation(marked_T[q][:, :, :], turned_ps[q][0:LO], ACT.Copy).then_inc(turned_kept[q], 1)

            def keep_pay(j, par):
                act.wait_ge(scattered[par], j * 16 * OCT)
                i = j * 2 + par
                t0 = bass.ds(i * OCT, OCT)
                s.activation(parts(par)[:, :, 0, :], edges[:, t0, 0:ED], ACT.Copy).then_inc(edge_high, 1)
                s.activation(pay[par][:, :, C_VALID], edges[:, t0, ED], ACT.Copy)
                s.activation(pay[par][:, :, C_NODE], nodef[:, t0], ACT.Copy)
                s.activation(pay[par][:, :, C_DST], dst_f[:, t0], ACT.Copy)
                act.wait_ge(edge_rest_ready, i + 1)
                s.activation(parts(par)[:, :, 1, :], edge_rest[:, :, :], ACT.Copy).then_inc(edge_mid, 1)

            def rank_turn(j, par, last=False, c=None):
                i = j * 2 + par
                table = c is not None
                if table:
                    act.wait_ge(hcT_made, c)
                    s.activation(hc[:, :], h[:, bass.ds(c, 1), :].rearrange("p a d -> p (a d)"),
                                 ACT.Copy).then_inc(hc_ready, 1)
                keep_turned(i, 1)
                keep_pay(j, par)
                if table:
                    act.wait_ge(hcT_made, c + 1)
                    act.wait_ge(tab_made, c)
                    s.activation(hcT[0:D, :], hcT_ps, ACT.Copy).then_inc(hcT_ready, 1)
                    s.activation(hT[0:D, 0:NODES].rearrange("f (p c) -> f c p", c=HI)[:, bass.ds(c, 1), :],
                                 hcT_ps.unsqueeze(1), ACT.Copy).then_inc(hcT_ready, 1)
                if not last:
                    keep_turned(i + 1, 0)
                if table:
                    act.wait_ge(tab_made, c + 1)
                    st.mark(s.activation(tab_src[:, bass.ds(c, 1), :], tab_ps[:, 0:H1].unsqueeze(1), ACT.Copy))
                    s.activation(tab_dst[:, bass.ds(c, 1), 0:H1], tab_ps[:, H1:2 * H1].unsqueeze(1),
                                 ACT.Copy).then_inc(tab_kept, 1)

            act.wait_ge(start_ready, 1)
            keep_turned(0, 0)
            act.wait_ge(rows_ready, 1)
            act.wait_ge(rows_in, 16)
            rank_turn(0, 0)
            with act.Fori(0, TAB_AT // 2) as j:
                rank_turn(j, 1)
                rank_turn(j + 1, 0)
            act.wait_ge(h_ready, 1)
            with act.Fori(TAB_AT // 2, TAB_END // 2) as j:
                rank_turn(j, 1, c=j * 2 + 1 - TAB_AT)
                rank_turn(j + 1, 0, c=j * 2 + 2 - TAB_AT)
            with act.Fori(TAB_END // 2, PAIRS // 2 - 1) as j:
                rank_turn(j, 1)
                rank_turn(j + 1, 0)
            rank_turn(PAIRS // 2 - 1, 1, c=HI - 1)
            rank_turn(PAIRS // 2, 0, last=True)
            act.wait_ge(tab_kept, HI)
            s.activation(tab_split[:, :, 0, :], tab_src[:, :, :], ACT.Copy).then_inc(tab_split_ready, 1)
            act.wait_ge(tab_rest_ready, 1)
            s.activation(tab_split[:, :, 1, :], tab_src[:, :, :], ACT.Copy).then_inc(tab_split_ready, 1)
            st = Steps(act, late_act)

            def prepare(i):
                t0 = i * OCT
                for q in range(2):
                    act.wait_ge(feat_turned, i * 2 + (q - 1) if not isinstance(i, int) else max(0, 2 * i + q - 1))
                    s.activation(feat[q][:, :, :], entries[:, bass.ds(t0 + q * QUAD, QUAD), 0:C_VALID]
                                 .bitcast(BF16), ACT.Copy).then_inc(feat_ready, 1)
                act.wait_ge(node_turned, i)
                s.activation(node_q[:, :], node[:, bass.ds(t0, OCT)], ACT.Copy).then_inc(node_q_ready, 1)
                act.wait_ge(hidden_ps_ready, i * QUAD)
                for q in range(2):
                    act.wait_ge(feat_turned, i * 2 + (q + 1))
                    s.activation(onehot_T[q][:, :, :], onehot_ps[q], ACT.Copy)
                    s.activation(feat_T[q][:, :, :], feat_ps[q], ACT.Copy).then_inc(feat_T_kept, 1)
                act.wait_ge(node_turned, i + 1)
                act.wait_ge(power_from, i)
                s.activation(node_T[:, :], node_ps, ACT.Copy, scale=APART).then_inc(node_T_kept, 1)

            def power_of(i):
                act.wait_ge(power_from, i + 1)
                act.wait_ge(power_turned, i)
                s.activation(power[:, :], top[:, :], ACT.Exp).then_inc(power_ready, 1)

            def keep(j, par):
                i = j * 2 + par
                act.wait_ge(gathered[par], (j + 1) * (16 * OCT))
                act.wait_ge(scaled_ready, i - 1 if not isinstance(i, int) else max(0, i - 1))
                s.activation(feats[par][:, :, 0:D], got[par][:, :, H1:TAB], ACT.Copy).then_inc(feats_kept, 1)
                act.wait_ge(summed[par], j * 2)
                s.activation(onehot_f[par][:, :, :], onehot[par][:, :, :], ACT.Copy).then_inc(onehot_f_kept, 1)

            def keep_sums(j, par):
                i = j * 2 + par
                at = [act.value_load(window_at[0:1, bass.ds(i * OCT + k, 1)], min_val=0, max_val=NODES - 1)
                      for k in range(OCT)]
                for q in range(2):
                    act.wait_ge(summed[par], j * 2 + (q + 1))
                    s.activation(firsts[:, bass.ds(i * OCT + q * QUAD, QUAD)], sum_ps[q][:, :, 0], ACT.Copy)
                    for k in range(QUAD):
                        ins = s.activation(sums[:, bass.ds(at[q * QUAD + k] + 1, P - 1)],
                                           sum_ps[q][:, k, 1:P], ACT.Copy)
                        if k < QUAD - 1:
                            st.link(ins)
                    ins.then_inc(sums_kept, 1)
                    act.wait_ge(sums_kept, i * 2 + (q + 1))

            def turn(j, par, first=False, last=False):
                i = j * 2 + par
                if not first:
                    power_of(i - 1)
                keep(j, par)
                if not last:
                    prepare(i + 1)
                if not first:
                    keep_sums(j - 1 + par, 1 - par)

            act.wait_ge(prepared, 1)
            prepare(0)
            turn(0, 0, first=True)
            with act.Fori(0, PAIRS // 2 - 1) as j:
                for par in (1, 0):
                    st.base = j * (2 * KEEP_STEPS) + (1 - par) * KEEP_STEPS
                    st.n = 0
                    turn(j + 1 - par, par)
                    assert st.n == KEEP_STEPS, st.n
            st.base, st.n = 0, (PAIRS - 3) * KEEP_STEPS
            turn(PAIRS // 2 - 1, 1)
            turn(PAIRS // 2, 0, last=True)
            power_of(PAIRS - 1)
            keep_sums(PAIRS // 2, 0)

            act.wait_ge(scales_exp, 1)
            for n in ("scale_f", "scale_l"):
                s.activation(row[n][:, 0:TILES], row[n][:, 0:TILES], ACT.Exp).then_inc(scales_ready, 1)
            act.wait_ge(cols_made, 1)
            s.activation(col[:, :, :], banks[2][0:TB, 0:4 * NTB].rearrange("p (n b) -> p n b", n=4), ACT.Copy
                         ).then_inc(cols_kept, 1)
            s.activation(firsts_T[:, :, :], banks[3][0:TB, 0:NTB * (D + 1)].rearrange("p (b f) -> p b f", b=NTB),
                         ACT.Copy).then_inc(cols_kept, 1)
            with act.Fori(0, CHUNKS) as c:
                act.wait_ge(msg_ps_ready, c + 1)
                act.wait_ge(result_T, c)
                s.activation(msg[0:D, :], banks[3][0:D, 0:CHUNK], ACT.Copy).then_inc(msg_ready, 1)
                act.wait_ge(gates_ps, c + 1)
                s.activation(gate_r[:, :], banks[4][0:D, 0:CHUNK], ACT.Sigmoid).then_inc(gate_rz, 1)
                s.activation(gate_z[:, :], banks[5][0:D, 0:CHUNK], ACT.Sigmoid).then_inc(gate_rz, 1)
                act.wait_ge(gate_n_in, c + 1)
                s.activation(gate_n[:, :], new[:, :], ACT.Tanh).then_inc(gate_n_ready, 1)

        @block.tensor
        def _(pe):
            t = nc.tensor

            with pe.Fori(0, PAIRS) as i:
                for q in range(2):
                    pe.wait_ge(onehot_ready[q], i + 1)
                    pe.wait_ge(count_kept[q], i)
                    for k in range(QUAD):
                        ins = t.matmul(count_ps[q][:, k, :], oh_lo[q][:, k, 0:LO], oh_hi[q][:, k, :],
                                       start=True, stop=True)
                    ins.then_inc(counted[q], 1)
            pe.wait_ge(total_ready, 1)
            t.matmul(base_ps, const("before", LO)[:, 0:LO], total1[:, :], start=True, stop=True
                     ).then_inc(base_ready, 1)

            def turn(j, q):
                pe.wait_ge(marked[q], j + 1)
                pe.wait_ge(turned_kept[q], j)
                for k in range(QUAD):
                    ins = t.transpose(turned_ps[q][0:LO, k, :], marks[q][:, k, 0:LO], ident_b[:, :])
                ins.then_inc(turned[q], 1)

            def compare(i, q):
                pe.wait_ge(turned_kept[q], i + 1)
                pe.wait_ge(start_split[q], i + 1)
                pe.wait_ge(rank_read[q], i)
                for k in range(QUAD):
                    m = marked_T[q][:, k, :]
                    t.matmul(gram_ps[q][:, k, :], m, m, start=True, stop=True)
                    ins = t.matmul(start_ps[q][:, k, :, :], m, start_q[q][:, k, :, :], start=True, stop=True)
                ins.then_inc(ranked[q], 1)

            def rank_turn(i, last=False, c=None):
                table = c is not None
                if table:
                    pe.wait_ge(consts_ready, 1)
                    pe.wait_ge(hc_ready, c + 1)
                    pe.wait_ge(hcT_ready, c * 2)
                    pe.nop(nofuse=True)
                    t.transpose(hcT_ps, hc[:, :], ident[0:LO, 0:LO]).then_inc(hcT_made, 1)
                turn(i, 1)
                compare(i, 0)
                if table:
                    pe.wait_ge(hcT_ready, c * 2 + 1)
                    pe.wait_ge(tab_kept, c)
                    t.matmul(tab_ps, hcT[:, :], const("w1", D + 1), start=True, stop=True
                             ).then_inc(tab_made, 1)
                if not last:
                    turn(i + 1, 0)
                compare(i, 1)

            pe.wait_ge(consts_ready, 1)
            turn(0, 0)
            with pe.Fori(0, TAB_AT) as i:
                rank_turn(i)
            with pe.Fori(TAB_AT, TAB_END) as i:
                rank_turn(i, c=i - TAB_AT)
            with pe.Fori(TAB_END, PAIRS - 2) as i:
                rank_turn(i)
            rank_turn(PAIRS - 2, c=HI - 1)
            rank_turn(PAIRS - 1, last=True)
            pe.wait_ge(node_ready, 1)
            t.matmul(first_ps, const("first"), node[:, :], start=True, stop=True)
            t.matmul(last_ps, const("last"), node[:, :], start=True, stop=True).then_inc(firsts_ps_ready, 1)
            pe.wait_ge(prepared, 1)

            def turn_onehots(i):
                for q in range(2):
                    pe.wait_ge(onehot_made, i + 1)
                    pe.wait_ge(feat_T_kept, max(0, i * 2 + q - 1) if isinstance(i, int) else i * 2 + (q - 1))
                    for k in range(QUAD):
                        ins = t.transpose(onehot_ps[q][:, k, :], onehot_now(i)[:, q * QUAD + k, :], ident_b[:, :])
                    pe.wait_ge(feat_ready, i * 2 + (q + 1))
                    for d in range(2):
                        ins = t.transpose(feat_ps[q][:, d, :],
                                          feat[q][:, 2 * d:2 * d + 2, :].rearrange("p t f -> p (t f)"),
                                          ident_b[:, :])
                    ins.then_inc(feat_turned, 1)
                pe.wait_ge(node_q_ready, i + 1)
                pe.wait_ge(node_T_kept, i)
                pe.nop(nofuse=True)
                t.transpose(node_ps, node_q[:, :], ident).then_inc(node_turned, 1)

            slot = {}

            def onehot_now(i):
                return onehot[slot["par"]]

            def hidden_of(j, par):
                i = j * 2 + par
                for d in range(QUAD):
                    q = d // 2
                    if d == 0:
                        pe.wait_ge(window_in[par], (j + 1) * (16 * OCT))
                    if d % 2 == 0:
                        pe.wait_ge(feat_T_kept, i * 2 + (q + 1))
                    pe.wait_ge(hidden_read, i * QUAD + (d - 1) if not isinstance(i, int)
                               else max(0, i * QUAD + d - 1))
                    for e in range(2):
                        k = 2 * d + e
                        o = hidden_ps[d % 2][:, e, :]
                        for part in range(PARTS):
                            t.matmul(o, onehot_T[q][:, k % QUAD, :],
                                     window[par][:, k, part * H1:(part + 1) * H1],
                                     start=(part == 0), stop=False)
                        for part in range(PARTS):
                            ins = t.matmul(o, feat_T[q][:, (k % QUAD) // 2, :], edge_w[:, part, e, :],
                                           start=False, stop=(part == PARTS - 1))
                    ins.then_inc(hidden_ps_ready, 1)
                    if d == 2:
                        yield

            def score_turn(i):
                pe.wait_ge(masked_ready, i + 1)
                pe.nop(nofuse=True)
                t.transpose(score_T, masked[:, :], ident).then_inc(masked_turned, 1)

            def power_turn(i):
                pe.wait_ge(power_ready, i + 1)
                pe.nop(nofuse=True)
                t.transpose(weight_ps, power[:, :], ident[0:OCT, 0:OCT]).then_inc(power_turned, 1)

            def sum_turn(j, par):
                i = j * 2 + par
                pe.wait_ge(scaled_ready, i + 1)
                pe.wait_ge(onehot_f_kept, i + 1)
                for q in range(2):
                    pe.wait_ge(sums_kept, i * 2)
                    for k in range(QUAD):
                        ins = t.matmul(sum_ps[q][:, k, :], scaled[par][:, q * QUAD + k, :],
                                       onehot_f[par][:, q * QUAD + k, :], start=True, stop=True)
                    ins.then_inc(summed[par], 1)

            def turn_(j, par, first=False, last=False):
                i = j * 2 + par
                if not first:
                    score_turn(i - 1)
                steps = hidden_of(j, par)
                next(steps)
                if not first:
                    power_turn(i - 1)
                for _ in steps:
                    pass
                if not last:
                    slot["par"] = 1 - par
                    turn_onehots(i + 1)
                if not first:
                    sum_turn(j - 1 + par, 1 - par)

            slot["par"] = 0
            turn_onehots(0)
            turn_(0, 0, first=True)
            with pe.Fori(0, PAIRS // 2 - 1) as j:
                turn_(j, 1)
                turn_(j + 1, 0)
            turn_(PAIRS // 2 - 1, 1)
            turn_(PAIRS // 2, 0, last=True)
            score_turn(PAIRS - 1)
            power_turn(PAIRS - 1)
            sum_turn(PAIRS // 2, 0)

            for n in range(2):
                for r in range(OCT):
                    ins = t.matmul(banks[n][0:1, r * PAIRS:(r + 1) * PAIRS], ident[0:OCT, r:r + 1],
                                   piece_top[:, n, :], start=True, stop=True)
            ins.then_inc(tops_on_row, 1)
            pe.wait_ge(scales_ready, 3)
            for n, name in enumerate(("scale_f", "scale_l", "first", "last")):
                for b in range(NTB):
                    t.matmul(banks[2][0:TB, n * NTB + b:n * NTB + b + 1],
                             row[name][:, b * TB:(b + 1) * TB], ident[0:1, 0:1], start=True, stop=True)
            for b in range(NTB):
                ins = t.transpose(banks[3][0:TB, b * (D + 1):(b + 1) * (D + 1)], firsts[:, b * TB:(b + 1) * TB],
                                  ident[0:D + 1, 0:D + 1])
            ins.then_inc(cols_made, 1)
            pe.wait_ge(parts_ready, 1)
            with pe.Fori(0, CHUNKS) as c:
                cols = bass.ds(c * CHUNK, CHUNK)
                pe.wait_ge(at_ready, c + 1)
                pe.wait_ge(merged_ready, c)
                for bank, lhs, at in ((0, last_parts, at_last), (1, first_parts, at_first)):
                    for b in range(NTB):
                        for part in range(PARTS):
                            ins = t.matmul(banks[bank][0:D + 1, 0:CHUNK], lhs[:, b, part, :], at[:, b, :],
                                           start=(b == part == 0), stop=(b == NTB - 1 and part == PARTS - 1))
                ins.then_inc(merged_ps, 1)
                pe.wait_ge(merged_ready, c + 1)
                pe.wait_ge(result_ready, c)
                t.matmul(banks[2][0:D + 1, 0:CHUNK], const("spread", D + 1), merged[:, :],
                         start=True, stop=True).then_inc(den_ps_ready, 1)
                pe.wait_ge(msg_in, c + 1)
                t.matmul(banks[3][0:D, 0:CHUNK], const("wlin", D + 1), merged[:, :], start=True, stop=True
                         ).then_inc(msg_ps_ready, 1)
                wih, whh = const("wih", D + 1), const("whh", D + 1)
                pe.wait_ge(gate_rz, c * 2)
                pe.wait_ge(gate_n_in, c)
                for n, bank in ((0, 4), (1, 5), (2, 6)):
                    t.matmul(banks[bank][0:D, 0:CHUNK], wih[:, n * D:(n + 1) * D], hT[:, cols],
                             start=True, stop=(n == 2))
                pe.wait_ge(msg_ready, c + 1)
                for n, bank in ((0, 4), (1, 5), (2, 7)):
                    ins = t.matmul(banks[bank][0:D, 0:CHUNK], whh[:, n * D:(n + 1) * D], msg[:, :],
                                   start=(n == 2), stop=True)
                ins.then_inc(gates_ps, 1)
                pe.wait_ge(result_T, c + 1)
                pe.nop(nofuse=True)
                for k in range(CHUNK // SUB):
                    ins = t.transpose(banks[2][0:SUB, k * D:(k + 1) * D], new[:, k * SUB:(k + 1) * SUB],
                                      ident[0:D, 0:D])
                ins.then_inc(result_ps, 1)

        @block.vector
        def _(dve):
            v = nc.vector
            st = Steps(dve, dve_step)
            dve.wait_ge(src_in, 16)
            st.link(v.tensor_copy(nodef[:, :], src_i[:, :]))
            st.link(v.tensor_scalar(lo[:, :], nodef[:, :], 1.0 / HI, 0.5 / HI - 0.5, ALU.mult, ALU.add))
            st.link(v.tensor_scalar(lo[:, :], lo[:, :], MAGIC, None, ALU.add))
            st.link(v.tensor_scalar(lo[:, :], lo[:, :], MAGIC, None, ALU.subtract))
            st.link(v.scalar_tensor_tensor(out=hi[:, :], in0=lo[:, :], scalar=-float(HI), in1=nodef[:, :],
                                           op0=ALU.mult, op1=ALU.add))
            st.mark(v.tensor_copy(lo_b[:, :], lo[:, :]))
            dve.wait_ge(pack_in, 16)
            st.link(v.tensor_copy(iota_b[:, :], iota))
            st.link(v.tensor_copy(hi_b[:, :], hi[:, :]))
            st.link(v.tensor_copy(ident_b[:, :], ident))
            v.memset(hcT[D:D + 1, :], 1.0).then_inc(consts_ready, 1)

            with dve.Fori(0, PAIRS) as i:
                for q in range(2):
                    dve.wait_ge(counted[q], i)
                    t0 = bass.ds(i * OCT + q * QUAD, QUAD)
                    v.tensor_tensor(oh_hi[q][:, :, :], iota_b[:, 0:HI].unsqueeze(1).broadcast_to((P, QUAD, HI)),
                                    hi_b[:, t0].unsqueeze(2).broadcast_to((P, QUAD, HI)), ALU.is_equal)
                    v.tensor_tensor(oh_lo[q][:, :, :], iota_b[:, :].unsqueeze(1).broadcast_to((P, QUAD, P)),
                                    lo_b[:, t0].unsqueeze(2).broadcast_to((P, QUAD, P)), ALU.is_equal
                                    ).then_inc(onehot_ready[q], 1)
            st.link(v.tensor_scalar(hi1[:, :], hi[:, :], 1.0, None, ALU.add))
            st.mark(v.tensor_tensor(hi1sq[:, :], hi1[:, :], hi1[:, :], ALU.mult))
            st.mark(v.reciprocal(rhi[:, :], hi1[:, :]))
            for q in range(2):
                dve.wait_ge(count_kept[q], PAIRS)
            v.tensor_reduce(total1[:, :], total[:, :], AX.X, ALU.add).then_inc(total_ready, 1)
            dve.wait_ge(base_ready, 1)
            st.link(v.tensor_copy(start[:, 0:1], base_ps))
            v.tensor_tensor_scan(start[:, 1:HI * TILES + 1], count[:, :], count[:, :], start[:, 0:1],
                                 ALU.add, ALU.max).then_inc(start_ready, 1)
            dve.wait_ge(std_ready, 1)
            v.reciprocal(rstd[:, :], std[:, :]).then_inc(rstd_ready, 1)
            dve.wait_ge(dst_in, 16)
            for par in range(2):
                v.memset(pay[par][:, :, PAY - 1:PAY], 0.0)
            v.tensor_copy(dst_f[:, :], dst_i[:, :]).then_inc(rows_ready, 1)
            dve.wait_ge(rows_in, 16)

            def mark_nodes(j, q):
                dve.wait_ge(turned[q], j)
                for k in range(QUAD):
                    at = bass.ds(j * OCT + q * QUAD + k, 1)
                    ins = v.tensor_scalar(marks[q][:, k, :], iota_b[:, :], lo[:, at], hi1[:, at],
                                          ALU.is_equal, ALU.mult)
                ins.then_inc(marked[q], 1)

            def split_start(j, q):
                dve.wait_ge(start_high[q], j + 1)
                v.tensor_tensor(start_q[q][:, :, 1, :], start_v[:, bass.ds(j * OCT + q * QUAD, QUAD), :],
                                start_q[q][:, :, 0, :], ALU.subtract).then_inc(start_split[q], 1)

            def edge_first_rest(i, par):
                dve.wait_ge(edge_high, i + 1)
                v.tensor_tensor(edge_rest[:, :, :], edges[:, bass.ds(i * OCT, OCT), 0:ED],
                                parts(par)[:, :, 0, :], ALU.subtract).then_inc(edge_rest_ready, 1)

            def edge_last_rest(i, par):
                dve.wait_ge(edge_mid, i + 1)
                v.tensor_tensor(parts(par)[:, :, 2, :], edge_rest[:, :, :], parts(par)[:, :, 1, :],
                                ALU.subtract).then_inc(edge_split, 1)

            def finish_steps(i):
                yield lambda: v.tensor_scalar(place[:, :], place[:, :], MAGIC, MAGIC, ALU.add, ALU.subtract)
                yield lambda: v.tensor_scalar(place_t[:, :], place[:, :], 1.0 / P, 0.5 / P - 0.5,
                                              ALU.mult, ALU.add)
                yield lambda: v.tensor_scalar(place_t[:, :], place_t[:, :], MAGIC, MAGIC, ALU.add, ALU.subtract)
                yield lambda: v.scalar_tensor_tensor(out=place_u[:, :], in0=place_t[:, :], scalar=-float(P),
                                                     in1=place[:, :], op0=ALU.mult, op1=ALU.add)

            def give_addresses(j, par):
                dve.wait_ge(scattered[par], j * 16 * OCT)
                v.scalar_tensor_tensor(out=addr[par][:, :], in0=place_u[:, :], scalar=float(TILES),
                                       in1=place_t[:, :], op0=ALU.mult, op1=ALU.add
                                       ).then_inc(addr_ready[par], 1)

            def rank_turn(j, par, first=False, last=False):
                i = j * 2 + par
                steps = finish_steps(i - 1) if not first else iter(())
                st.mark(v.tensor_tensor(
                    own_hi[:, :, :], iota[:, 0:HI].unsqueeze(1).broadcast_to((P, OCT, HI)),
                    hi[:, bass.ds(i * OCT, OCT)].unsqueeze(2).broadcast_to((P, OCT, HI)), ALU.is_equal))
                picked = st.n
                for q in range(2):
                    if not last:
                        mark_nodes(i + 1, q)
                    dve.wait_ge(ranked[q], i + 1)
                    for k in range(QUAD):
                        at = bass.ds(i * OCT + q * QUAD + k, 1)
                        r = q * QUAD + k
                        st.mark(v.scalar_tensor_tensor(
                            out=same[:, r, :], in0=gram_ps[q][:, k, :], scalar=hi1sq[:, at],
                            in1=const("after"), op0=ALU.is_equal, op1=ALU.mult, accum_out=rank[:, r:r + 1]))
                        step = next(steps, None)
                        if step:
                            st.link(step())
                    st.sync(picked)
                    half = slice(q * QUAD, (q + 1) * QUAD)
                    v.tensor_tensor(pick[:, half, :].rearrange("p t (s h) -> p t s h", s=2), start_ps[q],
                                    own_hi[:, half, :].unsqueeze(2).broadcast_to((P, QUAD, 2, HI)), ALU.mult
                                    ).then_inc(rank_read[q], 1)
                    if q == 0:
                        split_start(i, 1)
                    elif not last:
                        split_start(i + 1, 0)
                    if q == 0:
                        if not first:
                            give_addresses(j - 1 + par, 1 - par)
                        edge_first_rest(i, par)
                    else:
                        edge_last_rest(i, par)
                for q in range(2):
                    dve.wait_ge(rank_read[q], i + 1)
                if not first:
                    dve.wait_ge(addr_ready[1 - par], j + par)
                st.link(v.tensor_reduce(place[:, :], pick[:, :, :], AX.X, ALU.add))
                st.link(v.tensor_tensor(place[:, :], place[:, :], rhi[:, bass.ds(i * OCT, OCT)], ALU.mult))
                st.link(v.tensor_tensor(place[:, :], place[:, :], rank[:, :], ALU.add))

            for q in range(2):
                dve.wait_ge(counted[q], PAIRS)
            mark_nodes(0, 0)
            mark_nodes(0, 1)
            split_start(0, 0)
            rank_turn(0, 0, first=True)
            before = st.n
            with dve.Fori(0, PAIRS // 2 - 1) as j:
                for par in (1, 0):
                    st.base = j * (2 * RANK_STEPS) + (before + (1 - par) * RANK_STEPS)
                    st.n = 0
                    rank_turn(j + 1 - par, par)
                    assert st.n == RANK_STEPS, st.n
            st.base, st.n = 0, before + (PAIRS - 3) * RANK_STEPS
            rank_turn(PAIRS // 2 - 1, 1)
            rank_turn(PAIRS // 2, 0, last=True)
            for step in finish_steps(PAIRS - 1):
                st.link(step())
            give_addresses(PAIRS // 2, 0)
            dve.wait_ge(tab_split_ready, 1)
            v.tensor_tensor(tab_src[:, :, :], tab_src[:, :, :], tab_split[:, :, 0, :], ALU.subtract
                            ).then_inc(tab_rest_ready, 1)
            dve.wait_ge(tab_split_ready, 2)
            v.tensor_tensor(tab_split[:, :, 2, :], tab_src[:, :, :], tab_split[:, :, 1, :], ALU.subtract
                            ).then_inc(tab_split_ready, 1)
            st = Steps(dve, late_step)
            def give_dst(j, par):
                v.tensor_copy(dst_at[par][:, :], entries[:, bass.ds(j * (2 * OCT) + par * OCT, OCT), C_DST]
                              ).then_inc(dst_ready[par], 1)

            dve.wait_ge(sorted_first, 16)
            give_dst(0, 0)
            give_dst(0, 1)
            wedge = const("wedge", 2 * PARTS * ED).rearrange("p (s k f) -> p s k f", s=PARTS, k=2)
            st.link(v.tensor_copy(edge_w[:, :, :, :], wedge))
            st.link(v.tensor_tensor(edge_w_rest[:, :, :, :], wedge, edge_w[:, :, :, :], ALU.subtract))
            st.link(v.tensor_copy(edge_w[:, 1:3, :, :], edge_w_rest[:, 1:3, :, :]))
            st.link(v.tensor_tensor(edge_w_rest[:, 2, :, :], edge_w_rest[:, 2, :, :], edge_w[:, 2, :, :],
                                    ALU.subtract))
            st.mark(v.tensor_copy(edge_w[:, 2, :, :], edge_w_rest[:, 2, :, :]))
            v.memset(sums[:, :], 0.0)
            v.memset(hT[0:D, NODES:CHUNK * CHUNKS], 0.0)
            v.memset(hT[D:D + 1, :], 1.0)
            v.memset(x_out[:, CHUNKS * CHUNK // SUB - 1, :], 0.0).then_inc(rest_cleared, 1)
            for par in range(2):
                v.memset(feats[par][:, :, D:D + 1], 1.0)
            v.memset(step_T[:, 0:P + 1], -APART)
            dve.wait_ge(sorted_in, 16)
            v.tensor_copy(node[:, :], entries[:, :, C_NODE]).then_inc(node_ready, 1)
            st.mark(v.tensor_scalar(penalty[:, :], entries[:, :, C_VALID], 1.0, -DUMMY, ALU.subtract, ALU.mult))
            dve.wait_ge(firsts_ps_ready, 1)
            st.mark(v.tensor_tensor(local[:, :], node[:, :], first_ps, ALU.subtract))
            st.mark(v.tensor_copy(row["first"][:, 0:TILES], first_ps[0:1, :]))
            st.mark(v.tensor_copy(row["last"][:, 0:TILES], last_ps))
            v.tensor_copy(window_at[:, :], first_ps[0:1, :]).then_inc(prepared, 1)
            dve.wait_ge(prepared, 1)

            def make_onehots(j, par):
                i = j * 2 + par
                dve.wait_ge(onehot_f_kept, i - 1 if not isinstance(i, int) else max(0, i - 1))
                v.tensor_tensor(onehot[par][:, :, :], iota.unsqueeze(1).broadcast_to((P, OCT, P)),
                                local[:, bass.ds(i * OCT, OCT)].unsqueeze(2).broadcast_to((P, OCT, P)),
                                ALU.is_equal).then_inc(onehot_made, 1)

            def weigh_steps(j, par):
                i = j * 2 + par
                dve.wait_ge(node_T_kept, i + 1)
                st.mark(v.tensor_tensor(step_T[:, 1:P], node_T[:, 0:P - 1], node_T[:, 1:P], ALU.subtract))
                yield
                st.sync()
                dve.wait_ge(masked_turned, i + 1)
                st.mark(v.tensor_tensor_scan(ahead[:, :], step_T[:, 0:P], score_T, 10 * DUMMY, ALU.add, ALU.max))
                st.mark(v.tensor_tensor_scan(behind[:, ::-1], step_T[:, P:0:-1], score_T[:, ::-1],
                                             10 * DUMMY, ALU.add, ALU.max))
                yield
                st.sync()
                dve.wait_ge(power_ready, i)
                st.mark(v.tensor_tensor(ahead[:, :], ahead[:, :], behind[:, :], ALU.max))
                yield
                st.sync()
                st.mark(v.tensor_copy(piece_top[:, :, bass.ds(i, 1)], ahead[:, 0:P:P - 1].unsqueeze(2)))
                v.tensor_tensor(top[:, :], score_T, ahead[:, :], ALU.subtract).then_inc(power_from, 1)
                yield
                dve.wait_ge(power_turned, i + 1)
                st.mark(v.tensor_tensor(weight[:, :], weight_ps, entries[:, bass.ds(i * OCT, OCT), C_VALID],
                                        ALU.mult))
                yield
                st.sync()
                dve.wait_ge(feats_kept, i + 1)
                dve.wait_ge(summed[par], j * 2)
                v.tensor_tensor(scaled[par][:, :, :], feats[par][:, :, :],
                                weight[:, :].unsqueeze(2).broadcast_to((P, OCT, D + 1)), ALU.mult
                                ).then_inc(scaled_ready, 1)
                yield

            def score_tiles(i, d):
                for e in range(2):
                    k = 2 * d + e
                    st.mark(v.scalar_tensor_tensor(
                        out=weighed[:, k, :], in0=hidden[d % 2][:, e, :], scalar=0.0, in1=const("w2"),
                        op0=ALU.max, op1=ALU.mult, accum_out=score[:, k:k + 1]))

            def turn(j, par, first=False, last=False, early=True):
                i = j * 2 + par
                before = weigh_steps(j - 1 + par, 1 - par) if not first else iter(())
                dve.wait_ge(gathered[par], (j + 1) * (16 * OCT))
                marks_at = {}
                for d in range(QUAD):
                    dve.wait_ge(hidden_ps_ready, i * QUAD + (d + 1))
                    if d >= 2:
                        st.sync(marks_at[d - 2])
                    v.tensor_tensor(hidden[d % 2][:, :, :], hidden_ps[d % 2], got[par][:, 2 * d:2 * d + 2, 0:H1],
                                    ALU.add).then_inc(hidden_read, 1)
                    next(before, None)
                    if d:
                        dve.wait_ge(hidden_read, i * QUAD + d)
                        score_tiles(i, d - 1)
                        marks_at[d - 1] = st.n
                    next(before, None)
                if early:
                    dve.wait_ge(feats_kept, i + 1)
                    dve.wait_ge(hidden_read, i * QUAD + QUAD)
                    give_dst(j + 1, par)
                for _ in before:
                    pass
                if not last:
                    make_onehots(j + par, 1 - par)
                dve.wait_ge(hidden_read, i * QUAD + QUAD)
                score_tiles(i, QUAD - 1)
                st.sync()
                st.link(v.tensor_tensor(score[:, :], score[:, :], const("b2").broadcast_to((P, OCT)), ALU.add))
                st.link(v.tensor_tensor(score[:, :], score[:, :], entries[:, bass.ds(i * OCT, OCT), C_VALID],
                                        ALU.mult))
                dve.wait_ge(masked_turned, i)
                v.tensor_tensor(masked[:, :], score[:, :], penalty[:, bass.ds(i * OCT, OCT)], ALU.add
                                ).then_inc(masked_ready, 1)
                dve.wait_ge(masked_ready, i + 1)

            make_onehots(0, 0)
            turn(0, 0, first=True)
            before_loop = st.n
            with dve.Fori(0, PAIRS // 2 - 1) as j:
                for par in (1, 0):
                    st.base = j * (2 * TURN_STEPS) + (before_loop + (1 - par) * TURN_STEPS)
                    st.n = 0
                    turn(j + 1 - par, par)
                    assert st.n == TURN_STEPS, st.n
            st.base, st.n = 0, before_loop + (PAIRS - 3) * TURN_STEPS
            turn(PAIRS // 2 - 1, 1, early=False)
            turn(PAIRS // 2, 0, last=True, early=False)
            for _ in weigh_steps(PAIRS // 2, 0):
                pass

            dve.wait_ge(tops_on_row, 1)
            R = {n: a[:, 0:TILES] for n, a in row.items()}
            for n, name in enumerate(("top_first", "top_last")):
                st.mark(v.tensor_copy(R[name].rearrange("p (i r) -> p r i", r=OCT),
                                      banks[n][0:1, 0:TILES].rearrange("p (r i) -> p r i", r=OCT)))
            st.mark(v.memset(row["link"][:, :], 0.0))
            st.link(v.tensor_tensor(R["one"], R["first"], R["last"], ALU.is_equal))
            st.link(v.tensor_tensor(row["link"][:, 1:TILES], row["last"][:, 0:TILES - 1],
                                    row["first"][:, 1:TILES], ALU.is_equal))
            st.link(v.tensor_tensor(R["pass_f"], R["one"], R["link"], ALU.mult))
            st.link(v.tensor_tensor(R["pass_b"], R["one"], row["link"][:, 1:TILES + 1], ALU.mult))
            for name in ("pass_f", "pass_b"):
                st.link(v.tensor_scalar(R[name], R[name], 1.0, APART, ALU.subtract, ALU.mult))
            st.link(v.tensor_scalar(row["link"][:, :], row["link"][:, :], 1.0, APART, ALU.subtract, ALU.mult))
            st.mark(v.memset(row["run_b"][:, TILES:TILES + 1], 10 * DUMMY))
            st.mark(v.memset(row["run_f"][:, 0:1], 10 * DUMMY))
            st.mark(v.tensor_tensor_scan(row["run_f"][:, 1:TILES + 1], R["pass_f"], R["top_last"], 10 * DUMMY,
                                         ALU.add, ALU.max))
            st.link(v.tensor_tensor_scan(R["run_b"][:, ::-1], R["pass_b"][:, ::-1], R["top_first"][:, ::-1],
                                         10 * DUMMY, ALU.add, ALU.max))
            st.link(v.tensor_tensor(R["scale_f"], row["run_f"][:, 0:TILES], R["link"], ALU.add))
            st.link(v.tensor_tensor(R["scale_f"], R["scale_f"], R["run_b"], ALU.max))
            st.link(v.tensor_tensor(R["scale_f"], R["top_first"], R["scale_f"], ALU.subtract))
            st.link(v.tensor_tensor(R["scale_l"], row["run_b"][:, 1:TILES + 1], row["link"][:, 1:TILES + 1], ALU.add))
            st.link(v.tensor_tensor(R["scale_l"], R["scale_l"], row["run_f"][:, 1:TILES + 1], ALU.max))
            v.tensor_tensor(R["scale_l"], R["top_last"], R["scale_l"], ALU.subtract).then_inc(scales_exp, 1)
            dve.wait_ge(scales_ready, 2)
            st.link(v.tensor_scalar(R["scale_l"], R["scale_l"], 1.0, None, ALU.subtract))
            st.link(v.tensor_scalar(R["one"], R["one"], -1.0, 1.0, ALU.mult, ALU.add))
            v.tensor_tensor(R["scale_l"], R["scale_l"], R["one"], ALU.mult).then_inc(scales_ready, 1)
            dve.wait_ge(cols_kept, 2)
            st.mark(v.tensor_tensor(firsts_T[:, :, :], firsts_T[:, :, :],
                                    col[:, 0, :].unsqueeze(2).broadcast_to((TB, NTB, D + 1)), ALU.mult))
            st.link(v.tensor_copy(last_rep[:, :, :], col[:, 1, :].unsqueeze(2).broadcast_to((TB, NTB, D + 1))))
            for whole, split in ((firsts_T, first_parts), (last_rep, last_parts)):
                for part in range(PARTS):
                    st.link(v.tensor_copy(split[:, :, part, :], whole[:, :, :]))
                    if part < PARTS - 1:
                        st.link(v.tensor_tensor(whole[:, :, :], whole[:, :, :], split[:, :, part, :],
                                                ALU.subtract))
            v.memset(msg[D:D + 1, :], 1.0).then_inc(parts_ready, 1)
            dve.wait_ge(parts_ready, 1)

            before_loop = st.n
            iota_c = const("iota")
            with dve.Fori(0, CHUNKS) as c:
                st.base, st.n = c * CHUNK_STEPS + before_loop, 0
                cols = bass.ds(c * CHUNK, CHUNK)
                dve.wait_ge(merged_ps, c)
                for n, at in ((2, at_first), (3, at_last)):
                    ins = v.tensor_tensor(
                        at[:, :, :], iota_c[0:TB, :].unsqueeze(1).broadcast_to((TB, NTB, CHUNK)),
                        col[:, n, :].unsqueeze(2).broadcast_to((TB, NTB, CHUNK)), ALU.is_equal)
                ins.then_inc(at_ready, 1)
                dve.wait_ge(at_ready, c + 1)
                st.mark(v.tensor_scalar(col[:, 2:4, :], col[:, 2:4, :], float(CHUNK), None, ALU.subtract))
                dve.wait_ge(merged_ps, c + 1)
                st.link(v.scalar_tensor_tensor(out=merged[:, :], in0=banks[0][0:D + 1, 0:CHUNK], scalar=1.0,
                                               in1=sums[:, cols], op0=ALU.add, op1=ALU.mult))
                v.tensor_tensor(merged[:, :], merged[:, :], banks[1][0:D + 1, 0:CHUNK], ALU.add
                                ).then_inc(merged_ready, 1)
                dve.wait_ge(den_ps_ready, c + 1)
                st.mark(v.tensor_scalar(some[:, :], banks[2][0:D, 0:CHUNK], 0.5, None, ALU.is_gt))
                st.link(v.tensor_scalar(den[:, :], banks[2][0:D + 1, 0:CHUNK], 0.5, None, ALU.max))
                st.link(v.reciprocal(den[:, :], den[:, :]))
                v.tensor_tensor(merged[:, :], merged[:, :], den[:, :], ALU.mult).then_inc(msg_in, 1)
                dve.wait_ge(gate_rz, c * 2 + 2)
                dve.wait_ge(gates_ps, c + 1)
                dve.wait_ge(result_ps, c)
                st.link(v.tensor_tensor(new[:, :], banks[7][0:D, 0:CHUNK], gate_r[:, :], ALU.mult))
                v.tensor_tensor(new[:, :], new[:, :], banks[6][0:D, 0:CHUNK], ALU.add).then_inc(gate_n_in, 1)
                dve.wait_ge(gate_n_ready, c + 1)
                st.link(v.tensor_tensor(new[:, :], msg[0:D, :], gate_n[:, :], ALU.subtract))
                st.link(v.tensor_tensor(new[:, :], new[:, :], gate_z[:, :], ALU.mult))
                st.link(v.tensor_tensor(new[:, :], new[:, :], gate_n[:, :], ALU.add))
                st.link(v.tensor_tensor(new[:, :], new[:, :], some[:, :], ALU.mult))
                st.link(v.scalar_tensor_tensor(out=old[:, :], in0=some[:, :], scalar=1.0, in1=hT[0:D, cols],
                                               op0=ALU.subtract, op1=ALU.mult))
                v.tensor_tensor(new[:, :], new[:, :], old[:, :], ALU.subtract).then_inc(result_T, 1)
                dve.wait_ge(x_again, 32)
                dve.wait_ge(result_ps, c + 1)
                n_sub = CHUNK // SUB
                v.tensor_tensor(result[:, bass.ds(c * n_sub, n_sub), :],
                                banks[2][0:SUB, 0:n_sub * D].rearrange("p (k d) -> p k d", k=n_sub),
                                x_out[:, bass.ds(c * n_sub, n_sub), :], ALU.add).then_inc(result_ready, 1)
                assert st.n == CHUNK_STEPS, st.n


TURN_STEPS = 6 + OCT + 2
KEEP_STEPS = 2 * (QUAD - 1)
CHUNK_STEPS = 11
RANK_STEPS = 1 + OCT + 4 + 3


def layout(x, src, dst, edge_attr_16, **w):
    cut = FULL * P
    spare = EXTRA * P - NODES - (EDGES - cut)
    def per_partition(edges, first, last):
        rest = np.concatenate([first, edges[cut:], np.full(spare, last, edges.dtype)])
        return np.concatenate([edges[:cut].reshape(P, FULL), rest.reshape(P, EXTRA)], 1)

    src = per_partition(src, np.arange(NODES, dtype=src.dtype), NODES - 1)
    dst = per_partition(dst, np.zeros(NODES, dst.dtype), 0)
    rows = np.zeros((P, TILES, ROW), edge_attr_16.dtype)
    rows[:, :FULL, :ED] = edge_attr_16[:cut].reshape(P, FULL, ED)
    rows[:, :FULL, ED] = 1
    rest = np.zeros((EXTRA * P, ROW), rows.dtype)
    rest[NODES:NODES + EDGES - cut, :ED] = edge_attr_16[cut:]
    rest[NODES:NODES + EDGES - cut, ED] = 1
    rows[:, FULL:] = rest.reshape(P, EXTRA, ROW)

    w = {name[len("L0_gnn_"):]: a for name, a in w.items()}
    pack = np.zeros((P, PACK), np.float32)

    def put(name, a, row=0, col=0):
        at = LAYOUT[name][0] + col
        pack[row:row + a.shape[0], at:at + a.shape[1]] = a

    i = np.arange(P)
    put("ident", np.eye(P))
    put("before", i[:, None] < i[None, :])
    put("after", i[None, :] < i[:, None])
    put("iota", np.broadcast_to(np.arange(CHUNK), (P, CHUNK)))
    put("first", np.broadcast_to((i == 0)[:, None], (P, P)))
    put("last", (i == P - 1)[:, None])
    put("spread", np.ones((1, D + 1)), D)
    att = w["W_att1"]
    put("w1", att[:, :D].T)
    put("w1", att[:, D + ED:].T, 0, H1)
    put("w1", w["b_att1"][None], D, H1)
    for q in range(PARTS):
        for k in range(2):
            for s in range(PARTS - q):
                put("wedge", att[:, D:D + ED].T, (k * PARTS + s) * ED, (q * 2 + k) * H1)
    put("w2", np.broadcast_to(w["W_att2"], (P, H1)))
    put("b2", np.broadcast_to(w["b_att2"], (P, 1)))
    for name, weight, bias in (("wlin", "W_lin", "b_lin"), ("wih", "W_ih", "b_ih"), ("whh", "W_hh", "b_hh")):
        put(name, w[weight].T)
        put(name, w[bias][None], D)
    return {"x": x, "src": src, "dst": dst, "rows": rows.reshape(P, TILES * ROW), "pack": pack}


def kernel(**inputs):
    import concourse.bacc as bacc
    from concourse.bass_utils import run_bass_kernel_spmd

    nc = bacc.Bacc("TRN2", target_bir_lowering=False, num_devices=1)
    arrays, args = {}, []
    for name, a in layout(**inputs).items():
        a = np.ascontiguousarray(a)
        arrays[f"in_{name}_dram"] = a
        args.append(nc.dram_tensor(f"in_{name}_dram", a.shape, mybir.dt.from_np(a.dtype),
                                   kind="ExternalInput").ap())
    out = nc.dram_tensor("out_0_dram", (NODES, D), F32, kind="ExternalOutput").ap()
    gnn_kernel(nc, *args, out)
    r = run_bass_kernel_spmd(nc, [arrays], core_ids=[0])
    return r.results[0]["out_0_dram"]
```

```python
import numpy as np
import concourse.bass as bass
from concourse import mybir
from contextlib import ExitStack

F32 = mybir.dt.float32
BF16 = mybir.dt.bfloat16
I32 = mybir.dt.int32
U32 = mybir.dt.uint32
ALU = mybir.AluOpType
ACT = mybir.ActivationFunctionType
AX = mybir.AxisListType

P = 128
NODES = 3125
EDGES = 53125
D = 64
ED = 16
H1 = 2 * D + ED
FULL = EDGES // P
TILES = (EDGES + NODES + P - 1) // P
EXTRA = TILES - FULL
LO, HI = 125, 25
QUAD = 4
PAIRS = TILES // (2 * QUAD)
OCT = 2 * QUAD
ROW = ED + 1
PARTS = 3
PAY = 28
C_VALID, C_NODE, C_DST = PARTS * ED // 2, PARTS * ED // 2 + 1, PARTS * ED // 2 + 2
TAB = H1 + D
CHUNK, CHUNKS, SUB = 448, 7, 112
TAB_AT = 7
TAB_END = TAB_AT + HI - 1
NPAD = NODES + P
WIDE = 3264
MAGIC = 12582912.0
DUMMY = -1e30
TWO = NODES
APART = 1e33
EPS = 1e-5
TB = 110
NTB = TILES // TB

LAYOUT, _at = {}, 0
for _name, _n in [("ident", P), ("before", P), ("after", P), ("iota", CHUNK), ("first", P),
                  ("w1", 2 * H1), ("wedge", 3 * 2 * H1), ("w2", H1), ("b2", 1), ("wlin", D), ("wih", 3 * D),
                  ("whh", 3 * D), ("last", 1), ("spread", D + 1)]:
    LAYOUT[_name] = (_at, _at + _n)
    _at += _n
PACK = _at


class Steps:

    def __init__(self, engine, sem):
        self.engine, self.sem, self.base, self.n = engine, sem, 0, 0

    def mark(self, ins):
        ins.then_inc(self.sem, 1)
        self.n += 1

    def sync(self, n=None):
        self.engine.wait_ge(self.sem, self.base + (self.n if n is None else n))

    def link(self, ins):
        self.mark(ins)
        self.sync()


def gnn_kernel(nc, x, src, dst, rows, pack, out):
    sorted_rows = nc.dram_tensor("sorted_rows", (TILES * P, PAY), F32, kind="Internal").ap()
    src_table = nc.dram_tensor("src_table", (NPAD, PARTS * H1), BF16, kind="Internal").ap()
    dst_table = nc.dram_tensor("dst_table", (NODES, TAB), F32, kind="Internal").ap()

    ctx = ExitStack()
    with ctx:
        def sb(name, shape, dt=F32):
            return ctx.enter_context(nc.sbuf_tensor(name, shape, dt))

        def sem(name):
            return ctx.enter_context(nc.semaphore(name))

        banks = [ctx.enter_context(nc.psum_tensor(f"bank{i}", [P, 512], F32)) for i in range(8)]

        wp = sb("wp", [P, PACK])

        def const(name, parts=P):
            a, b = LAYOUT[name]
            return wp[0:parts, a:b]

        ident, iota = const("ident"), const("iota")[:, 0:P]
        iota_b = sb("iota_b", [P, P], BF16)
        ident_b = sb("ident_b", [P, P], BF16)

        hT = sb("hT", [D + 1, CHUNK * CHUNKS])
        early = ExitStack()

        def eb(name, shape, dt=F32):
            return early.enter_context(nc.sbuf_tensor(name, shape, dt))

        xs = eb("xs", [LO, HI, D])
        h = eb("h", [LO, HI, D])
        mean = eb("mean", [LO, HI])
        var = eb("var", [LO, HI])
        std = eb("std", [LO, HI])
        rstd = eb("rstd", [LO, HI])
        hc = eb("hc", [LO, D])
        hcT = eb("hcT", [D + 1, LO])
        tab_src = eb("tab_src", [LO, HI, H1])
        tab_dst = eb("tab_dst", [LO, HI, TAB])
        zero_rows = eb("zero_rows", [P, PARTS * H1], BF16)

        edges = eb("edges", [P, TILES, ROW])
        edge_rest = eb("edge_rest", [P, OCT, ED])
        src_i = eb("src_i", [P, TILES], I32)
        dst_i = eb("dst_i", [P, TILES], I32)
        dst_f = eb("dst_f", [P, TILES])
        lo = eb("lo", [P, TILES])
        hi = eb("hi", [P, TILES])
        hi1 = eb("hi1", [P, TILES])
        hi1sq = eb("hi1sq", [P, TILES])
        rhi = eb("rhi", [P, TILES])
        nodef = eb("nodef", [P, TILES])

        oh_lo = [eb(f"oh_lo{q}", [P, QUAD, P], BF16) for q in range(2)]
        oh_hi = [eb(f"oh_hi{q}", [P, QUAD, HI], BF16) for q in range(2)]
        lo_b = eb("lo_b", [P, TILES], BF16)
        hi_b = eb("hi_b", [P, TILES], BF16)
        count = eb("count", [LO, HI * TILES], BF16)
        tab_split = count[:, 0:HI * PARTS * H1].rearrange("p (c s f) -> p c s f", c=HI, s=PARTS)
        total = eb("total", [LO, 2 * PAIRS])
        total1 = eb("total1", [LO, 1])
        start = eb("start", [LO, HI * TILES + 1])

        marked_T = [eb(f"marked_T{q}", [LO, QUAD, P], BF16) for q in range(2)]
        start_q = [eb(f"start_q{q}", [LO, QUAD, 2, HI], BF16) for q in range(2)]
        same = eb("same", [P, OCT, P], BF16)
        rank = [eb(f"rank{par}", [P, OCT]) for par in range(2)]
        own_hi = eb("own_hi", [P, OCT, HI])
        pick = eb("pick", [P, OCT, 2 * HI])
        place = eb("place", [P, OCT])
        place_t = eb("place_t", [P, OCT])
        place_u = eb("place_u", [P, OCT])
        addr = [eb(f"addr{par}", [P, OCT], U32) for par in range(2)]
        pay = [eb(f"pay{par}", [P, OCT, PAY]) for par in range(2)]

        early.close()

        sums = sb("sums", [D + 1, WIDE])
        firsts = sb("firsts", [D + 1, TILES])
        piece_top = sb("piece_top", [OCT, 2, PAIRS])
        window_at = sb("window_at", [1, TILES // 2], I32)
        row = {n: sb(f"row_{n}", [1, TILES + 1]) for n in ("first", "last")}
        x_out = sb("x_out", [SUB, CHUNKS * CHUNK // SUB, D])
        result = sb("result", [SUB, CHUNKS * CHUNK // SUB, D])
        middle = ExitStack()

        def mb(name, shape, dt=F32):
            return middle.enter_context(nc.sbuf_tensor(name, shape, dt))

        entries = mb("entries", [P, TILES, PAY])
        node = mb("node", [P, TILES])
        local = mb("local", [P, TILES])
        penalty = mb("penalty", [P, TILES])
        edge_w = mb("edge_w", [2 * PARTS * ED, PARTS, 2, H1], BF16)
        edge_w_rest = mb("edge_w_rest", [2 * PARTS * ED, PARTS, 2, H1])

        dst_at = [mb(f"dst_at{par}", [P, OCT], U32) for par in range(2)]
        got = [mb(f"got{par}", [P, OCT, TAB]) for par in range(2)]
        window = [mb(f"window{par}", [P, OCT, PARTS * H1], BF16) for par in range(2)]
        onehot = [mb(f"onehot{par}", [P, OCT, P], BF16) for par in range(2)]
        onehot_f = [mb(f"onehot_f{par}", [P, OCT, P]) for par in range(2)]
        onehot_T = [[mb(f"onehot_T{par}{q}", [P, QUAD, P], BF16) for q in range(2)] for par in range(2)]
        feat = [mb(f"feat{q}", [P, QUAD, PARTS * ED], BF16) for q in range(2)]
        feat_T = [[mb(f"feat_T{par}{q}", [2 * PARTS * ED, 2, P], BF16) for q in range(2)] for par in range(2)]
        hidden = [mb(f"hidden{d}", [P, 2, H1]) for d in range(2)]
        weighed = mb("weighed", [P, OCT, H1], BF16)
        score = mb("score", [P, OCT])
        masked = mb("masked", [P, OCT])
        local_b = mb("local_b", [P, TILES], BF16)
        node_q = mb("node_q", [P, OCT])

        node_T = mb("node_T", [OCT, P])
        step_T = mb("step_T", [OCT, P + 1])
        ahead = mb("ahead", [OCT, P])
        behind = mb("behind", [OCT, P])
        top = mb("top", [OCT, P])
        power = mb("power", [OCT, P])
        weight = mb("weight", [P, OCT])
        feats = [mb(f"feats{par}", [P, OCT, D + 1]) for par in range(2)]
        scaled = [mb(f"scaled{par}", [P, OCT, D + 1]) for par in range(2)]

        middle.close()

        row |= {n: sb(f"row_{n}", [1, TILES + 1]) for n in
                ("top_first", "top_last", "link", "one", "pass_f", "pass_b", "run_f", "run_b",
                 "scale_f", "scale_l")}
        col = sb("col", [TB, 4, NTB])
        firsts_T = sb("firsts_T", [TB, NTB, D + 1])
        first_parts = sb("first_parts", [TB, NTB, PARTS, D + 1], BF16)
        last_rep = sb("last_rep", [TB, NTB, D + 1])
        last_parts = sb("last_parts", [TB, NTB, PARTS, D + 1], BF16)
        at_first = sb("at_first", [TB, NTB, CHUNK], BF16)
        at_last = sb("at_last", [TB, NTB, CHUNK], BF16)

        merged = sb("merged", [D + 1, CHUNK])
        den = sb("den", [D + 1, CHUNK])
        old = sb("old", [D, CHUNK])
        none = sb("none", [D, CHUNK], I32)
        msg = sb("msg", [D + 1, CHUNK])
        gate_r = sb("gate_r", [D, CHUNK])
        gate_z = sb("gate_z", [D, CHUNK])
        gate_n = sb("gate_n", [D, CHUNK])
        new = sb("new", [D, CHUNK])

        def parts(par):
            return pay[par][:, :, 0:C_VALID].bitcast(BF16).rearrange("p t (s f) -> p t s f", s=PARTS)

        count_v = count[:, :].rearrange("p (h t) -> p h t", h=HI)
        start_v = start[:, 0:HI * TILES].rearrange("p (h t) -> p t h", h=HI)

        def S(*names):
            return [sem(n) for n in names]

        x_in, src_in, dst_in, rows_in, pack_in = S("x_in", "src_in", "dst_in", "rows_in", "pack_in")
        dve_step, act_step, pool_step = S("dve_step", "act_step", "pool_step")
        var_ready, std_ready, rstd_ready, h_ready, rows_ready = S(
            "var_ready", "std_ready", "rstd_ready", "h_ready", "rows_ready")
        onehot_ready = S("onehot_ready0", "onehot_ready1")
        counted = S("counted0", "counted1")
        count_kept = S("count_kept0", "count_kept1")
        total_ready, base_ready, start_ready, consts_ready = S(
            "total_ready", "base_ready", "start_ready", "consts_ready")
        marked = S("marked0", "marked1")
        start_high = S("start_high0", "start_high1")
        start_split = S("start_split0", "start_split1")
        turned = S("turned0", "turned1")
        turned_kept = S("turned_kept0", "turned_kept1")
        ranked = S("ranked0", "ranked1")
        rank_read = S("rank_read0", "rank_read1")
        addr_ready = S("addr_ready_even", "addr_ready_odd")
        scattered = S("scattered_even", "scattered_odd")
        tab_split_ready, edge_high, edge_rest_ready, edge_mid, edge_split = S(
            "tab_split_ready", "edge_high", "edge_rest_ready", "edge_mid", "edge_split")
        tab_rest_ready = sem("tab_rest_ready")
        rest_cleared = sem("rest_cleared")
        col_moved, ident_ready = S("col_moved", "ident_ready")
        hc_ready, hcT_made, hcT_ready, tab_made, tab_kept, tables_out = S(
            "hc_ready", "hcT_made", "hcT_ready", "tab_made", "tab_kept", "tables_out")

        late_step = sem("late_step")
        sorted_first, sorted_in, x_again, piece_rows, node_ready, firsts_ps_ready, prepared, dst_ready0, dst_ready1 = S(
            "sorted_first", "sorted_in", "x_again", "piece_rows", "node_ready", "firsts_ps_ready", "prepared",
            "dst_ready_even", "dst_ready_odd")
        dst_ready = [dst_ready0, dst_ready1]
        gathered = [S("gathered_even0", "gathered_even1"), S("gathered_odd0", "gathered_odd1")]
        summed = S("summed_even", "summed_odd")
        sums_kept = S("sums_kept0", "sums_kept1")
        window_in = S("window_in_even", "window_in_odd")
        (onehot_made, feat_ready, feat_turned, feat_T_kept, hidden_ps_ready,
         hidden_read, scored, masked_ready, masked_turned, node_q_ready, node_turned, node_T_kept, node_T_read, power_from,
         power_ready, power_turned, weight_read, feats_kept, onehot_f_kept, scaled_ready) = S(
            "onehot_made", "feat_ready", "feat_turned", "feat_T_kept",
            "hidden_ps_ready", "hidden_read", "scored", "masked_ready", "masked_turned", "node_q_ready",
            "node_turned", "node_T_kept", "node_T_read", "power_from", "power_ready", "power_turned", "weight_read",
            "feats_kept", "onehot_f_kept", "scaled_ready")
        (tops_on_row, tops_read, scales_exp, scales_ready, cols_made, cols_kept, parts_step, parts_ready, at_ready, merged_ps, merged_ready,
         den_ps_ready, msg_in, msg_ps_ready, msg_ready, gates_ps, gate_rz, gate_n_in, gate_n_ready, result_T, result_ps,
         result_ready, stored) = S(
            "tops_on_row", "tops_read", "scales_exp", "scales_ready", "cols_made", "cols_kept", "parts_step", "parts_ready", "at_ready",
            "merged_ps", "merged_ready", "den_ps_ready", "msg_in", "msg_ps_ready", "msg_ready", "gates_ps",
            "gate_rz", "gate_n_in", "gate_n_ready", "result_T", "result_ps", "result_ready", "stored")

        onehot_ps = [banks[q][:, 0:256].bitcast(BF16).rearrange("p (t e) -> p t e", t=QUAD) for q in range(2)]
        feat_ps = [banks[q][0:2 * PARTS * ED, 256:384].bitcast(BF16)
                   .rearrange("p (t e) -> p t e", t=2) for q in range(2)]
        hidden_ps = [banks[3 + d][:, 0:2 * H1].rearrange("p (t f) -> p t f", t=2) for d in range(2)]
        score_T = banks[5][0:OCT, 0:P]
        node_ps = banks[2][0:OCT, 0:P]
        weight_ps = banks[5][:, 2 * P:2 * P + OCT]
        sum_ps = [banks[6 + q][0:D + 1, :].rearrange("p (t n) -> p t n", t=QUAD) for q in range(2)]
        first_ps = banks[0][:, 0:TILES]
        last_ps = banks[1][0:1, 0:TILES]

        marks = oh_lo
        turned_ps = [banks[q][:, 0:256].bitcast(BF16).rearrange("p (t e) -> p t e", t=QUAD)
                     for q in range(2)]
        gram_ps = [banks[2 + q][:, :].rearrange("p (t e) -> p t e", t=QUAD) for q in range(2)]
        start_ps = [banks[4 + q][:, 0:2 * QUAD * HI].rearrange("p (t s h) -> p t s h", t=QUAD, s=2)
                    for q in range(2)]
        count_ps = [banks[q][0:LO, 0:QUAD * HI].rearrange("p (t h) -> p t h", t=QUAD)
                    for q in range(2)]
        base_ps = banks[2][0:LO, 0:1]
        hcT_ps = banks[6][0:D, 0:LO]
        tab_ps = banks[7][0:LO, 0:2 * H1]

        def windows_of(engine, i):
            at = []
            for k in range(QUAD):
                two = engine.value_load(window_at[0:1, bass.ds(i * QUAD + k, 1)], min_val=0,
                                        max_val=TWO * (NODES - 1) + NODES - 1)
                at += [two % TWO, two // TWO]
            return at

        block = ctx.enter_context(nc.Block())

        @block.sync
        def _(sp):
            sp.dma_start(src_i[:, :], src).then_inc(src_in, 16)
            sp.dma_start(wp[:, :], pack).then_inc(pack_in, 16)
            sp.dma_start(xs[:, :, :], x.rearrange("(p c) d -> p c d", c=HI)).then_inc(x_in, 16)
            sp.dma_start(dst_i[:, :], dst).then_inc(dst_in, 16)
            sp.dma_start(edges[:, :, :], rows.rearrange("p (t w) -> p t w", w=ROW)).then_inc(rows_in, 16)
            sp.wait_ge(h_ready, 3)
            sp.dma_start(src_table[NODES:NPAD, :], zero_rows[:, :]).then_inc(tables_out, 16)
            sp.wait_ge(tab_split_ready, PARTS)
            sp.dma_start(src_table[0:NODES, :].rearrange("(p c) f -> p (c f)", c=HI),
                         count[:, 0:HI * PARTS * H1]).then_inc(tables_out, 16)
            sp.dma_start(dst_table.rearrange("(p c) f -> p c f", c=HI),
                         tab_dst[:, :, :]).then_inc(tables_out, 16)
            sp.wait_ge(tables_out, 48)
            for par in range(2):
                sp.wait_ge(scattered[par], 16 * OCT * ((PAIRS + 1 - par) // 2))
            sorted_v = sorted_rows.rearrange("(p t) w -> p t w", t=TILES)
            sp.dma_start(entries[:, 0:2 * OCT, :], sorted_v[:, 0:2 * OCT, :]).then_inc(sorted_first, 16)
            sp.dma_start(entries[:, 2 * OCT:TILES, :], sorted_v[:, 2 * OCT:TILES, :]).then_inc(sorted_in, 16)

            def load_windows(j, par):
                i = j * 2 + par
                at = windows_of(sp, i)
                for k in range(OCT):
                    sp.dma_start(window[par][:, k, :], src_table[bass.ds(at[k], P), :]
                                 ).then_inc(window_in[par], 16)

            sp.wait_ge(prepared, 1)
            load_windows(0, 0)
            load_windows(0, 1)
            with sp.Fori(1, PAIRS // 2) as j:
                for par in range(2):
                    sp.wait_ge(hidden_ps_ready, j * (2 * QUAD) + (QUAD * par - QUAD))
                    load_windows(j, par)
            sp.wait_ge(hidden_ps_ready, (PAIRS - 2) * QUAD)
            load_windows(PAIRS // 2, 0)

            blocks = CHUNKS * CHUNK // SUB
            whole = (blocks - 1) * SUB
            sp.wait_ge(rest_cleared, 1)
            sp.dma_start(x_out[:, 0:blocks - 1, :], x[0:whole, :].rearrange("(k p) d -> p k d", p=SUB)
                         ).then_inc(x_again, 16)
            sp.dma_start(x_out[0:NODES - whole, blocks - 1, :], x[whole:NODES, :]).then_inc(x_again, 16)
            sp.wait_ge(result_ready, CHUNKS)
            sp.dma_start(out[0:whole, :].rearrange("(k p) d -> p k d", p=SUB), result[:, 0:blocks - 1, :]
                         ).then_inc(stored, 16)
            sp.dma_start(out[whole:NODES, :], result[0:NODES - whole, blocks - 1, :]).then_inc(stored, 16)
            sp.wait_ge(stored, 32)

        @block.gpsimd
        def _(pool):
            g = nc.gpsimd
            st = Steps(pool, pool_step)

            def wide(a):
                return a[:, :].unsqueeze(2).broadcast_to((LO, HI, D))

            def fold(n):
                while n:
                    st.link(g.tensor_tensor(h[:, :, 0:n], h[:, :, 0:n], h[:, :, n:2 * n], ALU.add))
                    n //= 2

            pool.wait_ge(x_in, 16)
            st.link(g.tensor_tensor(h[:, :, 0:D // 2], xs[:, :, 0:D // 2], xs[:, :, D // 2:D], ALU.add))
            fold(D // 4)
            st.link(g.tensor_scalar(mean[:, :], h[:, :, 0], 1.0 / D, None, ALU.mult))
            st.link(g.tensor_tensor(xs[:, :, :], xs[:, :, :], wide(mean), ALU.subtract))
            st.link(g.tensor_tensor(h[:, :, :], xs[:, :, :], xs[:, :, :], ALU.mult))
            fold(D // 2)
            g.tensor_scalar(var[:, :], h[:, :, 0], 1.0 / D, EPS, ALU.mult, ALU.add).then_inc(var_ready, 1)
            pool.wait_ge(rstd_ready, 1)
            st.link(g.tensor_tensor(h[:, :, :], xs[:, :, :], wide(rstd), ALU.mult))
            g.tensor_scalar(h[:, :, :], h[:, :, :], 0.0, None, ALU.max).then_inc(h_ready, 1)
            g.memset(zero_rows[:, :], 0.0).then_inc(h_ready, 1)
            pool.wait_ge(h_ready, 2)
            g.tensor_copy(tab_dst[:, :, H1:TAB], h[:, :, :]).then_inc(h_ready, 1)

            def scatter(j, par):
                pool.wait_ge(h_ready, 1)
                pool.wait_ge(addr_ready[par], j + 1)
                pool.wait_ge(edge_split, j * 2 + (par + 1))
                pool.nop(nofuse=True)
                for k in range(OCT):
                    g.indirect_dma_start(
                        sorted_rows, bass.IndirectOffsetOnAxis(ap=addr[par][:, k:k + 1], axis=0),
                        pay[par][:, k, :], None).then_inc(scattered[par], 16)

            with pool.Fori(0, PAIRS // 2) as j:
                for par in range(2):
                    scatter(j, par)
            scatter(PAIRS // 2, 0)
            def gather(j, par):
                for q in range(2):
                    pool.wait_ge(dst_ready[par], j * 2 + (q + 1))
                    pool.nop(nofuse=True)
                    for k in range(q * QUAD, (q + 1) * QUAD):
                        g.indirect_dma_start(
                            got[par][:, k, :], None, dst_table,
                            bass.IndirectOffsetOnAxis(ap=dst_at[par][:, k:k + 1], axis=0)
                        ).then_inc(gathered[par][q], 16)

            pool.wait_ge(tables_out, 48)
            with pool.Fori(0, PAIRS // 2) as j:
                for par in range(2):
                    gather(j, par)
            gather(PAIRS // 2, 0)

            pool.wait_ge(cols_kept, 2)

            def find_tiles(c):
                pool.wait_ge(merged_ps, c)
                pool.nop(nofuse=True)
                for n, at in ((2, at_first), (3, at_last)):
                    for b in range(NTB):
                        ins = g.tensor_scalar(at[:, b, :], const("iota")[0:TB, :], col[:, n, b:b + 1], None,
                                              ALU.is_equal)
                ins.then_inc(at_ready, 1)
                pool.wait_ge(at_ready, c + 1)
                pool.nop(nofuse=True)
                g.tensor_scalar(col[:, 2:4, :], col[:, 2:4, :], float(CHUNK), None, ALU.subtract
                                ).then_inc(col_moved, 1)
                pool.wait_ge(col_moved, c + 1)

            with pool.Fori(0, CHUNKS) as c:
                find_tiles(c)

        @block.scalar
        def _(act):
            s = nc.scalar
            st = Steps(act, act_step)
            act.wait_ge(pack_in, 16)
            s.activation(ident_b[:, :], ident, ACT.Copy).then_inc(ident_ready, 1)

            with act.Fori(0, PAIRS) as i:
                for q in range(2):
                    act.wait_ge(counted[q], i + 1)
                    t0 = i * OCT + q * QUAD
                    s.activation(count_v[:, :, bass.ds(t0, QUAD)], count_ps[q].rearrange("p t h -> p h t"),
                                 ACT.Copy, accum_out=total[:, bass.ds(i * 2 + q, 1)]
                                 ).then_inc(count_kept[q], 1)

            act.wait_ge(var_ready, 1)
            s.activation(std[:, :], var[:, :], ACT.Sqrt).then_inc(std_ready, 1)

            def keep_turned(j, q):
                act.wait_ge(ranked[q], j)
                t0 = j * OCT + q * QUAD
                s.activation(start_q[q][:, :, 0, :], start_v[:, bass.ds(t0, QUAD), :], ACT.Copy
                             ).then_inc(start_high[q], 1)
                act.wait_ge(turned[q], j + 1)
                s.activation(marked_T[q][:, :, :], turned_ps[q][0:LO], ACT.Copy).then_inc(turned_kept[q], 1)

            def keep_pay(j, par):
                act.wait_ge(scattered[par], j * 16 * OCT)
                i = j * 2 + par
                t0 = bass.ds(i * OCT, OCT)
                s.activation(parts(par)[:, :, 0, :], edges[:, t0, 0:ED], ACT.Copy).then_inc(edge_high, 1)
                s.activation(pay[par][:, :, C_VALID], edges[:, t0, ED], ACT.Copy)
                s.activation(pay[par][:, :, C_NODE], nodef[:, t0], ACT.Copy)
                s.activation(pay[par][:, :, C_DST], dst_f[:, t0], ACT.Copy)
                act.wait_ge(edge_rest_ready, i + 1)
                s.activation(parts(par)[:, :, 1, :], edge_rest[:, :, :], ACT.Copy).then_inc(edge_mid, 1)

            def rank_turn(j, par, first=False, last=False, c=None):
                i = j * 2 + par
                table = c is not None
                if table:
                    act.wait_ge(hcT_made, c)
                    s.activation(hc[:, :], h[:, bass.ds(c, 1), :].rearrange("p a d -> p (a d)"),
                                 ACT.Copy).then_inc(hc_ready, 1)
                keep_turned(i, 1)
                if not first:
                    keep_pay(j - 1 + par, 1 - par)
                if table:
                    act.wait_ge(hcT_made, c + 1)
                    act.wait_ge(tab_made, c)
                    s.activation(hcT[0:D, :], hcT_ps, ACT.Copy).then_inc(hcT_ready, 1)
                    s.activation(hT[0:D, 0:NODES].rearrange("f (p c) -> f c p", c=HI)[:, bass.ds(c, 1), :],
                                 hcT_ps.unsqueeze(1), ACT.Copy).then_inc(hcT_ready, 1)
                if not last:
                    keep_turned(i + 1, 0)
                if table:
                    act.wait_ge(tab_made, c + 1)
                    s.activation(tab_src[:, bass.ds(c, 1), :], tab_ps[:, 0:H1].unsqueeze(1), ACT.Copy)
                    s.activation(tab_dst[:, bass.ds(c, 1), 0:H1], tab_ps[:, H1:2 * H1].unsqueeze(1),
                                 ACT.Copy).then_inc(tab_kept, 1)

            act.wait_ge(start_ready, 1)
            keep_turned(0, 0)
            act.wait_ge(rows_ready, 1)
            act.wait_ge(rows_in, 16)
            rank_turn(0, 0, first=True)
            with act.Fori(0, TAB_AT // 2) as j:
                rank_turn(j, 1)
                rank_turn(j + 1, 0)
            act.wait_ge(h_ready, 1)
            with act.Fori(TAB_AT // 2, TAB_END // 2) as j:
                rank_turn(j, 1, c=j * 2 + 1 - TAB_AT)
                rank_turn(j + 1, 0, c=j * 2 + 2 - TAB_AT)
            rank_turn(TAB_END // 2, 1, c=HI - 1)
            act.wait_ge(tab_kept, HI)
            s.activation(tab_split[:, :, 0, :], tab_src[:, :, :], ACT.Copy).then_inc(tab_split_ready, 1)
            rank_turn(TAB_END // 2 + 1, 0)
            act.wait_ge(tab_rest_ready, 1)
            s.activation(tab_split[:, :, 1, :], tab_src[:, :, :], ACT.Copy).then_inc(tab_split_ready, 1)
            with act.Fori(TAB_END // 2 + 1, PAIRS // 2 - 1) as j:
                rank_turn(j, 1)
                rank_turn(j + 1, 0)
            rank_turn(PAIRS // 2 - 1, 1)
            rank_turn(PAIRS // 2, 0, last=True)
            keep_pay(PAIRS // 2, 0)

            def stage_feats(i):
                for q in range(2):
                    act.wait_ge(feat_turned, i * 2 + (q - 1) if not isinstance(i, int) else max(0, 2 * i + q - 1))
                    s.activation(feat[q][:, :, :], entries[:, bass.ds(i * OCT + q * QUAD, QUAD), 0:C_VALID]
                                 .bitcast(BF16), ACT.Copy).then_inc(feat_ready, 1)

            def keep_turned_steps(i, par):
                act.wait_ge(hidden_ps_ready, i * QUAD - QUAD if not isinstance(i, int)
                            else max(0, i * QUAD - QUAD))
                for q in range(2):
                    act.wait_ge(feat_turned, i * 2 + (q + 1))
                    s.activation(onehot_T[par][q][:, :, :], onehot_ps[q], ACT.Copy)
                    yield
                    s.activation(feat_T[par][q][:, :, :], feat_ps[q], ACT.Copy).then_inc(feat_T_kept, 1)
                    yield

            def keep_feats(j, par, q):
                i = j * 2 + par
                act.wait_ge(gathered[par][q], j * (16 * QUAD) + 16 * QUAD)
                act.wait_ge(scaled_ready, i - 1 if not isinstance(i, int) else max(0, i - 1))
                half = slice(q * QUAD, (q + 1) * QUAD)
                s.activation(feats[par][:, half, 0:D], got[par][:, half, H1:TAB], ACT.Copy
                             ).then_inc(feats_kept, 1)

            def sum_steps(j, par):
                i = j * 2 + par
                at = windows_of(act, i)
                yield
                for q in range(2):
                    act.wait_ge(summed[par], j * 2 + (q + 1))
                    s.activation(firsts[:, bass.ds(i * OCT + q * QUAD, QUAD)], sum_ps[q][:, :, 0], ACT.Copy)
                    for k in range(QUAD):
                        act.wait_ge(sums_kept[q if k else 1 - q], i * QUAD + (k if k or not q else QUAD))
                        s.activation(sums[:, bass.ds(at[q * QUAD + k] + 1, P - 1)],
                                     sum_ps[q][:, k, 1:P], ACT.Copy).then_inc(sums_kept[q], 1)
                        yield

            def turn(j, par, first=False, second=False, last=False):
                i = j * 2 + par
                sums_of = sum_steps(j - 1, par) if not (first or second) else iter(())
                turned_of = keep_turned_steps(i + 1, 1 - par) if not last else iter(())
                if not last:
                    stage_feats(i + 1)
                act.wait_ge(node_turned, i)
                s.activation(node_q[:, :], node[:, bass.ds(i * OCT, OCT)], ACT.Copy).then_inc(node_q_ready, 1)
                keep_feats(j, par, 0)
                next(sums_of, None)
                next(turned_of, None)
                if not first:
                    act.wait_ge(power_from, i)
                    act.wait_ge(power_turned, i - 1 if not isinstance(i, int) else max(0, i - 1))
                    s.activation(power[:, :], top[:, :], ACT.Exp).then_inc(power_ready, 1)
                next(sums_of, None)
                for _ in range(3):
                    next(turned_of, None)
                    next(sums_of, None)
                keep_feats(j, par, 1)
                next(sums_of, None)
                act.wait_ge(node_turned, i + 1)
                act.wait_ge(node_T_read, i)
                s.activation(node_T[:, :], node_ps, ACT.Copy, scale=APART).then_inc(node_T_kept, 1)
                next(sums_of, None)
                act.wait_ge(summed[par], j * 2)
                act.wait_ge(onehot_made, i + 1)
                s.activation(onehot_f[par][:, 0:QUAD, :], onehot[par][:, 0:QUAD, :], ACT.Copy)
                next(sums_of, None)
                s.activation(onehot_f[par][:, QUAD:OCT, :], onehot[par][:, QUAD:OCT, :], ACT.Copy
                             ).then_inc(onehot_f_kept, 1)
                next(sums_of, None)

            act.wait_ge(prepared, 1)
            stage_feats(0)
            for _ in keep_turned_steps(0, 0):
                pass
            turn(0, 0, first=True)
            turn(0, 1, second=True)
            with act.Fori(0, PAIRS // 2 - 1) as j:
                for par in range(2):
                    turn(j + 1, par)
            turn(PAIRS // 2, 0, last=True)
            for _ in sum_steps(PAIRS // 2 - 1, 1):
                pass
            act.wait_ge(power_from, PAIRS)
            s.activation(power[:, :], top[:, :], ACT.Exp).then_inc(power_ready, 1)
            for _ in sum_steps(PAIRS // 2, 0):
                pass

            act.wait_ge(scales_exp, 1)
            for n in ("scale_f", "scale_l"):
                s.activation(row[n][:, 0:TILES], row[n][:, 0:TILES], ACT.Exp).then_inc(scales_ready, 1)
            act.wait_ge(cols_made, 1)
            s.activation(col[:, :, :], banks[2][0:TB, 0:4 * NTB].rearrange("p (n b) -> p n b", n=4), ACT.Copy
                         ).then_inc(cols_kept, 1)
            s.activation(firsts_T[:, :, :], banks[3][0:TB, 0:NTB * (D + 1)].rearrange("p (b f) -> p b f", b=NTB),
                         ACT.Copy).then_inc(cols_kept, 1)

            def gru_chunk(c):
                act.wait_ge(msg_ps_ready, c + 1)
                act.wait_ge(result_T, c)
                s.activation(msg[0:D, :], banks[3][0:D, 0:CHUNK], ACT.Copy).then_inc(msg_ready, 1)
                s.activation(old[:, :], hT[0:D, bass.ds(c * CHUNK, CHUNK)], ACT.Copy)
                act.wait_ge(gates_ps, c + 1)
                s.activation(gate_r[:, :], banks[4][0:D, 0:CHUNK], ACT.Sigmoid).then_inc(gate_rz, 1)
                s.activation(gate_z[:, :], banks[4][D:2 * D, 0:CHUNK], ACT.Sigmoid).then_inc(gate_rz, 1)
                act.wait_ge(gate_n_in, c + 1)
                s.activation(gate_n[:, :], new[:, :], ACT.Tanh).then_inc(gate_n_ready, 1)

            gru_chunk(0)
            with act.Fori(1, CHUNKS) as c:
                gru_chunk(c)

        @block.tensor
        def _(pe):
            t = nc.tensor

            with pe.Fori(0, PAIRS) as i:
                for q in range(2):
                    pe.wait_ge(onehot_ready[q], i + 1)
                    pe.wait_ge(count_kept[q], i)
                    for k in range(QUAD):
                        ins = t.matmul(count_ps[q][:, k, :], oh_lo[q][:, k, 0:LO], oh_hi[q][:, k, :],
                                       start=True, stop=True)
                    ins.then_inc(counted[q], 1)
            pe.wait_ge(total_ready, 1)
            t.matmul(base_ps, const("before", LO)[:, 0:LO], total1[:, :], start=True, stop=True
                     ).then_inc(base_ready, 1)

            def turn(j, q):
                pe.wait_ge(marked[q], j + 1)
                pe.wait_ge(turned_kept[q], j)
                for k in range(QUAD):
                    ins = t.transpose(turned_ps[q][0:LO, k, :], marks[q][:, k, 0:LO], ident_b[:, :])
                ins.then_inc(turned[q], 1)

            def compare(i, q):
                pe.wait_ge(turned_kept[q], i + 1)
                pe.wait_ge(start_split[q], i + 1)
                pe.wait_ge(rank_read[q], i)
                for k in range(QUAD):
                    m = marked_T[q][:, k, :]
                    t.matmul(gram_ps[q][:, k, :], m, m, start=True, stop=True)
                    ins = t.matmul(start_ps[q][:, k, :, :], m, start_q[q][:, k, :, :], start=True, stop=True)
                ins.then_inc(ranked[q], 1)

            def rank_turn(i, last=False, c=None):
                table = c is not None
                if table:
                    pe.wait_ge(consts_ready, 1)
                    pe.wait_ge(hc_ready, c + 1)
                    pe.wait_ge(hcT_ready, c * 2)
                    pe.nop(nofuse=True)
                    t.transpose(hcT_ps, hc[:, :], ident[0:LO, 0:LO]).then_inc(hcT_made, 1)
                turn(i, 1)
                compare(i, 0)
                if table:
                    pe.wait_ge(hcT_ready, c * 2 + 1)
                    pe.wait_ge(tab_kept, c)
                    t.matmul(tab_ps, hcT[:, :], const("w1", D + 1), start=True, stop=True
                             ).then_inc(tab_made, 1)
                if not last:
                    turn(i + 1, 0)
                compare(i, 1)

            pe.wait_ge(ident_ready, 1)
            turn(0, 0)
            with pe.Fori(0, TAB_AT) as i:
                rank_turn(i)
            with pe.Fori(TAB_AT, TAB_END) as i:
                rank_turn(i, c=i - TAB_AT)
            rank_turn(TAB_END, c=HI - 1)
            with pe.Fori(TAB_END + 1, PAIRS - 1) as i:
                rank_turn(i)
            rank_turn(PAIRS - 1, last=True)
            pe.wait_ge(node_ready, 1)
            t.matmul(first_ps, const("first"), node[:, :], start=True, stop=True)
            t.matmul(last_ps, const("last"), node[:, :], start=True, stop=True).then_inc(firsts_ps_ready, 1)
            pe.wait_ge(prepared, 1)

            def turn_onehots(i, par):
                for q in range(2):
                    pe.wait_ge(onehot_made, i + 1)
                    pe.wait_ge(feat_T_kept, max(0, i * 2 + q - 1) if isinstance(i, int) else i * 2 + (q - 1))
                    for k in range(QUAD):
                        ins = t.transpose(onehot_ps[q][:, k, :], onehot[par][:, q * QUAD + k, :], ident_b[:, :])
                    pe.wait_ge(feat_ready, i * 2 + (q + 1))
                    for d in range(2):
                        ins = t.transpose(feat_ps[q][:, d, :],
                                          feat[q][:, 2 * d:2 * d + 2, :].rearrange("p t f -> p (t f)"),
                                          ident_b[:, :])
                    ins.then_inc(feat_turned, 1)

            def turn_nodes(i):
                pe.wait_ge(node_q_ready, i + 1)
                pe.wait_ge(node_T_kept, i)
                pe.nop(nofuse=True)
                t.transpose(node_ps, node_q[:, :], ident).then_inc(node_turned, 1)

            def hidden_of(j, par, d):
                i = j * 2 + par
                q = d // 2
                if d == 0:
                    pe.wait_ge(window_in[par], (j + 1) * (16 * OCT))
                if d % 2 == 0:
                    pe.wait_ge(feat_T_kept, i * 2 + (q + 1))
                pe.wait_ge(hidden_read, i * QUAD + (d - 1) if not isinstance(i, int)
                           else max(0, i * QUAD + d - 1))
                for e in range(2):
                    k = 2 * d + e
                    o = hidden_ps[d % 2][:, e, :]
                    for part in range(PARTS):
                        t.matmul(o, onehot_T[par][q][:, k % QUAD, :],
                                 window[par][:, k, part * H1:(part + 1) * H1],
                                 start=(part == 0), stop=False)
                    for part in range(PARTS):
                        ins = t.matmul(o, feat_T[par][q][:, (k % QUAD) // 2, :], edge_w[:, part, e, :],
                                       start=False, stop=(part == PARTS - 1))
                ins.then_inc(hidden_ps_ready, 1)

            def score_turn(i):
                pe.wait_ge(masked_ready, i + 1)
                pe.nop(nofuse=True)
                t.transpose(score_T, masked[:, :], ident).then_inc(masked_turned, 1)

            def power_turn(i):
                pe.wait_ge(power_ready, i + 1)
                pe.nop(nofuse=True)
                t.transpose(weight_ps, power[:, :], ident[0:OCT, 0:OCT]).then_inc(power_turned, 1)

            def sum_turn(j, par):
                i = j * 2 + par
                pe.wait_ge(scaled_ready, i + 1)
                pe.wait_ge(onehot_f_kept, i + 1)
                for q in range(2):
                    pe.wait_ge(sums_kept[q], i * QUAD)
                    for k in range(QUAD):
                        ins = t.matmul(sum_ps[q][:, k, :], scaled[par][:, q * QUAD + k, :],
                                       onehot_f[par][:, q * QUAD + k, :], start=True, stop=True)
                    ins.then_inc(summed[par], 1)

            def turn_(j, par, first=False, second=False, last=False):
                i = j * 2 + par
                hidden_of(j, par, 0)
                if not first:
                    score_turn(i - 1)
                hidden_of(j, par, 1)
                if not (first or second):
                    sum_turn(j - 1, par)
                if not last:
                    turn_onehots(i + 1, 1 - par)
                turn_nodes(i)
                hidden_of(j, par, 2)
                hidden_of(j, par, 3)
                if not first:
                    power_turn(i - 1)

            turn_onehots(0, 0)
            turn_(0, 0, first=True)
            turn_(0, 1, second=True)
            with pe.Fori(0, PAIRS // 2 - 1) as j:
                turn_(j + 1, 0)
                turn_(j + 1, 1)
            turn_(PAIRS // 2, 0, last=True)
            score_turn(PAIRS - 1)
            sum_turn(PAIRS // 2 - 1, 1)
            power_turn(PAIRS - 1)
            sum_turn(PAIRS // 2, 0)

            for n in range(2):
                for r in range(OCT):
                    ins = t.matmul(banks[n][0:1, r * PAIRS:(r + 1) * PAIRS], ident[0:OCT, r:r + 1],
                                   piece_top[:, n, :], start=True, stop=True)
            ins.then_inc(tops_on_row, 1)
            pe.wait_ge(scales_ready, 3)
            for n, name in enumerate(("scale_f", "scale_l", "first", "last")):
                for b in range(NTB):
                    t.matmul(banks[2][0:TB, n * NTB + b:n * NTB + b + 1],
                             row[name][:, b * TB:(b + 1) * TB], ident[0:1, 0:1], start=True, stop=True)
            for b in range(NTB):
                ins = t.transpose(banks[3][0:TB, b * (D + 1):(b + 1) * (D + 1)], firsts[:, b * TB:(b + 1) * TB],
                                  ident[0:D + 1, 0:D + 1])
            ins.then_inc(cols_made, 1)
            pe.wait_ge(parts_ready, 1)
            wih, whh = const("wih", D + 1), const("whh", D + 1)

            def merge_chunk(c):
                pe.wait_ge(at_ready, c + 1)
                pe.wait_ge(merged_ready, c)
                for bank, lhs, at in ((0, last_parts, at_last), (1, first_parts, at_first)):
                    for b in range(NTB):
                        for part in range(PARTS):
                            ins = t.matmul(banks[bank][0:D + 1, 0:CHUNK], lhs[:, b, part, :], at[:, b, :],
                                           start=(b == part == 0), stop=(b == NTB - 1 and part == PARTS - 1))
                ins.then_inc(merged_ps, 1)

            def spread_den(c):
                pe.wait_ge(merged_ready, c + 1)
                pe.wait_ge(msg_in, c)
                t.matmul(banks[2][0:D + 1, 0:CHUNK], const("spread", D + 1), merged[:, :],
                         start=True, stop=True).then_inc(den_ps_ready, 1)

            def gru_chunk(c, more=True):
                cols = bass.ds(c * CHUNK, CHUNK)
                pe.wait_ge(gate_rz, c * 2)
                pe.wait_ge(gate_n_in, c)
                t.matmul(banks[4][:, 0:CHUNK], wih[:, 0:2 * D], hT[:, cols], start=True, stop=False)
                t.matmul(banks[6][0:D, 0:CHUNK], wih[:, 2 * D:3 * D], hT[:, cols], start=True, stop=True)
                pe.wait_ge(msg_in, c + 1)
                t.matmul(banks[3][0:D, 0:CHUNK], const("wlin", D + 1), merged[:, :], start=True, stop=True
                         ).then_inc(msg_ps_ready, 1)
                pe.wait_ge(msg_ready, c + 1)
                t.matmul(banks[4][:, 0:CHUNK], whh[:, 0:2 * D], msg[:, :], start=False, stop=True)
                t.matmul(banks[7][0:D, 0:CHUNK], whh[:, 2 * D:3 * D], msg[:, :], start=True, stop=True
                         ).then_inc(gates_ps, 1)
                if more:
                    merge_chunk(c + 1)
                pe.wait_ge(result_ready, c)
                pe.wait_ge(result_T, c + 1)
                pe.nop(nofuse=True)
                for k in range(CHUNK // SUB):
                    ins = t.transpose(banks[5][0:SUB, k * D:(k + 1) * D], new[:, k * SUB:(k + 1) * SUB],
                                      ident[0:D, 0:D])
                ins.then_inc(result_ps, 1)
                if more:
                    spread_den(c + 1)

            merge_chunk(0)
            spread_den(0)
            with pe.Fori(0, CHUNKS - 1) as c:
                gru_chunk(c)
            gru_chunk(CHUNKS - 1, more=False)

        @block.vector
        def _(dve):
            v = nc.vector
            st = Steps(dve, dve_step)
            dve.wait_ge(src_in, 16)
            st.link(v.tensor_copy(nodef[:, :], src_i[:, :]))
            st.link(v.tensor_scalar(lo[:, :], nodef[:, :], 1.0 / HI, 0.5 / HI - 0.5, ALU.mult, ALU.add))
            st.link(v.tensor_scalar(lo[:, :], lo[:, :], MAGIC, None, ALU.add))
            st.link(v.tensor_scalar(lo[:, :], lo[:, :], MAGIC, None, ALU.subtract))
            st.link(v.scalar_tensor_tensor(out=hi[:, :], in0=lo[:, :], scalar=-float(HI), in1=nodef[:, :],
                                           op0=ALU.mult, op1=ALU.add))
            st.mark(v.tensor_copy(lo_b[:, :], lo[:, :]))
            dve.wait_ge(pack_in, 16)
            st.link(v.tensor_copy(iota_b[:, :], iota))
            st.link(v.tensor_copy(hi_b[:, :], hi[:, :]))
            v.memset(hcT[D:D + 1, :], 1.0).then_inc(consts_ready, 1)

            with dve.Fori(0, PAIRS) as i:
                for q in range(2):
                    dve.wait_ge(counted[q], i)
                    t0 = bass.ds(i * OCT + q * QUAD, QUAD)
                    v.tensor_tensor(oh_hi[q][:, :, :], iota_b[:, 0:HI].unsqueeze(1).broadcast_to((P, QUAD, HI)),
                                    hi_b[:, t0].unsqueeze(2).broadcast_to((P, QUAD, HI)), ALU.is_equal)
                    v.tensor_tensor(oh_lo[q][:, :, :], iota_b[:, :].unsqueeze(1).broadcast_to((P, QUAD, P)),
                                    lo_b[:, t0].unsqueeze(2).broadcast_to((P, QUAD, P)), ALU.is_equal
                                    ).then_inc(onehot_ready[q], 1)
            st.link(v.tensor_scalar(hi1[:, :], hi[:, :], 1.0, None, ALU.add))
            st.mark(v.tensor_tensor(hi1sq[:, :], hi1[:, :], hi1[:, :], ALU.mult))
            st.mark(v.reciprocal(rhi[:, :], hi1[:, :]))
            for q in range(2):
                dve.wait_ge(count_kept[q], PAIRS)
            v.tensor_reduce(total1[:, :], total[:, :], AX.X, ALU.add).then_inc(total_ready, 1)
            dve.wait_ge(std_ready, 1)
            v.reciprocal(rstd[:, :], std[:, :]).then_inc(rstd_ready, 1)
            dve.wait_ge(base_ready, 1)
            st.link(v.tensor_copy(start[:, 0:1], base_ps))
            v.tensor_tensor_scan(start[:, 1:HI * TILES + 1], count[:, :], count[:, :], start[:, 0:1],
                                 ALU.add, ALU.max).then_inc(start_ready, 1)
            dve.wait_ge(dst_in, 16)
            for par in range(2):
                v.memset(pay[par][:, :, PAY - 1:PAY], 0.0)
            v.tensor_copy(dst_f[:, :], dst_i[:, :]).then_inc(rows_ready, 1)
            dve.wait_ge(rows_in, 16)

            def mark_nodes(j, q, run_step=lambda: None):
                dve.wait_ge(turned[q], j)
                for k in range(QUAD):
                    at = bass.ds(j * OCT + q * QUAD + k, 1)
                    ins = v.tensor_scalar(marks[q][:, k, :], iota_b[:, :], lo[:, at], hi1[:, at],
                                          ALU.is_equal, ALU.mult)
                    if k < QUAD - 1:
                        run_step()
                ins.then_inc(marked[q], 1)

            def split_start(j, q):
                dve.wait_ge(start_high[q], j + 1)
                v.tensor_tensor(start_q[q][:, :, 1, :], start_v[:, bass.ds(j * OCT + q * QUAD, QUAD), :],
                                start_q[q][:, :, 0, :], ALU.subtract).then_inc(start_split[q], 1)

            def edge_first_rest(i, par):
                dve.wait_ge(edge_high, i + 1)
                v.tensor_tensor(edge_rest[:, :, :], edges[:, bass.ds(i * OCT, OCT), 0:ED],
                                parts(par)[:, :, 0, :], ALU.subtract).then_inc(edge_rest_ready, 1)

            def edge_last_rest(i, par):
                dve.wait_ge(edge_mid, i + 1)
                v.tensor_tensor(parts(par)[:, :, 2, :], edge_rest[:, :, :], parts(par)[:, :, 1, :],
                                ALU.subtract).then_inc(edge_split, 1)

            def finish_steps(i, par):
                yield lambda: v.tensor_tensor(place[:, :], place[:, :], rhi[:, bass.ds(i * OCT, OCT)], ALU.mult)
                yield lambda: v.tensor_tensor(place[:, :], place[:, :], rank[par][:, :], ALU.add)
                yield lambda: v.tensor_scalar(place[:, :], place[:, :], MAGIC, MAGIC, ALU.add, ALU.subtract)
                yield lambda: v.tensor_scalar(place_t[:, :], place[:, :], 1.0 / P, 0.5 / P - 0.5,
                                              ALU.mult, ALU.add)
                yield lambda: v.tensor_scalar(place_t[:, :], place_t[:, :], MAGIC, MAGIC, ALU.add, ALU.subtract)
                yield lambda: v.scalar_tensor_tensor(out=place_u[:, :], in0=place_t[:, :], scalar=-float(P),
                                                     in1=place[:, :], op0=ALU.mult, op1=ALU.add)

            def give_addresses(j, par):
                dve.wait_ge(scattered[par], j * 16 * OCT)
                v.scalar_tensor_tensor(out=addr[par][:, :], in0=place_u[:, :], scalar=float(TILES),
                                       in1=place_t[:, :], op0=ALU.mult, op1=ALU.add
                                       ).then_inc(addr_ready[par], 1)

            def rank_turn(j, par, first=False, last=False):
                i = j * 2 + par
                steps = finish_steps(i - 1, 1 - par) if not first else iter(())
                done = []

                def run_step():
                    step = next(steps, None)
                    if step:
                        if done:
                            st.sync(done[-1])
                        st.mark(step())
                        done.append(st.n)

                st.mark(v.tensor_tensor(
                    own_hi[:, :, :], iota[:, 0:HI].unsqueeze(1).broadcast_to((P, OCT, HI)),
                    hi[:, bass.ds(i * OCT, OCT)].unsqueeze(2).broadcast_to((P, OCT, HI)), ALU.is_equal))
                picked = st.n
                if not first:
                    edge_first_rest(i - 1, 1 - par)
                for q in range(2):
                    if not last:
                        mark_nodes(i + 1, q, run_step)
                    dve.wait_ge(ranked[q], i + 1)
                    for k in range(QUAD):
                        at = bass.ds(i * OCT + q * QUAD + k, 1)
                        r = q * QUAD + k
                        run_step()
                        st.mark(v.scalar_tensor_tensor(
                            out=same[:, r, :], in0=gram_ps[q][:, k, :], scalar=hi1sq[:, at],
                            in1=const("after"), op0=ALU.is_equal, op1=ALU.mult,
                            accum_out=rank[par][:, r:r + 1]))
                    st.sync(picked)
                    half = slice(q * QUAD, (q + 1) * QUAD)
                    v.tensor_tensor(pick[:, half, :].rearrange("p t (s h) -> p t s h", s=2), start_ps[q],
                                    own_hi[:, half, :].unsqueeze(2).broadcast_to((P, QUAD, 2, HI)), ALU.mult
                                    ).then_inc(rank_read[q], 1)
                    if q == 0:
                        split_start(i, 1)
                    elif not last:
                        split_start(i + 1, 0)
                    if q == 0 and not first:
                        edge_last_rest(i - 1, 1 - par)
                        while len(done) < 6:
                            run_step()
                        st.sync(done[-1])
                        give_addresses(j - 1 + par, 1 - par)
                for q in range(2):
                    dve.wait_ge(rank_read[q], i + 1)
                if not first:
                    dve.wait_ge(addr_ready[1 - par], j + par)
                st.sync()
                st.link(v.tensor_reduce(place[:, :], pick[:, :, :], AX.X, ALU.add))

            for q in range(2):
                dve.wait_ge(counted[q], PAIRS)
            mark_nodes(0, 0)
            mark_nodes(0, 1)
            split_start(0, 0)
            rank_turn(0, 0, first=True)
            before = st.n

            def rank_turns(start, end):
                with dve.Fori(start, end) as j:
                    for par in (1, 0):
                        st.base = j * (2 * RANK_STEPS) + (before + (1 - par) * RANK_STEPS)
                        st.n = 0
                        rank_turn(j + 1 - par, par)
                        assert st.n == RANK_STEPS, st.n

            rank_turns(0, TAB_END // 2 + 1)
            dve.wait_ge(tab_split_ready, 1)
            v.tensor_tensor(tab_src[:, :, :], tab_src[:, :, :], tab_split[:, :, 0, :], ALU.subtract
                            ).then_inc(tab_rest_ready, 1)
            split_turn = TAB_END // 2 + 1
            st.base, st.n = 0, before + 2 * split_turn * RANK_STEPS
            rank_turn(split_turn, 1)
            rank_turn(split_turn + 1, 0)
            dve.wait_ge(tab_split_ready, 2)
            v.tensor_tensor(tab_split[:, :, 2, :], tab_src[:, :, :], tab_split[:, :, 1, :], ALU.subtract
                            ).then_inc(tab_split_ready, 1)
            rank_turns(split_turn + 1, PAIRS // 2 - 1)
            st.base, st.n = 0, before + (PAIRS - 3) * RANK_STEPS
            rank_turn(PAIRS // 2 - 1, 1)
            rank_turn(PAIRS // 2, 0, last=True)
            edge_first_rest(PAIRS - 1, 0)
            for step in finish_steps(PAIRS - 1, 0):
                st.link(step())
            edge_last_rest(PAIRS - 1, 0)
            give_addresses(PAIRS // 2, 0)
            st = Steps(dve, late_step)
            def give_dst(j, par, q):
                half = slice(q * QUAD, (q + 1) * QUAD)
                v.tensor_copy(dst_at[par][:, half],
                              entries[:, bass.ds(j * (2 * OCT) + (par * OCT + q * QUAD), QUAD), C_DST]
                              ).then_inc(dst_ready[par], 1)

            dve.wait_ge(sorted_first, 16)
            for par in range(2):
                for q in range(2):
                    give_dst(0, par, q)
            wedge = const("wedge", 2 * PARTS * ED).rearrange("p (s k f) -> p s k f", s=PARTS, k=2)
            st.link(v.tensor_copy(edge_w[:, :, :, :], wedge))
            st.link(v.tensor_tensor(edge_w_rest[:, :, :, :], wedge, edge_w[:, :, :, :], ALU.subtract))
            st.link(v.tensor_copy(edge_w[:, 1:3, :, :], edge_w_rest[:, 1:3, :, :]))
            st.link(v.tensor_tensor(edge_w_rest[:, 2, :, :], edge_w_rest[:, 2, :, :], edge_w[:, 2, :, :],
                                    ALU.subtract))
            st.mark(v.tensor_copy(edge_w[:, 2, :, :], edge_w_rest[:, 2, :, :]))
            v.memset(sums[:, :], 0.0)
            v.memset(hT[0:D, NODES:CHUNK * CHUNKS], 0.0)
            v.memset(hT[D:D + 1, :], 1.0)
            v.memset(x_out[:, CHUNKS * CHUNK // SUB - 1, :], 0.0).then_inc(rest_cleared, 1)
            for par in range(2):
                v.memset(feats[par][:, :, D:D + 1], 1.0)
            v.memset(step_T[:, 0:P + 1], -APART)
            dve.wait_ge(sorted_in, 16)
            v.tensor_copy(node[:, :], entries[:, :, C_NODE]).then_inc(node_ready, 1)
            st.link(v.tensor_scalar(penalty[:, :], entries[:, :, C_VALID], 1.0, -DUMMY, ALU.subtract, ALU.mult))
            st.mark(v.tensor_scalar(penalty[:, :], penalty[:, :], const("b2"), None, ALU.add))
            dve.wait_ge(firsts_ps_ready, 1)
            st.mark(v.tensor_tensor(local_b[:, :], node[:, :], first_ps, ALU.subtract))
            st.mark(v.tensor_copy(row["first"][:, 0:TILES], first_ps[0:1, :]))
            st.mark(v.tensor_copy(row["last"][:, 0:TILES], last_ps))
            st.sync()
            v.scalar_tensor_tensor(out=window_at[:, :], in0=row["first"][:, 1:TILES:2], scalar=float(TWO),
                                   in1=row["first"][:, 0:TILES:2], op0=ALU.mult, op1=ALU.add
                                   ).then_inc(prepared, 1)
            dve.wait_ge(prepared, 1)

            def make_onehots(j, par):
                i = j * 2 + par
                dve.wait_ge(onehot_f_kept, i - 1 if not isinstance(i, int) else max(0, i - 1))
                v.tensor_tensor(onehot[par][:, :, :], iota_b[:, :].unsqueeze(1).broadcast_to((P, OCT, P)),
                                local_b[:, bass.ds(i * OCT, OCT)].unsqueeze(2).broadcast_to((P, OCT, P)),
                                ALU.is_equal).then_inc(onehot_made, 1)

            def weigh_steps(j, par):
                i = j * 2 + par
                dve.wait_ge(node_T_kept, i + 1)
                v.tensor_tensor(step_T[:, 1:P], node_T[:, 0:P - 1], node_T[:, 1:P], ALU.subtract
                                ).then_inc(node_T_read, 1)
                yield
                dve.wait_ge(node_T_read, i + 1)
                dve.wait_ge(masked_turned, i + 1)
                st.mark(v.tensor_tensor_scan(ahead[:, :], step_T[:, 0:P], score_T, 10 * DUMMY, ALU.add, ALU.max))
                st.mark(v.tensor_tensor_scan(behind[:, ::-1], step_T[:, P:0:-1], score_T[:, ::-1],
                                             10 * DUMMY, ALU.add, ALU.max))
                at = st.n
                yield
                st.sync(at)
                dve.wait_ge(power_ready, i)
                st.mark(v.tensor_tensor(ahead[:, :], ahead[:, :], behind[:, :], ALU.max))
                at = st.n
                yield
                st.sync(at)
                st.mark(v.tensor_copy(piece_top[:, :, bass.ds(i, 1)], ahead[:, 0:P:P - 1].unsqueeze(2)))
                v.tensor_tensor(top[:, :], score_T, ahead[:, :], ALU.subtract).then_inc(power_from, 1)
                yield
                dve.wait_ge(power_turned, i + 1)
                st.mark(v.tensor_tensor(weight[:, :], weight_ps, entries[:, bass.ds(i * OCT, OCT), C_VALID],
                                        ALU.mult))
                at = st.n
                yield
                st.sync(at)
                dve.wait_ge(feats_kept, i * 2 + 2)
                dve.wait_ge(summed[par], j * 2)
                v.tensor_tensor(scaled[par][:, :, :], feats[par][:, :, :],
                                weight[:, :].unsqueeze(2).broadcast_to((P, OCT, D + 1)), ALU.mult
                                ).then_inc(scaled_ready, 1)
                yield

            def score_tiles(i, d):
                for e in range(2):
                    k = 2 * d + e
                    st.mark(v.scalar_tensor_tensor(
                        out=weighed[:, k, :], in0=hidden[d % 2][:, e, :], scalar=0.0, in1=const("w2"),
                        op0=ALU.max, op1=ALU.mult, accum_out=score[:, k:k + 1]))

            def turn(j, par, first=False, last=False, early=True):
                i = j * 2 + par
                before = weigh_steps(j - 1 + par, 1 - par) if not first else iter(())
                marks_at = {}

                def add_hidden(d):
                    if d % 2 == 0:
                        dve.wait_ge(gathered[par][d // 2], j * (16 * QUAD) + 16 * QUAD)
                    dve.wait_ge(hidden_ps_ready, i * QUAD + (d + 1))
                    if d >= 2:
                        st.sync(marks_at[d - 2])
                    v.tensor_tensor(hidden[d % 2][:, :, :], hidden_ps[d % 2], got[par][:, 2 * d:2 * d + 2, 0:H1],
                                    ALU.add).then_inc(hidden_read, 1)

                def score_tiles(d):
                    dve.wait_ge(hidden_read, i * QUAD + (d + 1))
                    for e in range(2):
                        k = 2 * d + e
                        st.mark(v.scalar_tensor_tensor(
                            out=weighed[:, k, :], in0=hidden[d % 2][:, e, :], scalar=0.0, in1=const("w2"),
                            op0=ALU.max, op1=ALU.mult, accum_out=score[:, k:k + 1]))
                    marks_at[d] = st.n

                next(before, None)
                add_hidden(0)
                if not last:
                    make_onehots(j + par, 1 - par)
                score_tiles(0)
                next(before, None)
                add_hidden(1)
                next(before, None)
                score_tiles(1)
                if early:
                    dve.wait_ge(feats_kept, i * 2 + 1)
                    give_dst(j + 1, par, 0)
                next(before, None)
                add_hidden(2)
                add_hidden(3)
                score_tiles(2)
                next(before, None)
                score_tiles(3)
                if early:
                    dve.wait_ge(feats_kept, i * 2 + 2)
                    give_dst(j + 1, par, 1)
                next(before, None)
                st.sync()
                dve.wait_ge(masked_turned, i)
                v.tensor_tensor(masked[:, :], score[:, :], penalty[:, bass.ds(i * OCT, OCT)], ALU.add
                                ).then_inc(masked_ready, 1)

            make_onehots(0, 0)
            turn(0, 0, first=True)
            before_loop = st.n
            with dve.Fori(0, PAIRS // 2 - 1) as j:
                for par in (1, 0):
                    st.base = j * (2 * TURN_STEPS) + (before_loop + (1 - par) * TURN_STEPS)
                    st.n = 0
                    turn(j + 1 - par, par)
                    assert st.n == TURN_STEPS, st.n
            st.base, st.n = 0, before_loop + (PAIRS - 3) * TURN_STEPS
            turn(PAIRS // 2 - 1, 1, early=False)
            turn(PAIRS // 2, 0, last=True, early=False)
            for _ in weigh_steps(PAIRS // 2, 0):
                pass

            dve.wait_ge(tops_on_row, 1)
            R = {n: a[:, 0:TILES] for n, a in row.items()}
            for n, name in enumerate(("top_first", "top_last")):
                st.mark(v.tensor_copy(R[name].rearrange("p (i r) -> p r i", r=OCT),
                                      banks[n][0:1, 0:TILES].rearrange("p (r i) -> p r i", r=OCT)))
            st.mark(v.memset(row["link"][:, :], 0.0))
            st.link(v.tensor_tensor(R["one"], R["first"], R["last"], ALU.is_equal))
            st.link(v.tensor_tensor(row["link"][:, 1:TILES], row["last"][:, 0:TILES - 1],
                                    row["first"][:, 1:TILES], ALU.is_equal))
            st.link(v.tensor_tensor(R["pass_f"], R["one"], R["link"], ALU.mult))
            st.link(v.tensor_tensor(R["pass_b"], R["one"], row["link"][:, 1:TILES + 1], ALU.mult))
            for name in ("pass_f", "pass_b"):
                st.link(v.tensor_scalar(R[name], R[name], 1.0, APART, ALU.subtract, ALU.mult))
            st.link(v.tensor_scalar(row["link"][:, :], row["link"][:, :], 1.0, APART, ALU.subtract, ALU.mult))
            st.mark(v.memset(row["run_b"][:, TILES:TILES + 1], 10 * DUMMY))
            st.mark(v.memset(row["run_f"][:, 0:1], 10 * DUMMY))
            st.mark(v.tensor_tensor_scan(row["run_f"][:, 1:TILES + 1], R["pass_f"], R["top_last"], 10 * DUMMY,
                                         ALU.add, ALU.max))
            st.link(v.tensor_tensor_scan(R["run_b"][:, ::-1], R["pass_b"][:, ::-1], R["top_first"][:, ::-1],
                                         10 * DUMMY, ALU.add, ALU.max))
            st.link(v.tensor_tensor(R["scale_f"], row["run_f"][:, 0:TILES], R["link"], ALU.add))
            st.link(v.tensor_tensor(R["scale_f"], R["scale_f"], R["run_b"], ALU.max))
            st.link(v.tensor_tensor(R["scale_f"], R["top_first"], R["scale_f"], ALU.subtract))
            st.link(v.tensor_tensor(R["scale_l"], row["run_b"][:, 1:TILES + 1], row["link"][:, 1:TILES + 1], ALU.add))
            st.link(v.tensor_tensor(R["scale_l"], R["scale_l"], row["run_f"][:, 1:TILES + 1], ALU.max))
            v.tensor_tensor(R["scale_l"], R["top_last"], R["scale_l"], ALU.subtract).then_inc(scales_exp, 1)
            dve.wait_ge(scales_ready, 2)
            st.link(v.tensor_scalar(R["scale_l"], R["scale_l"], 1.0, None, ALU.subtract))
            st.link(v.tensor_scalar(R["one"], R["one"], -1.0, 1.0, ALU.mult, ALU.add))
            v.tensor_tensor(R["scale_l"], R["scale_l"], R["one"], ALU.mult).then_inc(scales_ready, 1)
            dve.wait_ge(cols_kept, 2)
            st.mark(v.tensor_tensor(firsts_T[:, :, :], firsts_T[:, :, :],
                                    col[:, 0, :].unsqueeze(2).broadcast_to((TB, NTB, D + 1)), ALU.mult))
            st.link(v.tensor_copy(last_rep[:, :, :], col[:, 1, :].unsqueeze(2).broadcast_to((TB, NTB, D + 1))))
            for whole, split in ((firsts_T, first_parts), (last_rep, last_parts)):
                for part in range(PARTS):
                    st.link(v.tensor_copy(split[:, :, part, :], whole[:, :, :]))
                    if part < PARTS - 1:
                        st.link(v.tensor_tensor(whole[:, :, :], whole[:, :, :], split[:, :, part, :],
                                                ALU.subtract))
            v.memset(msg[D:D + 1, :], 1.0).then_inc(parts_ready, 1)
            dve.wait_ge(parts_ready, 1)


            def merge_chunk(c):
                dve.wait_ge(merged_ps, c + 1)
                st.link(v.scalar_tensor_tensor(out=merged[:, :], in0=banks[0][0:D + 1, 0:CHUNK], scalar=1.0,
                                               in1=sums[:, bass.ds(c * CHUNK, CHUNK)],
                                               op0=ALU.add, op1=ALU.mult))
                v.tensor_tensor(merged[:, :], merged[:, :], banks[1][0:D + 1, 0:CHUNK], ALU.add
                                ).then_inc(merged_ready, 1)

            def divide_chunk(c):
                dve.wait_ge(den_ps_ready, c + 1)
                st.mark(v.tensor_scalar(none[:, :], banks[2][0:D, 0:CHUNK], 0.5, None, ALU.is_lt))
                st.link(v.tensor_scalar(den[:, :], banks[2][0:D + 1, 0:CHUNK], 0.5, None, ALU.max))
                st.link(v.reciprocal(den[:, :], den[:, :]))
                v.tensor_tensor(merged[:, :], merged[:, :], den[:, :], ALU.mult).then_inc(msg_in, 1)

            def gru_chunk(c, more=True):
                dve.wait_ge(gate_rz, c * 2 + 2)
                dve.wait_ge(gates_ps, c + 1)
                dve.wait_ge(result_ps, c)
                st.link(v.tensor_tensor(new[:, :], banks[7][0:D, 0:CHUNK], gate_r[:, :], ALU.mult))
                v.tensor_tensor(new[:, :], new[:, :], banks[6][0:D, 0:CHUNK], ALU.add).then_inc(gate_n_in, 1)
                dve.wait_ge(gate_n_ready, c + 1)
                st.link(v.tensor_tensor(new[:, :], msg[0:D, :], gate_n[:, :], ALU.subtract))
                st.link(v.tensor_tensor(new[:, :], new[:, :], gate_z[:, :], ALU.mult))
                st.link(v.tensor_tensor(new[:, :], new[:, :], gate_n[:, :], ALU.add))
                dve.nop(nofuse=True)
                v.copy_predicated(new[:, :], none[:, :], old[:, :]).then_inc(result_T, 1)
                if more:
                    dve.wait_ge(msg_ps_ready, c + 1)
                    merge_chunk(c + 1)
                dve.wait_ge(x_again, 32)
                dve.wait_ge(result_ps, c + 1)
                n_sub = CHUNK // SUB
                v.tensor_tensor(result[:, bass.ds(c * n_sub, n_sub), :],
                                banks[5][0:SUB, 0:n_sub * D].rearrange("p (k d) -> p k d", k=n_sub),
                                x_out[:, bass.ds(c * n_sub, n_sub), :], ALU.add).then_inc(result_ready, 1)
                if more:
                    dve.wait_ge(result_T, c + 1)
                    divide_chunk(c + 1)

            merge_chunk(0)
            divide_chunk(0)
            before_loop = st.n
            with dve.Fori(0, CHUNKS - 1) as c:
                st.base, st.n = c * CHUNK_STEPS + before_loop, 0
                gru_chunk(c)
                assert st.n == CHUNK_STEPS, st.n
            st.base, st.n = 0, before_loop + (CHUNKS - 1) * CHUNK_STEPS
            gru_chunk(CHUNKS - 1, more=False)


TURN_STEPS = 5 + OCT
CHUNK_STEPS = 8
RANK_STEPS = 1 + OCT + 6 + 1


def layout(x, src, dst, edge_attr_16, **w):
    cut = FULL * P
    spare = EXTRA * P - NODES - (EDGES - cut)
    def per_partition(edges, first, last):
        rest = np.concatenate([first, edges[cut:], np.full(spare, last, edges.dtype)])
        return np.concatenate([edges[:cut].reshape(P, FULL), rest.reshape(P, EXTRA)], 1)

    src = per_partition(src, np.arange(NODES, dtype=src.dtype), NODES - 1)
    dst = per_partition(dst, np.zeros(NODES, dst.dtype), 0)
    rows = np.zeros((P, TILES, ROW), edge_attr_16.dtype)
    rows[:, :FULL, :ED] = edge_attr_16[:cut].reshape(P, FULL, ED)
    rows[:, :FULL, ED] = 1
    rest = np.zeros((EXTRA * P, ROW), rows.dtype)
    rest[NODES:NODES + EDGES - cut, :ED] = edge_attr_16[cut:]
    rest[NODES:NODES + EDGES - cut, ED] = 1
    rows[:, FULL:] = rest.reshape(P, EXTRA, ROW)

    w = {name[len("L0_gnn_"):]: a for name, a in w.items()}
    pack = np.zeros((P, PACK), np.float32)

    def put(name, a, row=0, col=0):
        at = LAYOUT[name][0] + col
        pack[row:row + a.shape[0], at:at + a.shape[1]] = a

    i = np.arange(P)
    put("ident", np.eye(P))
    put("before", i[:, None] < i[None, :])
    put("after", i[None, :] < i[:, None])
    put("iota", np.broadcast_to(np.arange(CHUNK), (P, CHUNK)))
    put("first", np.broadcast_to((i == 0)[:, None], (P, P)))
    put("last", (i == P - 1)[:, None])
    put("spread", np.ones((1, D + 1)), D)
    att = w["W_att1"]
    put("w1", att[:, :D].T)
    put("w1", att[:, D + ED:].T, 0, H1)
    put("w1", w["b_att1"][None], D, H1)
    for q in range(PARTS):
        for k in range(2):
            for s in range(PARTS - q):
                put("wedge", att[:, D:D + ED].T, (k * PARTS + s) * ED, (q * 2 + k) * H1)
    put("w2", np.broadcast_to(w["W_att2"], (P, H1)))
    put("b2", np.broadcast_to(w["b_att2"], (P, 1)))
    for name, weight, bias in (("wlin", "W_lin", "b_lin"), ("wih", "W_ih", "b_ih"), ("whh", "W_hh", "b_hh")):
        put(name, w[weight].T)
        put(name, w[bias][None], D)
    return {"x": x, "src": src, "dst": dst, "rows": rows.reshape(P, TILES * ROW), "pack": pack}


def kernel(**inputs):
    import concourse.bacc as bacc
    from concourse.bass_utils import run_bass_kernel_spmd

    nc = bacc.Bacc("TRN2", target_bir_lowering=False, num_devices=1)
    arrays, args = {}, []
    for name, a in layout(**inputs).items():
        a = np.ascontiguousarray(a)
        arrays[f"in_{name}_dram"] = a
        args.append(nc.dram_tensor(f"in_{name}_dram", a.shape, mybir.dt.from_np(a.dtype),
                                   kind="ExternalInput").ap())
    out = nc.dram_tensor("out_0_dram", (NODES, D), F32, kind="ExternalOutput").ap()
    gnn_kernel(nc, *args, out)
    r = run_bass_kernel_spmd(nc, [arrays], core_ids=[0])
    return r.results[0]["out_0_dram"]
```

```python
import numpy as np
import concourse.bass as bass
from concourse import mybir
from contextlib import ExitStack

F32 = mybir.dt.float32
BF16 = mybir.dt.bfloat16
I32 = mybir.dt.int32
U32 = mybir.dt.uint32
ALU = mybir.AluOpType
ACT = mybir.ActivationFunctionType
AX = mybir.AxisListType

P = 128
NODES = 3125
EDGES = 53125
D = 64
ED = 16
H1 = 2 * D + ED
FULL = EDGES // P
TILES = (EDGES + NODES + P - 1) // P
EXTRA = TILES - FULL
LO, HI = 125, 25
QUAD = 4
OCT = 2 * QUAD
TURNS = TILES // OCT
ROW = ED + 1
PARTS = 3
PAY = 28
C_VALID, C_NODE, C_DST = PARTS * ED // 2, PARTS * ED // 2 + 1, PARTS * ED // 2 + 2
TAB = H1 + D
CHUNK, CHUNKS, SUB = 448, 7, 112
TAB_AT = 7
TAB_END = TAB_AT + HI - 1
TAB_OUT = 5
TABLES_OUT = 16 * (1 + 2 * HI // TAB_OUT)
EARLY = 4
AHEAD = EARLY * 2 * OCT
NPAD = NODES + P
WIDE = 3264
MAGIC = 12582912.0
DUMMY = -1e30
TWO = NODES
APART = 1e33
EPS = 1e-5
TB = 110
NTB = TILES // TB

LAYOUT, _at = {}, 0
for _name, _n in [("ident", P), ("before", P), ("after", P), ("iota", CHUNK), ("first", P),
                  ("w1", 2 * H1), ("wedge", 3 * 2 * H1), ("w2", H1), ("b2", 1), ("wlin", D), ("wih", 3 * D),
                  ("whh", 3 * D), ("last", 1), ("spread", D)]:
    LAYOUT[_name] = (_at, _at + _n)
    _at += _n
PACK = _at


class Steps:

    def __init__(self, engine, sem):
        self.engine, self.sem, self.base, self.n = engine, sem, 0, 0

    def mark(self, ins):
        ins.then_inc(self.sem, 1)
        self.n += 1

    def sync(self, n=None):
        self.engine.wait_ge(self.sem, self.base + (self.n if n is None else n))

    def link(self, ins):
        self.mark(ins)
        self.sync()


def gnn_kernel(nc, x, src, dst, rows, pack, out):
    sorted_rows = nc.dram_tensor("sorted_rows", (TILES * P, PAY), F32, kind="Internal").ap()
    src_table = nc.dram_tensor("src_table", (NPAD, PARTS * H1), BF16, kind="Internal").ap()
    dst_table = nc.dram_tensor("dst_table", (NODES, TAB), F32, kind="Internal").ap()

    ctx = ExitStack()
    with ctx:
        def sb(name, shape, dt=F32):
            return ctx.enter_context(nc.sbuf_tensor(name, shape, dt))

        def sem(name):
            return ctx.enter_context(nc.semaphore(name))

        banks = [ctx.enter_context(nc.psum_tensor(f"bank{i}", [P, 512], F32)) for i in range(8)]

        wp = sb("wp", [P, PACK])

        def const(name, parts=P):
            a, b = LAYOUT[name]
            return wp[0:parts, a:b]

        ident, iota = const("ident"), const("iota")[:, 0:P]
        iota_b = sb("iota_b", [P, P], BF16)
        ident_b = sb("ident_b", [P, P], BF16)

        hT = sb("hT", [D + 1, CHUNK * CHUNKS])
        early = ExitStack()

        def eb(name, shape, dt=F32):
            return early.enter_context(nc.sbuf_tensor(name, shape, dt))

        xs = eb("xs", [LO, HI, D])
        h = eb("h", [LO, HI, D])
        mean = eb("mean", [LO, HI])
        var = eb("var", [LO, HI])
        std = eb("std", [LO, HI])
        rstd = eb("rstd", [LO, HI])
        hc = eb("hc", [LO, D])
        hcT = eb("hcT", [D + 1, LO])
        tab_src = eb("tab_src", [LO, HI, H1])
        tab_dst = eb("tab_dst", [LO, HI, TAB])
        zero_rows = eb("zero_rows", [P, PARTS * H1], BF16)

        edges = eb("edges", [P, TILES, ROW])
        edge_rest = eb("edge_rest", [P, OCT, ED])
        src_i = eb("src_i", [P, TILES], I32)
        dst_i = eb("dst_i", [P, TILES], I32)
        dst_f = eb("dst_f", [P, TILES])
        lo = eb("lo", [P, TILES])
        hi = eb("hi", [P, TILES])
        hi1 = eb("hi1", [P, TILES])
        hi1sq = eb("hi1sq", [P, TILES])
        rhi = eb("rhi", [P, TILES])
        nodef = eb("nodef", [P, TILES])

        oh_lo = [eb(f"oh_lo{par}", [P, OCT, LO], BF16) for par in range(2)]
        oh_hi = [eb(f"oh_hi{par}", [P, OCT, HI], BF16) for par in range(2)]
        lo_b = eb("lo_b", [P, TILES], BF16)
        hi_b = eb("hi_b", [P, TILES], BF16)
        count = eb("count", [LO, HI * TILES], BF16)
        tab_split = count[:, 0:HI * PARTS * H1].rearrange("p (c s f) -> p c s f", c=HI, s=PARTS)
        total = eb("total", [LO, TURNS])
        total1 = eb("total1", [LO, 1])
        start = eb("start", [LO, HI * TILES + 1])

        marked_T = [eb(f"marked_T{q}", [LO, QUAD, P], BF16) for q in range(2)]
        start_q = [eb(f"start_q{q}", [LO, QUAD, 2, HI], BF16) for q in range(2)]
        same = eb("same", [P, OCT, P], BF16)
        rank = [eb(f"rank{par}", [P, OCT]) for par in range(2)]
        own_hi = eb("own_hi", [P, OCT, HI])
        pick = eb("pick", [P, OCT, 2 * HI])
        place = eb("place", [P, OCT])
        place_t = eb("place_t", [P, OCT])
        place_u = eb("place_u", [P, OCT])
        addr = [eb(f"addr{par}", [P, OCT], U32) for par in range(2)]
        pay = [eb(f"pay{par}", [P, OCT, PAY]) for par in range(2)]

        early.close()

        sums = sb("sums", [D + 1, WIDE])
        firsts = sb("firsts", [D + 1, TILES])
        piece_top = sb("piece_top", [OCT, 2, TURNS])
        window_at = sb("window_at", [1, TILES // 2], I32)
        row = {n: sb(f"row_{n}", [1, TILES + 1]) for n in
               ("first", "last", "top_first", "top_last", "link", "one", "pass_f", "pass_b", "run_f", "run_b",
                "scale_f", "scale_l")}
        x_out = sb("x_out", [SUB, CHUNKS * CHUNK // SUB, D])
        result = sb("result", [SUB, CHUNKS * CHUNK // SUB, D])
        edge_w = sb("edge_w", [2 * PARTS * ED, PARTS, 2, H1], BF16)
        edge_w_rest = sb("edge_w_rest", [2 * PARTS * ED, PARTS, 2, H1])
        middle = ExitStack()

        def mb(name, shape, dt=F32):
            return middle.enter_context(nc.sbuf_tensor(name, shape, dt))

        entries = mb("entries", [P, TILES, PAY])
        node = mb("node", [P, TILES])
        penalty = mb("penalty", [P, TILES])

        dst_at = [mb(f"dst_at{par}", [P, OCT], U32) for par in range(2)]
        got = [mb(f"got{par}", [P, OCT, TAB]) for par in range(2)]
        window = [mb(f"window{par}", [P, OCT, PARTS * H1], BF16) for par in range(2)]
        onehot = [mb(f"onehot{par}", [P, OCT, P], BF16) for par in range(2)]
        onehot_f = [mb(f"onehot_f{par}", [P, OCT, P]) for par in range(2)]
        onehot_T = [[mb(f"onehot_T{par}{q}", [P, QUAD, P], BF16) for q in range(2)] for par in range(2)]
        feat = [mb(f"feat{q}", [P, QUAD, PARTS * ED], BF16) for q in range(2)]
        feat_T = [[mb(f"feat_T{par}{q}", [2 * PARTS * ED, 2, P], BF16) for q in range(2)] for par in range(2)]
        hidden = [mb(f"hidden{d}", [P, 2, H1]) for d in range(2)]
        weighed = mb("weighed", [P, OCT, H1], BF16)
        score = mb("score", [P, OCT])
        masked = mb("masked", [P, OCT])
        local_b = mb("local_b", [P, TILES], BF16)
        node_q = mb("node_q", [P, OCT])

        node_T = mb("node_T", [OCT, P])
        step_T = mb("step_T", [OCT, P + 1])
        ahead = mb("ahead", [OCT, P])
        behind = mb("behind", [OCT, P])
        top = mb("top", [OCT, P])
        power = mb("power", [OCT, P])
        weight = mb("weight", [P, OCT])
        feats = [mb(f"feats{par}", [P, OCT, D + 1]) for par in range(2)]
        scaled = [mb(f"scaled{par}", [P, OCT, D + 1]) for par in range(2)]

        middle.close()

        col = sb("col", [TB, 4, NTB])
        firsts_T = sb("firsts_T", [TB, NTB, D + 1])
        first_parts = sb("first_parts", [TB, NTB, PARTS, D + 1], BF16)
        last_rep = sb("last_rep", [TB, NTB, D + 1])
        last_parts = sb("last_parts", [TB, NTB, PARTS, D + 1], BF16)
        at_first = sb("at_first", [TB, NTB, CHUNK], BF16)
        at_last = sb("at_last", [TB, NTB, CHUNK], BF16)

        merged = sb("merged", [D + 1, CHUNK])
        den = sb("den", [D, CHUNK])
        old = sb("old", [D, CHUNK])
        none = sb("none", [D, CHUNK], I32)
        msg = sb("msg", [D + 1, CHUNK])
        gate_r = sb("gate_r", [D, CHUNK])
        gate_z = sb("gate_z", [D, CHUNK])
        gate_n = sb("gate_n", [D, CHUNK])
        new = sb("new", [D, CHUNK])

        def parts(par):
            return pay[par][:, :, 0:C_VALID].bitcast(BF16).rearrange("p t (s f) -> p t s f", s=PARTS)

        count_v = count[:, :].rearrange("p (h t) -> p h t", h=HI)
        start_v = start[:, 0:HI * TILES].rearrange("p (h t) -> p t h", h=HI)

        def sems(*names):
            return [sem(n) for n in names]

        x_in, src_in, dst_in, rows_in, pack_in = sems("x_in", "src_in", "dst_in", "rows_in", "pack_in")
        dve_step, late_step, pool_step = sems("dve_step", "late_step", "pool_step")
        var_ready, std_ready, rstd_ready, h_ready = sems("var_ready", "std_ready", "rstd_ready", "h_ready")
        onehot_ready = sems("onehot_ready_even", "onehot_ready_odd")
        counted = sems("counted_even", "counted_odd")
        count_kept = sems("count_kept_even", "count_kept_odd")
        ident_ready, consts_ready, total_ready, base_ready, start_ready, rows_ready = sems(
            "ident_ready", "consts_ready", "total_ready", "base_ready", "start_ready", "rows_ready")
        hi1_ready = sem("hi1_ready")
        marked = sems("marked0", "marked1")
        turned = sems("turned0", "turned1")
        turned_kept = sems("turned_kept0", "turned_kept1")
        start_high = sems("start_high0", "start_high1")
        start_split = sems("start_split0", "start_split1")
        ranked = sems("ranked0", "ranked1")
        rank_read = sems("rank_read0", "rank_read1")
        edge_high, edge_rest_ready, edge_mid, edge_split = sems(
            "edge_high", "edge_rest_ready", "edge_mid", "edge_split")
        addr_ready = sems("addr_ready_even", "addr_ready_odd")
        scattered = sems("scattered_even", "scattered_odd")
        hc_ready, hcT_made, hcT_ready, tab_made, tab_kept = sems(
            "hc_ready", "hcT_made", "hcT_ready", "tab_made", "tab_kept")
        tab_rest_ready, tab_mid, tab_split_ready, tables_out = sems(
            "tab_rest_ready", "tab_mid", "tab_split_ready", "tables_out")
        sorted_first, sorted_in, node_ready, firsts_ps_ready, prepared, rest_cleared = sems(
            "sorted_first", "sorted_in", "node_ready", "firsts_ps_ready", "prepared", "rest_cleared")
        dst_ready = sems("dst_ready_even", "dst_ready_odd")
        gathered = [sems("gathered_even0", "gathered_even1"), sems("gathered_odd0", "gathered_odd1")]
        window_in = sems("window_in_even", "window_in_odd")
        onehot_made, feat_ready, feat_turned, feat_T_kept, hidden_ps_ready, hidden_read = sems(
            "onehot_made", "feat_ready", "feat_turned", "feat_T_kept", "hidden_ps_ready", "hidden_read")
        masked_ready, masked_turned, node_q_ready, node_turned, node_T_kept, node_T_read = sems(
            "masked_ready", "masked_turned", "node_q_ready", "node_turned", "node_T_kept", "node_T_read")
        power_from, power_ready, power_turned = sems("power_from", "power_ready", "power_turned")
        feats_kept, onehot_f_kept, scaled_ready = sems("feats_kept", "onehot_f_kept", "scaled_ready")
        summed = sems("summed_even", "summed_odd")
        sums_kept = sems("sums_kept0", "sums_kept1")
        tops_on_row, scales_exp, scales_ready, cols_made, cols_kept, col_moved, parts_ready = sems(
            "tops_on_row", "scales_exp", "scales_ready", "cols_made", "cols_kept", "col_moved",
            "parts_ready")
        at_ready = sems("at_last_ready", "at_first_ready")
        merged_ps = sems("last_parts_ps", "first_parts_ps")
        merged_ready, den_ps_ready, none_ready, msg_ps_ready, msg_ready = sems(
            "merged_ready", "den_ps_ready", "none_ready", "msg_ps_ready", "msg_ready")
        gates_ps, gate_rz, gate_n_in, gate_n_ready, result_T, result_ps, result_ready = sems(
            "gates_ps", "gate_rz", "gate_n_in", "gate_n_ready", "result_T", "result_ps", "result_ready")
        x_again, stored = sems("x_again", "stored")

        onehot_ps = [banks[q][:, 0:256].bitcast(BF16).rearrange("p (t e) -> p t e", t=QUAD) for q in range(2)]
        feat_ps = [banks[q][0:2 * PARTS * ED, 256:384].bitcast(BF16)
                   .rearrange("p (t e) -> p t e", t=2) for q in range(2)]
        hidden_ps = [banks[3 + d][:, 0:2 * H1].rearrange("p (t f) -> p t f", t=2) for d in range(2)]
        score_T = banks[5][0:OCT, 0:P]
        node_ps = banks[2][0:OCT, 0:P]
        weight_ps = banks[5][:, 2 * P:2 * P + OCT]
        sum_ps = [banks[6 + q][0:D + 1, :].rearrange("p (t n) -> p t n", t=QUAD) for q in range(2)]
        sorted_parts = [(banks[0][:, 0:AHEAD], banks[1][0:1, 0:AHEAD], slice(0, AHEAD)),
                        (banks[6][:, 0:TILES - AHEAD], banks[7][0:1, 0:TILES - AHEAD], slice(AHEAD, TILES))]

        marks = [oh_lo[0][:, q * QUAD:(q + 1) * QUAD, :] for q in range(2)]
        turned_ps = [banks[q][:, 0:256].bitcast(BF16).rearrange("p (t e) -> p t e", t=QUAD)
                     for q in range(2)]
        gram_ps = [banks[2 + q][:, :].rearrange("p (t e) -> p t e", t=QUAD) for q in range(2)]
        start_ps = [banks[4 + q][:, 0:2 * QUAD * HI].rearrange("p (t s h) -> p t s h", t=QUAD, s=2)
                    for q in range(2)]
        count_ps = [banks[par][0:LO, 0:OCT * HI].rearrange("p (t h) -> p t h", t=OCT) for par in range(2)]
        base_ps = banks[2][0:LO, 0:1]
        hcT_ps = banks[6][0:D, 0:LO]
        tab_ps = banks[7][0:LO, 0:2 * H1]

        def windows_of(engine, i):
            at = []
            for k in range(QUAD):
                two = engine.value_load(window_at[0:1, bass.ds(i * QUAD + k, 1)], min_val=0,
                                        max_val=TWO * (NODES - 1) + NODES - 1)
                at += [two % TWO, two // TWO]
            return at

        block = ctx.enter_context(nc.Block())

        @block.sync
        def _(sp):
            sp.dma_start(src_i[:, :], src).then_inc(src_in, 16)
            sp.dma_start(wp[:, :], pack).then_inc(pack_in, 16)
            sp.dma_start(xs[:, :, :], x.rearrange("(p c) d -> p c d", c=HI)).then_inc(x_in, 16)
            sp.dma_start(dst_i[:, :], dst).then_inc(dst_in, 16)
            sp.dma_start(edges[:, :, :], rows.rearrange("p (t w) -> p t w", w=ROW)).then_inc(rows_in, 16)
            sp.wait_ge(h_ready, 3)
            sp.dma_start(src_table[NODES:NPAD, :], zero_rows[:, :]).then_inc(tables_out, 16)
            src_table_v = src_table[0:NODES, :].rearrange("(p c) f -> p c f", c=HI)
            dst_table_v = dst_table.rearrange("(p c) f -> p c f", c=HI)
            for c in range(0, HI, TAB_OUT):
                sp.wait_ge(tab_split_ready, c + TAB_OUT)
                sp.dma_start(src_table_v[:, c:c + TAB_OUT, :],
                             tab_split[:, c:c + TAB_OUT, :, :].rearrange("p c s f -> p c (s f)")
                             ).then_inc(tables_out, 16)
                sp.dma_start(dst_table_v[:, c:c + TAB_OUT, :], tab_dst[:, c:c + TAB_OUT, :]
                             ).then_inc(tables_out, 16)
            sp.wait_ge(tables_out, TABLES_OUT)
            for par in range(2):
                sp.wait_ge(scattered[par], 16 * OCT * ((TURNS + 1 - par) // 2))
            sorted_v = sorted_rows.rearrange("(p t) w -> p t w", t=TILES)
            sp.dma_start(entries[:, 0:AHEAD, :], sorted_v[:, 0:AHEAD, :]).then_inc(sorted_first, 16)

            def load_rest(n):
                if n:
                    sp.wait_ge(sorted_in, 16 * n)
                a = AHEAD + n * (TILES - AHEAD) // EARLY
                b = AHEAD + (n + 1) * (TILES - AHEAD) // EARLY
                sp.dma_start(entries[:, a:b, :], sorted_v[:, a:b, :]).then_inc(sorted_in, 16)

            def load_windows(j, par):
                i = j * 2 + par
                at = windows_of(sp, i)
                for k in range(OCT):
                    sp.dma_start(window[par][:, k, :], src_table[bass.ds(at[k], P), :]
                                 ).then_inc(window_in[par], 16)

            sp.wait_ge(prepared, 1)
            load_windows(0, 0)
            load_windows(0, 1)

            def load_later_windows(j):
                for par in range(2):
                    sp.wait_ge(hidden_ps_ready, j * (2 * QUAD) + (QUAD * par - QUAD))
                    load_windows(j, par)

            load_rest(0)
            for j in range(1, EARLY):
                load_rest(j)
                load_later_windows(j)
            sp.wait_ge(prepared, 2)
            with sp.Fori(EARLY, TURNS // 2) as j:
                load_later_windows(j)
            sp.wait_ge(hidden_ps_ready, (TURNS - 2) * QUAD)
            load_windows(TURNS // 2, 0)

            blocks = CHUNKS * CHUNK // SUB
            whole = (blocks - 1) * SUB
            sp.wait_ge(rest_cleared, 1)
            sp.dma_start(x_out[:, 0:blocks - 1, :], x[0:whole, :].rearrange("(k p) d -> p k d", p=SUB)
                         ).then_inc(x_again, 16)
            sp.dma_start(x_out[0:NODES - whole, blocks - 1, :], x[whole:NODES, :]).then_inc(x_again, 16)
            sp.wait_ge(result_ready, CHUNKS)
            sp.dma_start(out[0:whole, :].rearrange("(k p) d -> p k d", p=SUB), result[:, 0:blocks - 1, :]
                         ).then_inc(stored, 16)
            sp.dma_start(out[whole:NODES, :], result[0:NODES - whole, blocks - 1, :]).then_inc(stored, 16)
            sp.wait_ge(stored, 32)

        @block.gpsimd
        def _(pool):
            g = nc.gpsimd
            st = Steps(pool, pool_step)

            def wide(a):
                return a[:, :].unsqueeze(2).broadcast_to((LO, HI, D))

            def fold(n):
                while n:
                    st.link(g.tensor_tensor(h[:, :, 0:n], h[:, :, 0:n], h[:, :, n:2 * n], ALU.add))
                    n //= 2

            pool.wait_ge(x_in, 16)
            st.link(g.tensor_tensor(h[:, :, 0:D // 2], xs[:, :, 0:D // 2], xs[:, :, D // 2:D], ALU.add))
            fold(D // 4)
            st.link(g.tensor_scalar(mean[:, :], h[:, :, 0], 1.0 / D, None, ALU.mult))
            st.link(g.tensor_tensor(xs[:, :, :], xs[:, :, :], wide(mean), ALU.subtract))
            st.link(g.tensor_tensor(h[:, :, :], xs[:, :, :], xs[:, :, :], ALU.mult))
            fold(D // 2)
            g.tensor_scalar(var[:, :], h[:, :, 0], 1.0 / D, EPS, ALU.mult, ALU.add).then_inc(var_ready, 1)
            pool.wait_ge(consts_ready, 1)
            g.tensor_scalar(hi1[:, :], hi[:, :], 1.0, None, ALU.add).then_inc(hi1_ready, 1)
            pool.wait_ge(hi1_ready, 1)
            g.tensor_tensor(hi1sq[:, :], hi1[:, :], hi1[:, :], ALU.mult).then_inc(hi1_ready, 1)
            pool.wait_ge(rstd_ready, 1)
            st.link(g.tensor_tensor(h[:, :, :], xs[:, :, :], wide(rstd), ALU.mult))
            g.tensor_scalar(h[:, :, :], h[:, :, :], 0.0, None, ALU.max).then_inc(h_ready, 1)
            g.memset(zero_rows[:, :], 0.0).then_inc(h_ready, 1)
            pool.wait_ge(h_ready, 2)
            g.tensor_copy(tab_dst[:, :, H1:TAB], h[:, :, :]).then_inc(h_ready, 1)

            def scatter(j, par):
                pool.wait_ge(h_ready, 1)
                pool.wait_ge(addr_ready[par], j + 1)
                pool.wait_ge(edge_split, j * 2 + (par + 1))
                pool.nop(nofuse=True)
                for k in range(OCT):
                    g.indirect_dma_start(
                        sorted_rows, bass.IndirectOffsetOnAxis(ap=addr[par][:, k:k + 1], axis=0),
                        pay[par][:, k, :], None).then_inc(scattered[par], 16)

            with pool.Fori(0, TURNS // 2) as j:
                for par in range(2):
                    scatter(j, par)
            scatter(TURNS // 2, 0)

            def gather(j, par):
                for q in range(2):
                    pool.wait_ge(dst_ready[par], j * 2 + (q + 1))
                    pool.nop(nofuse=True)
                    for k in range(q * QUAD, (q + 1) * QUAD):
                        g.indirect_dma_start(
                            got[par][:, k, :], None, dst_table,
                            bass.IndirectOffsetOnAxis(ap=dst_at[par][:, k:k + 1], axis=0)
                        ).then_inc(gathered[par][q], 16)

            pool.wait_ge(tables_out, TABLES_OUT)
            with pool.Fori(0, TURNS // 2) as j:
                for par in range(2):
                    gather(j, par)
            gather(TURNS // 2, 0)

            pool.wait_ge(cols_kept, 1)

            def find_tiles(c):
                for k, (n, at) in enumerate(((3, at_last), (2, at_first))):
                    pool.wait_ge(merged_ps[k], c)
                    pool.nop(nofuse=True)
                    for b in range(NTB):
                        ins = g.tensor_scalar(at[:, b, :], const("iota")[0:TB, :], col[:, n, b:b + 1], None,
                                              ALU.is_equal)
                    ins.then_inc(at_ready[k], 1)
                pool.wait_ge(at_ready[0], c + 1)
                pool.wait_ge(at_ready[1], c + 1)
                pool.nop(nofuse=True)
                g.tensor_scalar(col[:, 2:4, :], col[:, 2:4, :], float(CHUNK), None, ALU.subtract
                                ).then_inc(col_moved, 1)
                pool.wait_ge(col_moved, c + 1)

            with pool.Fori(0, CHUNKS) as c:
                find_tiles(c)

        @block.scalar
        def _(act):
            s = nc.scalar
            act.wait_ge(pack_in, 16)
            s.activation(ident_b[:, :], ident, ACT.Copy).then_inc(ident_ready, 1)

            def keep_counts(j, par):
                act.wait_ge(counted[par], j + 1)
                i = j * 2 + par
                s.activation(count_v[:, :, bass.ds(i * OCT, OCT)], count_ps[par].rearrange("p t h -> p h t"),
                             ACT.Copy, accum_out=total[:, bass.ds(i, 1)]).then_inc(count_kept[par], 1)

            with act.Fori(0, TURNS // 2) as j:
                for par in range(2):
                    keep_counts(j, par)
            keep_counts(TURNS // 2, 0)
            act.wait_ge(var_ready, 1)
            s.activation(std[:, :], var[:, :], ACT.Sqrt).then_inc(std_ready, 1)

            def keep_turned(j, q):
                act.wait_ge(ranked[q], j)
                t0 = j * OCT + q * QUAD
                s.activation(start_q[q][:, :, 0, :], start_v[:, bass.ds(t0, QUAD), :], ACT.Copy
                             ).then_inc(start_high[q], 1)
                act.wait_ge(turned[q], j + 1)
                s.activation(marked_T[q][:, :, :], turned_ps[q][0:LO], ACT.Copy).then_inc(turned_kept[q], 1)

            def keep_pay(j, par):
                act.wait_ge(scattered[par], j * 16 * OCT)
                i = j * 2 + par
                t0 = bass.ds(i * OCT, OCT)
                s.activation(parts(par)[:, :, 0, :], edges[:, t0, 0:ED], ACT.Copy).then_inc(edge_high, 1)
                s.activation(pay[par][:, :, C_VALID], edges[:, t0, ED], ACT.Copy)
                s.activation(pay[par][:, :, C_NODE], nodef[:, t0], ACT.Copy)
                s.activation(pay[par][:, :, C_DST], dst_f[:, t0], ACT.Copy)
                act.wait_ge(edge_rest_ready, i + 1)
                s.activation(parts(par)[:, :, 1, :], edge_rest[:, :, :], ACT.Copy).then_inc(edge_mid, 1)

            def rank_turn(j, par, first=False, last=False, c=None):
                i = j * 2 + par
                table = c is not None
                if table:
                    act.wait_ge(hcT_made, c)
                    s.activation(hc[:, :], h[:, bass.ds(c, 1), :].rearrange("p a d -> p (a d)"),
                                 ACT.Copy).then_inc(hc_ready, 1)
                keep_turned(i, 1)
                if not first:
                    keep_pay(j - 1 + par, 1 - par)
                if table:
                    act.wait_ge(hcT_made, c + 1)
                    act.wait_ge(tab_made, c)
                    s.activation(hcT[0:D, :], hcT_ps, ACT.Copy).then_inc(hcT_ready, 1)
                    s.activation(hT[0:D, 0:NODES].rearrange("f (p c) -> f c p", c=HI)[:, bass.ds(c, 1), :],
                                 hcT_ps.unsqueeze(1), ACT.Copy).then_inc(hcT_ready, 1)
                if not last:
                    keep_turned(i + 1, 0)
                if table:
                    act.wait_ge(tab_made, c + 1)
                    s.activation(tab_split[:, bass.ds(c, 1), 0, :], tab_ps[:, 0:H1].unsqueeze(1), ACT.Copy)
                    s.activation(tab_src[:, bass.ds(c, 1), :], tab_ps[:, 0:H1].unsqueeze(1), ACT.Copy)
                    s.activation(tab_dst[:, bass.ds(c, 1), 0:H1], tab_ps[:, H1:2 * H1].unsqueeze(1),
                                 ACT.Copy).then_inc(tab_kept, 1)
                    act.wait_ge(tab_rest_ready, c + 1)
                    s.activation(tab_split[:, bass.ds(c, 1), 1, :], tab_src[:, bass.ds(c, 1), :], ACT.Copy
                                 ).then_inc(tab_mid, 1)

            act.wait_ge(start_ready, 1)
            keep_turned(0, 0)
            act.wait_ge(rows_ready, 1)
            act.wait_ge(rows_in, 16)
            rank_turn(0, 0, first=True)
            with act.Fori(0, TAB_AT // 2) as j:
                rank_turn(j, 1)
                rank_turn(j + 1, 0)
            act.wait_ge(h_ready, 1)
            with act.Fori(TAB_AT // 2, TAB_END // 2) as j:
                rank_turn(j, 1, c=j * 2 + 1 - TAB_AT)
                rank_turn(j + 1, 0, c=j * 2 + 2 - TAB_AT)
            rank_turn(TAB_END // 2, 1, c=HI - 1)
            rank_turn(TAB_END // 2 + 1, 0)
            with act.Fori(TAB_END // 2 + 1, TURNS // 2 - 1) as j:
                rank_turn(j, 1)
                rank_turn(j + 1, 0)
            rank_turn(TURNS // 2 - 1, 1)
            rank_turn(TURNS // 2, 0, last=True)
            keep_pay(TURNS // 2, 0)

            def stage_feats(i):
                for q in range(2):
                    act.wait_ge(feat_turned, i * 2 + (q - 1) if not isinstance(i, int) else max(0, 2 * i + q - 1))
                    s.activation(feat[q][:, :, :], entries[:, bass.ds(i * OCT + q * QUAD, QUAD), 0:C_VALID]
                                 .bitcast(BF16), ACT.Copy).then_inc(feat_ready, 1)

            def keep_turned_steps(i, par):
                act.wait_ge(hidden_ps_ready, i * QUAD - QUAD if not isinstance(i, int)
                            else max(0, i * QUAD - QUAD))
                for q in range(2):
                    act.wait_ge(feat_turned, i * 2 + (q + 1))
                    s.activation(onehot_T[par][q][:, :, :], onehot_ps[q], ACT.Copy)
                    yield
                    s.activation(feat_T[par][q][:, :, :], feat_ps[q], ACT.Copy).then_inc(feat_T_kept, 1)
                    yield

            def keep_feats(j, par, q):
                i = j * 2 + par
                act.wait_ge(gathered[par][q], j * (16 * QUAD) + 16 * QUAD)
                act.wait_ge(scaled_ready, i - 1 if not isinstance(i, int) else max(0, i - 1))
                half = slice(q * QUAD, (q + 1) * QUAD)
                s.activation(feats[par][:, half, 0:D], got[par][:, half, H1:TAB], ACT.Copy
                             ).then_inc(feats_kept, 1)

            def sum_steps(j, par):
                i = j * 2 + par
                at = windows_of(act, i)
                yield
                for q in range(2):
                    act.wait_ge(summed[par], j * 2 + (q + 1))
                    s.activation(firsts[:, bass.ds(i * OCT + q * QUAD, QUAD)], sum_ps[q][:, :, 0], ACT.Copy)
                    for k in range(QUAD):
                        act.wait_ge(sums_kept[q if k else 1 - q], i * QUAD + (k if k or not q else QUAD))
                        s.activation(sums[:, bass.ds(at[q * QUAD + k] + 1, P - 1)],
                                     sum_ps[q][:, k, 1:P], ACT.Copy).then_inc(sums_kept[q], 1)
                        yield

            def turn(j, par, first=False, second=False, last=False):
                i = j * 2 + par
                sums_of = sum_steps(j - 1, par) if not (first or second) else iter(())
                turned_of = keep_turned_steps(i + 1, 1 - par) if not last else iter(())
                if not last:
                    stage_feats(i + 1)
                act.wait_ge(node_turned, i)
                s.activation(node_q[:, :], node[:, bass.ds(i * OCT, OCT)], ACT.Copy).then_inc(node_q_ready, 1)
                keep_feats(j, par, 0)
                next(sums_of, None)
                next(turned_of, None)
                if not first:
                    act.wait_ge(power_from, i)
                    act.wait_ge(power_turned, i - 1 if not isinstance(i, int) else max(0, i - 1))
                    s.activation(power[:, :], top[:, :], ACT.Exp).then_inc(power_ready, 1)
                next(sums_of, None)
                for _ in range(3):
                    next(turned_of, None)
                    next(sums_of, None)
                keep_feats(j, par, 1)
                next(sums_of, None)
                act.wait_ge(node_turned, i + 1)
                act.wait_ge(node_T_read, i)
                s.activation(node_T[:, :], node_ps, ACT.Copy, scale=APART).then_inc(node_T_kept, 1)
                next(sums_of, None)
                act.wait_ge(summed[par], j * 2)
                act.wait_ge(onehot_made, i + 1)
                s.activation(onehot_f[par][:, 0:QUAD, :], onehot[par][:, 0:QUAD, :], ACT.Copy)
                next(sums_of, None)
                s.activation(onehot_f[par][:, QUAD:OCT, :], onehot[par][:, QUAD:OCT, :], ACT.Copy
                             ).then_inc(onehot_f_kept, 1)
                next(sums_of, None)

            act.wait_ge(prepared, 1)
            stage_feats(0)
            for _ in keep_turned_steps(0, 0):
                pass
            turn(0, 0, first=True)
            turn(0, 1, second=True)
            with act.Fori(1, EARLY - 1) as j:
                for par in range(2):
                    turn(j, par)
            act.wait_ge(prepared, 2)
            with act.Fori(EARLY - 1, TURNS // 2) as j:
                for par in range(2):
                    turn(j, par)
            turn(TURNS // 2, 0, last=True)
            for _ in sum_steps(TURNS // 2 - 1, 1):
                pass
            act.wait_ge(power_from, TURNS)
            s.activation(power[:, :], top[:, :], ACT.Exp).then_inc(power_ready, 1)
            for _ in sum_steps(TURNS // 2, 0):
                pass

            act.wait_ge(cols_made, 1)
            s.activation(col[:, 2:4, :], banks[4][0:TB, 0:2 * NTB].rearrange("p (n b) -> p n b", n=2), ACT.Copy
                         ).then_inc(cols_kept, 1)
            for k, n in enumerate(("scale_f", "scale_l")):
                act.wait_ge(scales_exp, k + 1)
                s.activation(row[n][:, 0:TILES], row[n][:, 0:TILES], ACT.Exp).then_inc(scales_ready, 1)
            act.wait_ge(cols_made, 2)
            s.activation(col[:, 0:2, :], banks[2][0:TB, 0:2 * NTB].rearrange("p (n b) -> p n b", n=2), ACT.Copy
                         ).then_inc(cols_kept, 1)
            s.activation(firsts_T[:, :, :], banks[3][0:TB, 0:NTB * (D + 1)].rearrange("p (b f) -> p b f", b=NTB),
                         ACT.Copy).then_inc(cols_kept, 1)

            def gru_chunk(c):
                act.wait_ge(result_T, c)
                s.activation(old[:, :], hT[0:D, bass.ds(c * CHUNK, CHUNK)], ACT.Copy)
                act.wait_ge(gates_ps, c + 1)
                s.activation(gate_r[:, :], banks[4][0:D, 0:CHUNK], ACT.Sigmoid).then_inc(gate_rz, 1)
                s.activation(gate_z[:, :], banks[4][D:2 * D, 0:CHUNK], ACT.Sigmoid).then_inc(gate_rz, 1)
                act.wait_ge(gate_n_in, c + 1)
                s.activation(gate_n[:, :], new[:, :], ACT.Tanh).then_inc(gate_n_ready, 1)

            gru_chunk(0)
            with act.Fori(1, CHUNKS) as c:
                gru_chunk(c)

        @block.tensor
        def _(pe):
            t = nc.tensor

            def count_tiles(j, par):
                pe.wait_ge(onehot_ready[par], j + 1)
                pe.wait_ge(count_kept[par], j)
                for k in range(OCT):
                    ins = t.matmul(count_ps[par][:, k, :], oh_lo[par][:, k, :], oh_hi[par][:, k, :],
                                   start=True, stop=True)
                ins.then_inc(counted[par], 1)

            with pe.Fori(0, TURNS // 2) as j:
                for par in range(2):
                    count_tiles(j, par)
            count_tiles(TURNS // 2, 0)
            pe.wait_ge(total_ready, 1)
            t.matmul(base_ps, const("before", LO)[:, 0:LO], total1[:, :], start=True, stop=True
                     ).then_inc(base_ready, 1)

            def turn(j, q):
                pe.wait_ge(marked[q], j + 1)
                pe.wait_ge(turned_kept[q], j)
                for k in range(QUAD):
                    ins = t.transpose(turned_ps[q][0:LO, k, :], marks[q][:, k, :], ident_b[:, :])
                ins.then_inc(turned[q], 1)

            def compare(i, q):
                pe.wait_ge(turned_kept[q], i + 1)
                pe.wait_ge(start_split[q], i + 1)
                pe.wait_ge(rank_read[q], i)
                for k in range(QUAD):
                    m = marked_T[q][:, k, :]
                    t.matmul(gram_ps[q][:, k, :], m, m, start=True, stop=True)
                    ins = t.matmul(start_ps[q][:, k, :, :], m, start_q[q][:, k, :, :], start=True, stop=True)
                ins.then_inc(ranked[q], 1)

            def rank_turn(i, last=False, c=None):
                table = c is not None
                if table:
                    pe.wait_ge(consts_ready, 1)
                    pe.wait_ge(hc_ready, c + 1)
                    pe.wait_ge(hcT_ready, c * 2)
                    pe.nop(nofuse=True)
                    t.transpose(hcT_ps, hc[:, :], ident[0:LO, 0:LO]).then_inc(hcT_made, 1)
                turn(i, 1)
                compare(i, 0)
                if table:
                    pe.wait_ge(hcT_ready, c * 2 + 1)
                    pe.wait_ge(tab_kept, c)
                    t.matmul(tab_ps, hcT[:, :], const("w1", D + 1), start=True, stop=True
                             ).then_inc(tab_made, 1)
                if not last:
                    turn(i + 1, 0)
                compare(i, 1)

            pe.wait_ge(ident_ready, 1)
            turn(0, 0)
            with pe.Fori(0, TAB_AT) as i:
                rank_turn(i)
            with pe.Fori(TAB_AT, TAB_END) as i:
                rank_turn(i, c=i - TAB_AT)
            rank_turn(TAB_END, c=HI - 1)
            with pe.Fori(TAB_END + 1, TURNS - 1) as i:
                rank_turn(i)
            rank_turn(TURNS - 1, last=True)
            def find_firsts(part, first_ps, last_ps, tiles):
                pe.wait_ge(node_ready, part + 1)
                t.matmul(first_ps, const("first"), node[:, tiles], start=True, stop=True)
                t.matmul(last_ps, const("last"), node[:, tiles], start=True, stop=True
                         ).then_inc(firsts_ps_ready, 1)
                pe.wait_ge(prepared, part + 1)

            find_firsts(0, *sorted_parts[0])

            def turn_onehots(i, par):
                for q in range(2):
                    pe.wait_ge(onehot_made, i + 1)
                    pe.wait_ge(feat_T_kept, max(0, i * 2 + q - 1) if isinstance(i, int) else i * 2 + (q - 1))
                    for k in range(QUAD):
                        ins = t.transpose(onehot_ps[q][:, k, :], onehot[par][:, q * QUAD + k, :], ident_b[:, :])
                    pe.wait_ge(feat_ready, i * 2 + (q + 1))
                    for d in range(2):
                        ins = t.transpose(feat_ps[q][:, d, :],
                                          feat[q][:, 2 * d:2 * d + 2, :].rearrange("p t f -> p (t f)"),
                                          ident_b[:, :])
                    ins.then_inc(feat_turned, 1)

            def turn_nodes(i):
                pe.wait_ge(node_q_ready, i + 1)
                pe.wait_ge(node_T_kept, i)
                pe.nop(nofuse=True)
                t.transpose(node_ps, node_q[:, :], ident).then_inc(node_turned, 1)

            def hidden_of(j, par, d):
                i = j * 2 + par
                q = d // 2
                if d == 0:
                    pe.wait_ge(window_in[par], (j + 1) * (16 * OCT))
                if d % 2 == 0:
                    pe.wait_ge(feat_T_kept, i * 2 + (q + 1))
                pe.wait_ge(hidden_read, i * QUAD + (d - 1) if not isinstance(i, int)
                           else max(0, i * QUAD + d - 1))
                for e in range(2):
                    k = 2 * d + e
                    o = hidden_ps[d % 2][:, e, :]
                    for part in range(PARTS):
                        t.matmul(o, onehot_T[par][q][:, k % QUAD, :],
                                 window[par][:, k, part * H1:(part + 1) * H1],
                                 start=(part == 0), stop=False)
                    for part in range(PARTS):
                        ins = t.matmul(o, feat_T[par][q][:, (k % QUAD) // 2, :], edge_w[:, part, e, :],
                                       start=False, stop=(part == PARTS - 1))
                ins.then_inc(hidden_ps_ready, 1)

            def score_turn(i):
                pe.wait_ge(masked_ready, i + 1)
                pe.nop(nofuse=True)
                t.transpose(score_T, masked[:, :], ident).then_inc(masked_turned, 1)

            def power_turn(i):
                pe.wait_ge(power_ready, i + 1)
                pe.nop(nofuse=True)
                t.transpose(weight_ps, power[:, :], ident[0:OCT, 0:OCT]).then_inc(power_turned, 1)

            def sum_turn(j, par):
                i = j * 2 + par
                pe.wait_ge(scaled_ready, i + 1)
                pe.wait_ge(onehot_f_kept, i + 1)
                for q in range(2):
                    pe.wait_ge(sums_kept[q], i * QUAD)
                    for k in range(QUAD):
                        ins = t.matmul(sum_ps[q][:, k, :], scaled[par][:, q * QUAD + k, :],
                                       onehot_f[par][:, q * QUAD + k, :], start=True, stop=True)
                    ins.then_inc(summed[par], 1)

            def turn_(j, par, first=False, second=False, last=False):
                i = j * 2 + par
                hidden_of(j, par, 0)
                if not first:
                    score_turn(i - 1)
                hidden_of(j, par, 1)
                if not (first or second):
                    sum_turn(j - 1, par)
                if not last:
                    turn_onehots(i + 1, 1 - par)
                turn_nodes(i)
                hidden_of(j, par, 2)
                hidden_of(j, par, 3)
                if not first:
                    power_turn(i - 1)

            turn_onehots(0, 0)
            turn_(0, 0, first=True)
            turn_(0, 1, second=True)
            with pe.Fori(1, EARLY - 1) as j:
                turn_(j, 0)
                turn_(j, 1)
            for q in range(2):
                pe.wait_ge(sums_kept[q], (2 * (EARLY - 1) - 2) * QUAD)
            find_firsts(1, *sorted_parts[1])
            with pe.Fori(EARLY - 1, TURNS // 2) as j:
                turn_(j, 0)
                turn_(j, 1)
            turn_(TURNS // 2, 0, last=True)
            score_turn(TURNS - 1)
            sum_turn(TURNS // 2 - 1, 1)
            power_turn(TURNS - 1)
            sum_turn(TURNS // 2, 0)

            for n in range(2):
                for r in range(OCT):
                    ins = t.matmul(banks[n][0:1, r * TURNS:(r + 1) * TURNS], ident[0:OCT, r:r + 1],
                                   piece_top[:, n, :], start=True, stop=True)
            ins.then_inc(tops_on_row, 1)
            def to_columns(bank, n, name):
                for b in range(NTB):
                    ins = t.matmul(banks[bank][0:TB, n * NTB + b:n * NTB + b + 1],
                                   row[name][:, b * TB:(b + 1) * TB], ident[0:1, 0:1], start=True, stop=True)
                return ins

            to_columns(4, 0, "first")
            to_columns(4, 1, "last").then_inc(cols_made, 1)
            pe.wait_ge(sums_kept[1], TURNS * QUAD)
            for b in range(NTB):
                t.transpose(banks[3][0:TB, b * (D + 1):(b + 1) * (D + 1)], firsts[:, b * TB:(b + 1) * TB],
                            ident[0:D + 1, 0:D + 1])
            pe.wait_ge(scales_ready, 3)
            to_columns(2, 0, "scale_f")
            to_columns(2, 1, "scale_l").then_inc(cols_made, 1)
            pe.wait_ge(parts_ready, 1)
            wih, whh = const("wih", D + 1), const("whh", D + 1)

            def merge_chunk(c):
                pe.wait_ge(merged_ready, c)
                for bank, lhs, at in ((0, last_parts, at_last), (1, first_parts, at_first)):
                    pe.wait_ge(at_ready[bank], c + 1)
                    for b in range(NTB):
                        for part in range(PARTS):
                            ins = t.matmul(banks[bank][0:D + 1, 0:CHUNK], lhs[:, b, part, :], at[:, b, :],
                                           start=(b == part == 0), stop=(b == NTB - 1 and part == PARTS - 1))
                    ins.then_inc(merged_ps[bank], 1)

            def sum_msg(c):
                pe.wait_ge(merged_ready, c + 1)
                pe.wait_ge(none_ready, c)
                t.matmul(banks[2][0:D, 0:CHUNK], const("spread", D + 1), merged[:, :],
                         start=True, stop=True).then_inc(den_ps_ready, 1)
                pe.wait_ge(msg_ready, c)
                t.matmul(banks[3][0:D, 0:CHUNK], const("wlin", D + 1), merged[:, :], start=True, stop=True
                         ).then_inc(msg_ps_ready, 1)

            def turn_result(c):
                pe.wait_ge(result_ready, c)
                pe.wait_ge(result_T, c + 1)
                pe.nop(nofuse=True)
                for k in range(CHUNK // SUB):
                    ins = t.transpose(banks[5][0:SUB, k * D:(k + 1) * D], new[:, k * SUB:(k + 1) * SUB],
                                      ident[0:D, 0:D])
                ins.then_inc(result_ps, 1)

            def gru_chunk(c, first=False, last=False):
                cols = bass.ds(c * CHUNK, CHUNK)
                pe.wait_ge(gate_rz, c * 2)
                pe.wait_ge(gate_n_in, c)
                t.matmul(banks[4][:, 0:CHUNK], wih[:, 0:2 * D], hT[:, cols], start=True, stop=False)
                t.matmul(banks[6][0:D, 0:CHUNK], wih[:, 2 * D:3 * D], hT[:, cols], start=True, stop=True)
                if not last:
                    merge_chunk(c + 1)
                pe.wait_ge(msg_ready, c + 1)
                t.matmul(banks[4][:, 0:CHUNK], whh[:, 0:2 * D], msg[:, :], start=False, stop=True)
                t.matmul(banks[7][0:D, 0:CHUNK], whh[:, 2 * D:3 * D], msg[:, :], start=True, stop=True
                         ).then_inc(gates_ps, 1)
                if not first:
                    turn_result(c - 1)
                if not last:
                    sum_msg(c + 1)

            merge_chunk(0)
            sum_msg(0)
            gru_chunk(0, first=True)
            with pe.Fori(1, CHUNKS - 1) as c:
                gru_chunk(c)
            gru_chunk(CHUNKS - 1, last=True)
            turn_result(CHUNKS - 1)

        @block.vector
        def _(dve):
            v = nc.vector
            st = Steps(dve, dve_step)
            dve.wait_ge(src_in, 16)
            st.link(v.tensor_copy(nodef[:, :], src_i[:, :]))
            st.link(v.tensor_scalar(lo[:, :], nodef[:, :], 1.0 / HI, 0.5 / HI - 0.5, ALU.mult, ALU.add))
            st.link(v.tensor_scalar(lo[:, :], lo[:, :], MAGIC, None, ALU.add))
            st.link(v.tensor_scalar(lo[:, :], lo[:, :], MAGIC, None, ALU.subtract))
            st.link(v.scalar_tensor_tensor(out=hi[:, :], in0=lo[:, :], scalar=-float(HI), in1=nodef[:, :],
                                           op0=ALU.mult, op1=ALU.add))
            st.mark(v.tensor_copy(lo_b[:, :], lo[:, :]))
            dve.wait_ge(pack_in, 16)
            st.link(v.tensor_copy(iota_b[:, :], iota))
            st.link(v.tensor_copy(hi_b[:, :], hi[:, :]))
            v.memset(hcT[D:D + 1, :], 1.0).then_inc(consts_ready, 1)

            def make_count_onehots(j, par):
                dve.wait_ge(counted[par], j)
                tiles = bass.ds(j * (2 * OCT) + par * OCT, OCT)
                v.tensor_tensor(oh_hi[par][:, :, :], iota_b[:, 0:HI].unsqueeze(1).broadcast_to((P, OCT, HI)),
                                hi_b[:, tiles].unsqueeze(2).broadcast_to((P, OCT, HI)), ALU.is_equal)
                v.tensor_tensor(oh_lo[par][:, :, :], iota_b[:, 0:LO].unsqueeze(1).broadcast_to((P, OCT, LO)),
                                lo_b[:, tiles].unsqueeze(2).broadcast_to((P, OCT, LO)), ALU.is_equal
                                ).then_inc(onehot_ready[par], 1)

            with dve.Fori(0, TURNS // 2) as j:
                for par in range(2):
                    make_count_onehots(j, par)
            make_count_onehots(TURNS // 2, 0)
            dve.wait_ge(hi1_ready, 1)
            st.mark(v.reciprocal(rhi[:, :], hi1[:, :]))
            for par in range(2):
                dve.wait_ge(count_kept[par], TURNS // 2 + 1 - par)
            v.tensor_reduce(total1[:, :], total[:, :], AX.X, ALU.add).then_inc(total_ready, 1)
            dve.wait_ge(std_ready, 1)
            v.reciprocal(rstd[:, :], std[:, :]).then_inc(rstd_ready, 1)
            dve.wait_ge(base_ready, 1)
            st.link(v.tensor_copy(start[:, 0:1], base_ps))
            v.tensor_tensor_scan(start[:, 1:HI * TILES + 1], count[:, :], count[:, :], start[:, 0:1],
                                 ALU.add, ALU.max).then_inc(start_ready, 1)
            dve.wait_ge(dst_in, 16)
            for par in range(2):
                v.memset(pay[par][:, :, PAY - 1:PAY], 0.0)
            v.tensor_copy(dst_f[:, :], dst_i[:, :]).then_inc(rows_ready, 1)
            dve.wait_ge(rows_in, 16)

            def mark_nodes(j, q, between=iter(())):
                dve.wait_ge(turned[q], j)
                for k in range(QUAD):
                    at = bass.ds(j * OCT + q * QUAD + k, 1)
                    ins = v.tensor_scalar(marks[q][:, k, :], iota_b[:, 0:LO], lo[:, at], hi1[:, at],
                                          ALU.is_equal, ALU.mult)
                    if k < QUAD - 1:
                        next(between, None)
                ins.then_inc(marked[q], 1)

            def split_start(j, q):
                dve.wait_ge(start_high[q], j + 1)
                v.tensor_tensor(start_q[q][:, :, 1, :], start_v[:, bass.ds(j * OCT + q * QUAD, QUAD), :],
                                start_q[q][:, :, 0, :], ALU.subtract).then_inc(start_split[q], 1)

            def edge_first_rest(i, par):
                dve.wait_ge(edge_high, i + 1)
                v.tensor_tensor(edge_rest[:, :, :], edges[:, bass.ds(i * OCT, OCT), 0:ED],
                                parts(par)[:, :, 0, :], ALU.subtract).then_inc(edge_rest_ready, 1)

            def edge_last_rest(i, par):
                dve.wait_ge(edge_mid, i + 1)
                v.tensor_tensor(parts(par)[:, :, 2, :], edge_rest[:, :, :], parts(par)[:, :, 1, :],
                                ALU.subtract).then_inc(edge_split, 1)

            def finish_steps(i, par):
                st.mark(v.tensor_tensor(place[:, :], place[:, :], rhi[:, bass.ds(i * OCT, OCT)], ALU.mult))
                step = st.n
                yield
                st.sync(step)
                st.mark(v.tensor_tensor(place[:, :], place[:, :], rank[par][:, :], ALU.add))
                step = st.n
                yield
                st.sync(step)
                st.mark(v.tensor_scalar(place[:, :], place[:, :], MAGIC, MAGIC, ALU.add, ALU.subtract))
                step = st.n
                yield
                st.sync(step)
                st.mark(v.tensor_scalar(place_t[:, :], place[:, :], 1.0 / P, 0.5 / P - 0.5, ALU.mult, ALU.add))
                step = st.n
                yield
                st.sync(step)
                st.mark(v.tensor_scalar(place_t[:, :], place_t[:, :], MAGIC, MAGIC, ALU.add, ALU.subtract))
                step = st.n
                yield
                st.sync(step)
                st.mark(v.scalar_tensor_tensor(out=place_u[:, :], in0=place_t[:, :], scalar=-float(P),
                                               in1=place[:, :], op0=ALU.mult, op1=ALU.add))
                step = st.n
                yield
                st.sync(step)

            def give_addresses(j, par):
                dve.wait_ge(scattered[par], j * 16 * OCT)
                v.scalar_tensor_tensor(out=addr[par][:, :], in0=place_u[:, :], scalar=float(TILES),
                                       in1=place_t[:, :], op0=ALU.mult, op1=ALU.add
                                       ).then_inc(addr_ready[par], 1)

            def rank_turn(j, par, first=False, last=False, c=None):
                i = j * 2 + par
                steps = finish_steps(i - 1, 1 - par) if not first else iter(())
                st.mark(v.tensor_tensor(
                    own_hi[:, :, :], iota[:, 0:HI].unsqueeze(1).broadcast_to((P, OCT, HI)),
                    hi[:, bass.ds(i * OCT, OCT)].unsqueeze(2).broadcast_to((P, OCT, HI)), ALU.is_equal))
                picked = st.n
                if not first:
                    edge_first_rest(i - 1, 1 - par)
                for q in range(2):
                    if not last:
                        mark_nodes(i + 1, q, steps)
                    if q == 1 and c is not None:
                        dve.wait_ge(tab_kept, c + 1)
                        column = bass.ds(c, 1)
                        v.tensor_tensor(tab_src[:, column, :], tab_src[:, column, :],
                                        tab_split[:, column, 0, :], ALU.subtract).then_inc(tab_rest_ready, 1)
                    dve.wait_ge(ranked[q], i + 1)
                    for k in range(QUAD):
                        at = bass.ds(i * OCT + q * QUAD + k, 1)
                        r = q * QUAD + k
                        next(steps, None)
                        st.mark(v.scalar_tensor_tensor(
                            out=same[:, r, :], in0=gram_ps[q][:, k, :], scalar=hi1sq[:, at],
                            in1=const("after"), op0=ALU.is_equal, op1=ALU.mult,
                            accum_out=rank[par][:, r:r + 1]))
                    st.sync(picked)
                    half = slice(q * QUAD, (q + 1) * QUAD)
                    v.tensor_tensor(pick[:, half, :].rearrange("p t (s h) -> p t s h", s=2), start_ps[q],
                                    own_hi[:, half, :].unsqueeze(2).broadcast_to((P, QUAD, 2, HI)), ALU.mult
                                    ).then_inc(rank_read[q], 1)
                    if q == 0:
                        split_start(i, 1)
                    elif not last:
                        split_start(i + 1, 0)
                    if q == 0 and not first:
                        edge_last_rest(i - 1, 1 - par)
                        for _ in steps:
                            pass
                        give_addresses(j - 1 + par, 1 - par)
                if c is not None:
                    dve.wait_ge(tab_mid, c + 1)
                    v.tensor_tensor(tab_split[:, column, 2, :], tab_src[:, column, :],
                                    tab_split[:, column, 1, :], ALU.subtract).then_inc(tab_split_ready, 1)
                for q in range(2):
                    dve.wait_ge(rank_read[q], i + 1)
                if not first:
                    dve.wait_ge(addr_ready[1 - par], j + par)
                st.sync()
                st.link(v.tensor_reduce(place[:, :], pick[:, :, :], AX.X, ALU.add))

            dve.wait_ge(hi1_ready, 2)
            mark_nodes(0, 0)
            mark_nodes(0, 1)
            split_start(0, 0)
            rank_turn(0, 0, first=True)
            before = st.n

            def rank_turns(start, end, table=False):
                with dve.Fori(start, end) as j:
                    for par in (1, 0):
                        st.base = j * (2 * RANK_STEPS) + (before + (1 - par) * RANK_STEPS)
                        st.n = 0
                        rank_turn(j + 1 - par, par, c=j * 2 + (2 - par - TAB_AT) if table else None)
                        assert st.n == RANK_STEPS, st.n

            rank_turns(0, TAB_AT // 2)
            rank_turns(TAB_AT // 2, TAB_END // 2, table=True)
            st.base, st.n = 0, before + TAB_END // 2 * 2 * RANK_STEPS
            rank_turn(TAB_END // 2, 1, c=HI - 1)
            rank_turn(TAB_END // 2 + 1, 0)
            rank_turns(TAB_END // 2 + 1, TURNS // 2 - 1)
            st.base, st.n = 0, before + (TURNS - 3) * RANK_STEPS
            rank_turn(TURNS // 2 - 1, 1)
            rank_turn(TURNS // 2, 0, last=True)
            edge_first_rest(TURNS - 1, 0)
            for _ in finish_steps(TURNS - 1, 0):
                pass
            edge_last_rest(TURNS - 1, 0)
            give_addresses(TURNS // 2, 0)
            st = Steps(dve, late_step)
            dve.wait_ge(h_ready, 3)
            dve.wait_ge(tables_out, TABLES_OUT)
            wedge = const("wedge", 2 * PARTS * ED).rearrange("p (s k f) -> p s k f", s=PARTS, k=2)
            st.link(v.tensor_copy(edge_w[:, :, :, :], wedge))
            st.link(v.tensor_tensor(edge_w_rest[:, :, :, :], wedge, edge_w[:, :, :, :], ALU.subtract))
            st.link(v.tensor_copy(edge_w[:, 1:3, :, :], edge_w_rest[:, 1:3, :, :]))
            st.link(v.tensor_tensor(edge_w_rest[:, 2, :, :], edge_w_rest[:, 2, :, :], edge_w[:, 2, :, :],
                                    ALU.subtract))
            st.mark(v.tensor_copy(edge_w[:, 2, :, :], edge_w_rest[:, 2, :, :]))
            v.memset(sums[:, :], 0.0)
            v.memset(hT[0:D, NODES:CHUNK * CHUNKS], 0.0)
            v.memset(hT[D:D + 1, :], 1.0)
            v.memset(x_out[:, CHUNKS * CHUNK // SUB - 1, :], 0.0).then_inc(rest_cleared, 1)
            dve.wait_ge(rest_cleared, 1)

            def give_dst(j, par, q):
                half = slice(q * QUAD, (q + 1) * QUAD)
                v.tensor_copy(dst_at[par][:, half],
                              entries[:, bass.ds(j * (2 * OCT) + (par * OCT + q * QUAD), QUAD), C_DST]
                              ).then_inc(dst_ready[par], 1)

            dve.wait_ge(sorted_first, 16)
            for par in range(2):
                for q in range(2):
                    give_dst(0, par, q)
            for par in range(2):
                v.memset(feats[par][:, :, D:D + 1], 1.0)
            v.memset(step_T[:, 0:P + 1], -APART)

            def prepare(part, first_ps, last_ps, tiles):
                v.tensor_copy(node[:, tiles], entries[:, tiles, C_NODE]).then_inc(node_ready, 1)
                valid, low = entries[:, tiles, C_VALID], penalty[:, tiles]
                st.link(v.tensor_scalar(low, valid, 1.0, -DUMMY, ALU.subtract, ALU.mult))
                st.mark(v.tensor_scalar(low, low, const("b2"), None, ALU.add))
                dve.wait_ge(firsts_ps_ready, part + 1)
                st.mark(v.tensor_tensor(local_b[:, tiles], node[:, tiles], first_ps, ALU.subtract))
                st.mark(v.tensor_copy(row["first"][:, tiles], first_ps[0:1, :]))
                st.link(v.tensor_copy(row["last"][:, tiles], last_ps))
                pairs = slice(tiles.start // 2, tiles.stop // 2)
                v.scalar_tensor_tensor(out=window_at[:, pairs],
                                       in0=row["first"][:, tiles.start + 1:tiles.stop:2], scalar=float(TWO),
                                       in1=row["first"][:, tiles.start:tiles.stop:2],
                                       op0=ALU.mult, op1=ALU.add).then_inc(prepared, 1)

            prepare(0, *sorted_parts[0])
            dve.wait_ge(prepared, 1)

            def make_onehots(j, par):
                i = j * 2 + par
                dve.wait_ge(onehot_f_kept, i - 1 if not isinstance(i, int) else max(0, i - 1))
                v.tensor_tensor(onehot[par][:, :, :], iota_b[:, :].unsqueeze(1).broadcast_to((P, OCT, P)),
                                local_b[:, bass.ds(i * OCT, OCT)].unsqueeze(2).broadcast_to((P, OCT, P)),
                                ALU.is_equal).then_inc(onehot_made, 1)

            def weigh_steps(j, par):
                i = j * 2 + par
                dve.wait_ge(node_T_kept, i + 1)
                v.tensor_tensor(step_T[:, 1:P], node_T[:, 0:P - 1], node_T[:, 1:P], ALU.subtract
                                ).then_inc(node_T_read, 1)
                yield
                dve.wait_ge(node_T_read, i + 1)
                dve.wait_ge(masked_turned, i + 1)
                st.mark(v.tensor_tensor_scan(ahead[:, :], step_T[:, 0:P], score_T, 10 * DUMMY, ALU.add, ALU.max))
                st.mark(v.tensor_tensor_scan(behind[:, ::-1], step_T[:, P:0:-1], score_T[:, ::-1],
                                             10 * DUMMY, ALU.add, ALU.max))
                at = st.n
                yield
                st.sync(at)
                dve.wait_ge(power_ready, i)
                st.mark(v.tensor_tensor(ahead[:, :], ahead[:, :], behind[:, :], ALU.max))
                at = st.n
                yield
                st.sync(at)
                st.mark(v.tensor_copy(piece_top[:, :, bass.ds(i, 1)], ahead[:, 0:P:P - 1].unsqueeze(2)))
                v.tensor_tensor(top[:, :], score_T, ahead[:, :], ALU.subtract).then_inc(power_from, 1)
                yield
                dve.wait_ge(power_turned, i + 1)
                st.mark(v.tensor_tensor(weight[:, :], weight_ps, entries[:, bass.ds(i * OCT, OCT), C_VALID],
                                        ALU.mult))
                at = st.n
                yield
                st.sync(at)
                dve.wait_ge(feats_kept, i * 2 + 2)
                dve.wait_ge(summed[par], j * 2)
                v.tensor_tensor(scaled[par][:, :, :], feats[par][:, :, :],
                                weight[:, :].unsqueeze(2).broadcast_to((P, OCT, D + 1)), ALU.mult
                                ).then_inc(scaled_ready, 1)
                yield

            def score_tiles(i, d):
                for e in range(2):
                    k = 2 * d + e
                    st.mark(v.scalar_tensor_tensor(
                        out=weighed[:, k, :], in0=hidden[d % 2][:, e, :], scalar=0.0, in1=const("w2"),
                        op0=ALU.max, op1=ALU.mult, accum_out=score[:, k:k + 1]))

            def turn(j, par, first=False, last=False, early=True):
                i = j * 2 + par
                before = weigh_steps(j - 1 + par, 1 - par) if not first else iter(())
                marks_at = {}

                def add_hidden(d):
                    if d % 2 == 0:
                        dve.wait_ge(gathered[par][d // 2], j * (16 * QUAD) + 16 * QUAD)
                    dve.wait_ge(hidden_ps_ready, i * QUAD + (d + 1))
                    if d >= 2:
                        st.sync(marks_at[d - 2])
                    v.tensor_tensor(hidden[d % 2][:, :, :], hidden_ps[d % 2], got[par][:, 2 * d:2 * d + 2, 0:H1],
                                    ALU.add).then_inc(hidden_read, 1)

                def score_tiles(d):
                    dve.wait_ge(hidden_read, i * QUAD + (d + 1))
                    for e in range(2):
                        k = 2 * d + e
                        st.mark(v.scalar_tensor_tensor(
                            out=weighed[:, k, :], in0=hidden[d % 2][:, e, :], scalar=0.0, in1=const("w2"),
                            op0=ALU.max, op1=ALU.mult, accum_out=score[:, k:k + 1]))
                    marks_at[d] = st.n

                next(before, None)
                add_hidden(0)
                if not last:
                    make_onehots(j + par, 1 - par)
                score_tiles(0)
                next(before, None)
                add_hidden(1)
                next(before, None)
                score_tiles(1)
                if early:
                    dve.wait_ge(feats_kept, i * 2 + 1)
                    give_dst(j + 1, par, 0)
                next(before, None)
                add_hidden(2)
                add_hidden(3)
                score_tiles(2)
                next(before, None)
                score_tiles(3)
                if early:
                    dve.wait_ge(feats_kept, i * 2 + 2)
                    give_dst(j + 1, par, 1)
                next(before, None)
                st.sync()
                dve.wait_ge(masked_turned, i)
                v.tensor_tensor(masked[:, :], score[:, :], penalty[:, bass.ds(i * OCT, OCT)], ALU.add
                                ).then_inc(masked_ready, 1)

            make_onehots(0, 0)
            turn(0, 0, first=True)
            first_turn = st.n
            turn(0, 1)

            def turns(start, end):
                with dve.Fori(start, end) as j:
                    for par in range(2):
                        st.base = j * (2 * TURN_STEPS) + (first_turn + (par - 1) * TURN_STEPS)
                        st.n = 0
                        turn(j, par)
                        assert st.n == TURN_STEPS, st.n
                st.base, st.n = 0, first_turn + (2 * end - 1) * TURN_STEPS

            turns(1, EARLY - 1)
            dve.wait_ge(sorted_in, 16 * EARLY)
            steps_before = st.n
            prepare(1, *sorted_parts[1])
            first_turn += st.n - steps_before
            turns(EARLY - 1, TURNS // 2 - 1)
            turn(TURNS // 2 - 1, 0)
            turn(TURNS // 2 - 1, 1, early=False)
            turn(TURNS // 2, 0, last=True, early=False)
            R = {n: a[:, 0:TILES] for n, a in row.items()}

            def row_steps():
                st.mark(v.memset(row["link"][:, :], 0.0))
                st.mark(v.tensor_tensor(R["one"], R["first"], R["last"], ALU.is_equal))
                st.mark(v.memset(row["run_b"][:, TILES:TILES + 1], 10 * DUMMY))
                st.mark(v.memset(row["run_f"][:, 0:1], 10 * DUMMY))
                yield
                st.sync()
                st.link(v.tensor_tensor(row["link"][:, 1:TILES], row["last"][:, 0:TILES - 1],
                                        row["first"][:, 1:TILES], ALU.is_equal))
                yield
                st.mark(v.tensor_tensor(R["pass_f"], R["one"], R["link"], ALU.mult))
                st.link(v.tensor_tensor(R["pass_b"], R["one"], row["link"][:, 1:TILES + 1], ALU.mult))
                yield
                for name in ("pass_f", "pass_b"):
                    st.mark(v.tensor_scalar(R[name], R[name], 1.0, APART, ALU.subtract, ALU.mult))
                st.link(v.tensor_scalar(row["link"][:, :], row["link"][:, :], 1.0, APART, ALU.subtract, ALU.mult))
                st.link(v.tensor_scalar(R["one"], R["one"], -1.0, 1.0, ALU.mult, ALU.add))
                yield

            rows_of = row_steps()
            for _ in weigh_steps(TURNS // 2, 0):
                next(rows_of, None)
            for _ in rows_of:
                pass

            dve.wait_ge(tops_on_row, 1)
            for n, name in enumerate(("top_first", "top_last")):
                st.mark(v.tensor_copy(R[name].rearrange("p (i r) -> p r i", r=OCT),
                                      banks[n][0:1, 0:TILES].rearrange("p (r i) -> p r i", r=OCT)))
            st.sync()
            st.mark(v.tensor_tensor_scan(row["run_f"][:, 1:TILES + 1], R["pass_f"], R["top_last"], 10 * DUMMY,
                                         ALU.add, ALU.max))
            st.link(v.tensor_tensor_scan(R["run_b"][:, ::-1], R["pass_b"][:, ::-1], R["top_first"][:, ::-1],
                                         10 * DUMMY, ALU.add, ALU.max))
            st.mark(v.tensor_tensor(R["scale_f"], row["run_f"][:, 0:TILES], R["link"], ALU.add))
            st.link(v.tensor_tensor(R["scale_l"], row["run_b"][:, 1:TILES + 1], row["link"][:, 1:TILES + 1], ALU.add))
            st.mark(v.tensor_tensor(R["scale_f"], R["scale_f"], R["run_b"], ALU.max))
            st.link(v.tensor_tensor(R["scale_l"], R["scale_l"], row["run_f"][:, 1:TILES + 1], ALU.max))
            v.tensor_tensor(R["scale_f"], R["top_first"], R["scale_f"], ALU.subtract).then_inc(scales_exp, 1)
            v.tensor_tensor(R["scale_l"], R["top_last"], R["scale_l"], ALU.subtract).then_inc(scales_exp, 1)
            dve.wait_ge(scales_ready, 2)
            v.scalar_tensor_tensor(out=R["scale_l"], in0=R["scale_l"], scalar=1.0, in1=R["one"],
                                   op0=ALU.subtract, op1=ALU.mult).then_inc(scales_ready, 1)
            dve.wait_ge(cols_kept, 3)
            st.mark(v.tensor_tensor(firsts_T[:, :, :], firsts_T[:, :, :],
                                    col[:, 0, :].unsqueeze(2).broadcast_to((TB, NTB, D + 1)), ALU.mult))
            st.link(v.tensor_copy(last_rep[:, :, :], col[:, 1, :].unsqueeze(2).broadcast_to((TB, NTB, D + 1))))
            for part in range(PARTS):
                for whole, split in ((firsts_T, first_parts), (last_rep, last_parts)):
                    st.mark(v.tensor_copy(split[:, :, part, :], whole[:, :, :]))
                st.sync()
                if part < PARTS - 1:
                    for whole, split in ((firsts_T, first_parts), (last_rep, last_parts)):
                        st.mark(v.tensor_tensor(whole[:, :, :], whole[:, :, :], split[:, :, part, :],
                                                ALU.subtract))
                    st.sync()
            v.memset(msg[D:D + 1, :], 1.0).then_inc(parts_ready, 1)
            dve.wait_ge(parts_ready, 1)


            def merge_chunk(c):
                for bank in range(2):
                    dve.wait_ge(merged_ps[bank], c + 1)
                st.link(v.scalar_tensor_tensor(out=merged[:, :], in0=banks[0][0:D + 1, 0:CHUNK], scalar=1.0,
                                               in1=sums[:, bass.ds(c * CHUNK, CHUNK)],
                                               op0=ALU.add, op1=ALU.mult))
                v.tensor_tensor(merged[:, :], merged[:, :], banks[1][0:D + 1, 0:CHUNK], ALU.add
                                ).then_inc(merged_ready, 1)

            def invert_den(c):
                dve.wait_ge(den_ps_ready, c + 1)
                st.link(v.tensor_scalar(den[:, :], banks[2][0:D, 0:CHUNK], 0.5, None, ALU.max))
                st.link(v.reciprocal(den[:, :], den[:, :]))

            def give_msg(c):
                dve.wait_ge(msg_ps_ready, c + 1)
                v.tensor_tensor(msg[0:D, :], banks[3][0:D, 0:CHUNK], den[:, :], ALU.mult).then_inc(msg_ready, 1)

            def find_none(c):
                v.tensor_scalar(none[:, :], banks[2][0:D, 0:CHUNK], 0.5, None, ALU.is_lt).then_inc(none_ready, 1)

            def add_x(c):
                dve.wait_ge(x_again, 32)
                dve.wait_ge(result_ps, c + 1)
                n_sub = CHUNK // SUB
                v.tensor_tensor(result[:, bass.ds(c * n_sub, n_sub), :],
                                banks[5][0:SUB, 0:n_sub * D].rearrange("p (k d) -> p k d", k=n_sub),
                                x_out[:, bass.ds(c * n_sub, n_sub), :], ALU.add).then_inc(result_ready, 1)

            def gru_chunk(c, first=False, last=False):
                if not last:
                    merge_chunk(c + 1)
                dve.wait_ge(gate_rz, c * 2 + 2)
                dve.wait_ge(gates_ps, c + 1)
                dve.wait_ge(result_ps, c)
                st.mark(v.tensor_tensor(new[:, :], banks[7][0:D, 0:CHUNK], gate_r[:, :], ALU.mult))
                turned = st.n
                if not first:
                    add_x(c - 1)
                st.sync(turned)
                v.tensor_tensor(new[:, :], new[:, :], banks[6][0:D, 0:CHUNK], ALU.add).then_inc(gate_n_in, 1)
                if not last:
                    invert_den(c + 1)
                dve.wait_ge(gate_n_ready, c + 1)
                st.link(v.tensor_tensor(new[:, :], msg[0:D, :], gate_n[:, :], ALU.subtract))
                st.link(v.tensor_tensor(new[:, :], new[:, :], gate_z[:, :], ALU.mult))
                st.link(v.tensor_tensor(new[:, :], new[:, :], gate_n[:, :], ALU.add))
                dve.wait_ge(none_ready, c + 1)
                dve.nop(nofuse=True)
                v.copy_predicated(new[:, :], none[:, :], old[:, :]).then_inc(result_T, 1)
                if not last:
                    dve.wait_ge(result_T, c + 1)
                    find_none(c + 1)
                    give_msg(c + 1)

            merge_chunk(0)
            invert_den(0)
            give_msg(0)
            find_none(0)
            gru_chunk(0, first=True)
            before_loop = st.n
            with dve.Fori(1, CHUNKS - 1) as c:
                st.base, st.n = c * CHUNK_STEPS + (before_loop - CHUNK_STEPS), 0
                gru_chunk(c)
                assert st.n == CHUNK_STEPS, st.n
            st.base, st.n = 0, before_loop + (CHUNKS - 2) * CHUNK_STEPS
            gru_chunk(CHUNKS - 1, last=True)
            add_x(CHUNKS - 1)


TURN_STEPS = 5 + OCT
CHUNK_STEPS = 7
RANK_STEPS = 1 + OCT + 6 + 1


def layout(x, src, dst, edge_attr_16, **w):
    cut = FULL * P
    spare = EXTRA * P - NODES - (EDGES - cut)
    def per_partition(edges, first, last):
        rest = np.concatenate([first, edges[cut:], np.full(spare, last, edges.dtype)])
        return np.concatenate([edges[:cut].reshape(P, FULL), rest.reshape(P, EXTRA)], 1)

    src = per_partition(src, np.arange(NODES, dtype=src.dtype), NODES - 1)
    dst = per_partition(dst, np.zeros(NODES, dst.dtype), 0)
    rows = np.zeros((P, TILES, ROW), edge_attr_16.dtype)
    rows[:, :FULL, :ED] = edge_attr_16[:cut].reshape(P, FULL, ED)
    rows[:, :FULL, ED] = 1
    rest = np.zeros((EXTRA * P, ROW), rows.dtype)
    rest[NODES:NODES + EDGES - cut, :ED] = edge_attr_16[cut:]
    rest[NODES:NODES + EDGES - cut, ED] = 1
    rows[:, FULL:] = rest.reshape(P, EXTRA, ROW)

    w = {name[len("L0_gnn_"):]: a for name, a in w.items()}
    pack = np.zeros((P, PACK), np.float32)

    def put(name, a, row=0, col=0):
        at = LAYOUT[name][0] + col
        pack[row:row + a.shape[0], at:at + a.shape[1]] = a

    i = np.arange(P)
    put("ident", np.eye(P))
    put("before", i[:, None] < i[None, :])
    put("after", i[None, :] < i[:, None])
    put("iota", np.broadcast_to(np.arange(CHUNK), (P, CHUNK)))
    put("first", np.broadcast_to((i == 0)[:, None], (P, P)))
    put("last", (i == P - 1)[:, None])
    put("spread", np.ones((1, D)), D)
    att = w["W_att1"]
    put("w1", att[:, :D].T)
    put("w1", att[:, D + ED:].T, 0, H1)
    put("w1", w["b_att1"][None], D, H1)
    for q in range(PARTS):
        for k in range(2):
            for s in range(PARTS - q):
                put("wedge", att[:, D:D + ED].T, (k * PARTS + s) * ED, (q * 2 + k) * H1)
    put("w2", np.broadcast_to(w["W_att2"], (P, H1)))
    put("b2", np.broadcast_to(w["b_att2"], (P, 1)))
    for name, weight, bias in (("wlin", "W_lin", "b_lin"), ("wih", "W_ih", "b_ih"), ("whh", "W_hh", "b_hh")):
        put(name, w[weight].T)
        put(name, w[bias][None], D)
    return {"x": x, "src": src, "dst": dst, "rows": rows.reshape(P, TILES * ROW), "pack": pack}


def kernel(**inputs):
    import concourse.bacc as bacc
    from concourse.bass_utils import run_bass_kernel_spmd

    nc = bacc.Bacc("TRN2", target_bir_lowering=False, num_devices=1)
    arrays, args = {}, []
    for name, a in layout(**inputs).items():
        a = np.ascontiguousarray(a)
        arrays[f"in_{name}_dram"] = a
        args.append(nc.dram_tensor(f"in_{name}_dram", a.shape, mybir.dt.from_np(a.dtype),
                                   kind="ExternalInput").ap())
    out = nc.dram_tensor("out_0_dram", (NODES, D), F32, kind="ExternalOutput").ap()
    gnn_kernel(nc, *args, out)
    r = run_bass_kernel_spmd(nc, [arrays], core_ids=[0])
    return r.results[0]["out_0_dram"]
```
